# Optimizing a Trainium2 kernel written in Bass

```python
import numpy as np
import jax
import jax.numpy as jnp

def _softmax(x, axis=-1):
    return jax.nn.softmax(x, axis=axis)

def _gelu(x):
    return jax.nn.gelu(x, approximate=True)

def _silu(x):
    return jax.nn.silu(x)

def _sigmoid(x):
    return jax.nn.sigmoid(x)

def _layernorm(x, axis=-1, eps=1e-05):
    m = jnp.mean(x, axis=axis, keepdims=True)
    v = jnp.var(x, axis=axis, keepdims=True)
    return (x - m) / jnp.sqrt(v + eps)

def _scatter_add(tgt, idx, src, axis=0):
    return tgt.at[idx].add(src)

def _segment_sum(src, seg, n):
    return jax.ops.segment_sum(src, seg, n)
kernel_name = 'mk_adj_resnorm_d4_adj_r2_b7a286'

def setup_inputs(seed: int=0):
    np.random.seed(seed)
    _w = jnp.asarray

    def _rec_inputs():
        import jax
        import jax.numpy as jnp
        _gk = jax.random.key(seed)
        x = -0.0002928 + 1 * jax.random.normal(jax.random.fold_in(_gk, 1), (8, 1024, 128), jnp.float32)
        _a = jax.random.bernoulli(jax.random.fold_in(_gk, 2), 0.015625, (8, 1024, 1024))
        adj = _a.astype(jnp.int32)
        return (x, adj)
    x, adj = _rec_inputs()

    def _L0_gnn_setup():
        import jax, jax.numpy as jnp
        import numpy as np
        LEAKY_SLOPE = 0.2
        MASK_VAL = -9000000000000000.0
        key = jax.random.key(seed)
        k1, k2, k3 = jax.random.split(key, 3)
        B, N, D = (256, 64, 128)
        hidden = jax.random.normal(k1, (B, N, D), dtype=jnp.float32)
        adj = jax.random.randint(k2, (B, N, N), 0, 5)
        a = jax.random.normal(k3, (4, D), dtype=jnp.float32) * 0.1
        return {'hidden': hidden, 'adj': adj, 'a': a}
    _L0_gnn_all = _L0_gnn_setup()
    _L0_gnn_in = {k: v for k, v in _L0_gnn_all.items() if k in ('a',)}
    del _L0_gnn_all

    def _L1_gnn_setup():
        import jax, jax.numpy as jnp
        import numpy as np
        B, N, D = (128, 50, 128)
        NEG = -9000000000000000.0
        LEAKY_SLOPE = 0.2
        key = jax.random.key(seed)
        ks = jax.random.split(key, 6)
        hidden = jax.random.normal(ks[0], (B, N, D), dtype=jnp.float32)
        adj = jax.random.randint(ks[1], (B, N, N), 0, 5)
        a_0 = jax.random.normal(ks[2], (D, 1), dtype=jnp.float32) * 0.05
        a_1 = jax.random.normal(ks[3], (D, 1), dtype=jnp.float32) * 0.05
        a_2 = jax.random.normal(ks[4], (D, 1), dtype=jnp.float32) * 0.05
        a_3 = jax.random.normal(ks[5], (D, 1), dtype=jnp.float32) * 0.05
        return {'hidden': hidden, 'adj': adj, 'a_0': a_0, 'a_1': a_1, 'a_2': a_2, 'a_3': a_3}
    _L1_gnn_all = _L1_gnn_setup()
    _L1_gnn_in = {k: v for k, v in _L1_gnn_all.items() if k in ('a_0', 'a_1', 'a_2', 'a_3')}
    del _L1_gnn_all

    def _L2_gnn_setup():
        import jax, jax.numpy as jnp
        import numpy as np
        B, L, IN = (16, 512, 128)
        H, C = (4, 32)
        key = jax.random.key(seed)
        k1, k2, k3, k4, k5, k6 = jax.random.split(key, 6)
        x = jax.random.normal(k1, (B, L, IN), dtype=jnp.float32)
        adj = jax.random.randint(k2, (B, L, L), 0, 2, dtype=jnp.int32)
        s_w = (6.0 / (IN + H * C)) ** 0.5
        W = jax.random.uniform(k3, (H * C, IN), jnp.float32, -s_w, s_w)
        b = jnp.zeros((H * C,), jnp.float32)
        s_a = (6.0 / (1 + C)) ** 0.5
        att_src = jax.random.uniform(k4, (1, H, C), jnp.float32, -s_a, s_a)
        att_dst = jax.random.uniform(k5, (1, H, C), jnp.float32, -s_a, s_a)
        return {'x': x, 'adj': adj, 'W': W, 'b': b, 'att_src': att_src, 'att_dst': att_dst}
    _L2_gnn_all = _L2_gnn_setup()
    _L2_gnn_in = {k: v for k, v in _L2_gnn_all.items() if k in ('W', 'b', 'att_src', 'att_dst')}
    del _L2_gnn_all

    def _L3_gnn_setup():
        import jax, jax.numpy as jnp
        import numpy as np
        B, N = (4, 1024)
        IN_F, OUT_F, H = (128, 128, 8)
        HD = OUT_F // H
        ALPHA = 0.2
        TIME_DECAY = 0.1
        key = jax.random.key(seed)
        k1, k2, k3, k4, k5 = jax.random.split(key, 5)
        node_features = jax.random.normal(k1, (B, N, IN_F), dtype=jnp.float32)
        adj_matrix = jax.random.randint(k2, (B, N, N), 0, 2, dtype=jnp.int32)
        time_matrix = jax.random.uniform(k3, (B, N, N), dtype=jnp.float32)

        def xavier(k, shape, fan_in, fan_out):
            bound = 1.414 * np.sqrt(6.0 / (fan_in + fan_out))
            return jax.random.uniform(k, shape, minval=-bound, maxval=bound, dtype=jnp.float32)
        W = xavier(k4, (H, IN_F, HD), IN_F, HD)
        a = xavier(k5, (H, 2 * HD, 1), 2 * HD, 1)
        return {'node_features': node_features, 'adj_matrix': adj_matrix, 'time_matrix': time_matrix, 'W': W, 'a': a}
    _L3_gnn_all = _L3_gnn_setup()
    _L3_gnn_in = {k: v for k, v in _L3_gnn_all.items() if k in ('W', 'a')}
    del _L3_gnn_all
    return {'x': x, 'adj': adj, 'L0_gnn_a': _L0_gnn_in['a'], 'L1_gnn_a_0': _L1_gnn_in['a_0'], 'L1_gnn_a_1': _L1_gnn_in['a_1'], 'L1_gnn_a_2': _L1_gnn_in['a_2'], 'L1_gnn_a_3': _L1_gnn_in['a_3'], 'L2_gnn_W': _L2_gnn_in['W'], 'L2_gnn_b': _L2_gnn_in['b'], 'L2_gnn_att_src': _L2_gnn_in['att_src'], 'L2_gnn_att_dst': _L2_gnn_in['att_dst'], 'L3_gnn_W': _L3_gnn_in['W'], 'L3_gnn_a': _L3_gnn_in['a']}

def reference(x, adj, L0_gnn_a, L1_gnn_a_0, L1_gnn_a_1, L1_gnn_a_2, L1_gnn_a_3, L2_gnn_W, L2_gnn_b, L2_gnn_att_src, L2_gnn_att_dst, L3_gnn_W, L3_gnn_a):
    import jax
    import jax.numpy as jnp

    def _L0_gnn_ref(hidden, adj, a):
        import jax, jax.numpy as jnp
        import numpy as np
        LEAKY_SLOPE = 0.2
        MASK_VAL = -9000000000000000.0
        e = jnp.einsum('kd,bid,bjd->kbij', a, hidden, hidden)
        e = jnp.where(e >= 0, e, LEAKY_SLOPE * e)
        mask = jnp.full(e.shape[1:], MASK_VAL, dtype=e.dtype)
        alpha = jnp.where(adj == 1, e[0], mask)
        alpha = jnp.where(adj == 2, e[1], alpha)
        alpha = jnp.where(adj == 3, e[2], alpha)
        alpha = jnp.where(adj == 4, e[3], alpha)
        alpha = jax.nn.softmax(alpha, axis=-1)
        return jnp.matmul(alpha, hidden)

    def _L1_gnn_ref(hidden, adj, a_0, a_1, a_2, a_3):
        import jax, jax.numpy as jnp
        import numpy as np
        B, N, D = (128, 50, 128)
        NEG = -9000000000000000.0
        LEAKY_SLOPE = 0.2
        A = jnp.concatenate([a_0, a_1, a_2, a_3], axis=1)
        e = jnp.einsum('bid,bjd,dk->bkij', hidden, hidden, A)
        e = jax.nn.leaky_relu(e, negative_slope=LEAKY_SLOPE)
        scores = jnp.full_like(e[:, 0], NEG)
        scores = jnp.where(adj == 1, e[:, 0], scores)
        scores = jnp.where(adj == 2, e[:, 1], scores)
        scores = jnp.where(adj == 3, e[:, 2], scores)
        scores = jnp.where(adj == 4, e[:, 3], scores)
        attn = jax.nn.softmax(scores, axis=-1)
        return jnp.einsum('bij,bjd->bid', attn, hidden)

    def _L2_gnn_ref(x, adj, W, b, att_src, att_dst):
        import jax, jax.numpy as jnp
        import numpy as np
        B, L, IN = (16, 512, 128)
        H, C = (4, 32)
        Bx, Lx, _ = x.shape
        Hh, Cc = (att_src.shape[1], att_src.shape[2])
        xp = (x @ W.T + b).reshape(Bx, Lx, Hh, Cc)
        a_src = jnp.einsum('blhc,hc->bhl', xp, att_src[0])
        a_dst = jnp.einsum('blhc,hc->bhl', xp, att_dst[0])
        scores = jax.nn.leaky_relu(a_src[:, :, None, :] + a_dst[:, :, :, None], negative_slope=0.2)
        eye = jnp.eye(Lx, dtype=bool)
        mask = jnp.where((adj > 0) | eye, 0.0, -jnp.inf)
        alpha = jax.nn.softmax(scores + mask[:, None, :, :], axis=-1)
        out = jnp.einsum('bhij,bjhc->bihc', alpha, xp)
        return out.reshape(Bx, Lx, Hh * Cc)

    def _L3_gnn_ref(node_features, adj_matrix, time_matrix, W, a):
        import jax, jax.numpy as jnp
        import numpy as np
        B, N = (4, 1024)
        IN_F, OUT_F, H = (128, 128, 8)
        HD = OUT_F // H
        ALPHA = 0.2
        TIME_DECAY = 0.1
        current_time = jnp.max(time_matrix)
        time_weights = jnp.exp(-TIME_DECAY * (current_time - time_matrix))
        h = jnp.einsum('bni,hio->bhno', node_features, W)
        a_src = a[:, :HD, 0]
        a_dst = a[:, HD:, 0]
        e_i = jnp.einsum('bhnd,hd->bhn', h, a_src)
        e_j = jnp.einsum('bhnd,hd->bhn', h, a_dst)
        e = e_i[:, :, :, None] + e_j[:, :, None, :]
        e = jax.nn.leaky_relu(e, negative_slope=ALPHA)
        e = e * time_weights[:, None, :, :]
        mask = adj_matrix[:, None, :, :] == 0
        e = jnp.where(mask, -jnp.inf, e)
        attention = jax.nn.softmax(e, axis=-1)
        out = jnp.einsum('bhij,bhjo->bhio', attention, h)
        out = jnp.transpose(out, (0, 2, 1, 3)).reshape(node_features.shape[0], node_features.shape[1], -1)
        return jax.nn.elu(out)
    x = _layernorm(x + _L0_gnn_ref(x, adj, L0_gnn_a), axis=-1)
    x = _layernorm(x + _L1_gnn_ref(x, adj, L1_gnn_a_0, L1_gnn_a_1, L1_gnn_a_2, L1_gnn_a_3), axis=-1)
    x = _layernorm(x + _L2_gnn_ref(x, adj, L2_gnn_W, L2_gnn_b, L2_gnn_att_src, L2_gnn_att_dst), axis=-1)
    x = _layernorm(x + _L3_gnn_ref(x, adj, adj, L3_gnn_W, L3_gnn_a), axis=-1)
    return x

_drawn_inputs = setup_inputs


def setup_inputs(seed=0):
    import zlib

    import numpy as np

    out = dict(_drawn_inputs(seed))
    spreads = {'L2_gnn_b': (0.0, 0.1)}
    factors = {}
    for name, (base, spread) in spreads.items():
        noise = np.random.default_rng([zlib.crc32(name.encode()), seed]).standard_normal(out[name].shape)
        drawn = base * np.exp(spread * noise) if base else spread * noise
        out[name] = jnp.asarray(drawn.astype(out[name].dtype))
    for name, factor in factors.items():
        out[name] = (out[name] * factor).astype(out[name].dtype)
    return out
```

```python
import concourse.bass as bass
from concourse import mybir
from concourse.alu_op_type import AluOpType as ALU
from contextlib import ExitStack

F32 = mybir.dt.float32
BF16 = mybir.dt.bfloat16
I32 = mybir.dt.int32
ACT = mybir.ActivationFunctionType
AX = mybir.AxisListType

B, N, D = 8, 1024, 128
T = N // 128
HALF = N // 2
SLOPE = 0.2
DECAY = 0.1
EPS = 1e-5
BIG = 4.5e16
STEEP = 1e30
NP = 3


CREDIT = 1


class Steps:

    def __init__(self, eng, sem, base):
        self.eng, self.sem, self.base, self.n = eng, sem, base, 0

    def done(self, ins):
        ins.then_inc(self.sem, 1)
        self.n += 1

    def carry(self):
        self.eng.sem_inc(self.sem, 1)
        self.n += 1

    def wait(self):
        self.eng.wait_ge(self.sem, self.base + self.n)


class Heads:

    def __init__(self, layer, heads):
        self.layer, self.H, self.C = layer, heads, D // heads
        self.W = self.C + 1
        self.QCOL = D + heads
        self.cols = D + 2 * heads


L2, L3 = Heads(2, 4), Heads(3, 8)


RELU_TILES = (1, 2, 3, 5, 6, 7)
CMP_TILES = (0, 4)
RELUS = len(RELU_TILES)


def is_first(h):
    return isinstance(h, int) and h == 0


def is_last(h, H):
    return isinstance(h, int) and h == H - 1


class AttentionSems:

    def __init__(self, sem, l):
        self.t_ready = sem(f"t_ready_{l}")
        self.xt_done = sem(f"xt_done_{l}")
        self.at_done = sem(f"at_done_{l}")
        self.s_ready = sem(f"s_ready_{l}")
        self.lift_done = sem(f"lift_done_{l}")
        self.e_done = sem(f"e_done_{l}")
        self.nm_ready = sem(f"nm_ready_{l}")
        self.p_ready = sem(f"p_ready_{l}")
        self.pt_ready = sem(f"pt_ready_{l}")
        self.pt_act = sem(f"pt_act_{l}")
        self.pt_dve = sem(f"pt_dve_{l}")
        self.pv_ready = sem(f"pv_ready_{l}")
        self.var_ready = sem(f"var_ready_{l}")
        self.rstd_ready = sem(f"rstd_ready_{l}")
        self.x_done = sem(f"x_done_{l}")


class HeadsSems:

    def __init__(self, sem, l):
        self.t_ready = sem(f"t_ready_{l}")
        self.xt_done = sem(f"xt_done_{l}")
        self.pj_ready = sem(f"pj_ready_{l}")
        self.xp_done = sem(f"xp_done_{l}")
        self.qr_ready = sem(f"qr_ready_{l}")
        self.q_hi = sem(f"q_hi_{l}")
        self.q_res = sem(f"q_res_{l}")
        self.q_mid = sem(f"q_mid_{l}")
        self.q_split = sem(f"q_split_{l}")
        self.qb_ready = sem(f"qb_ready_{l}")
        self.qb_evac = sem(f"qb_evac_{l}")
        self.krep_done = sem(f"krep_done_{l}")
        self.mb_ready = sem(f"mb_ready_{l}")
        self.shift_done = sem(f"shift_done_{l}")
        self.ac_done = sem(f"ac_done_{l}")
        self.cast1 = sem(f"cast1_{l}")
        self.res1 = sem(f"res1_{l}")
        self.cast2 = sem(f"cast2_{l}")
        self.parts_done = sem(f"parts_done_{l}")
        self.uv_done = sem(f"uv_done_{l}")
        self.mask_done = sem(f"mask_done_{l}")
        self.mv_ready = sem(f"mv_ready_{l}")
        self.mv_evac = sem(f"mv_evac_{l}")
        self.relu_done = sem(f"relu_done_{l}")
        self.cmp_done = sem(f"cmp_done_{l}")
        self.g_ready = sem(f"g_ready_{l}")
        self.o_ready = sem(f"o_ready_{l}")
        self.o_evac = sem(f"o_evac_{l}")
        self.combined = sem(f"combined_{l}")
        self.neg_out = sem(f"neg_out_{l}")
        self.exp_out = sem(f"exp_out_{l}")
        self.var_ready = sem(f"var_ready_{l}")
        self.rstd_ready = sem(f"rstd_ready_{l}")
        self.x_done = sem(f"x_done_{l}")


class KindSems:

    def __init__(self, sem, l):
        self.kind_mask = sem(f"kind_mask_{l}")
        self.kind_ready = sem(f"kind_ready_{l}")
        self.kind_lift = sem(f"kind_lift_{l}")
        self.kind_sum = sem(f"kind_sum_{l}")
        self.kind_max = sem(f"kind_max_{l}")


class GeneralSems:

    def __init__(self, sem, l):
        self.row_loaded = sem(f"row_loaded_{l}")
        self.row_less = sem(f"row_less_{l}")
        self.tw_done = sem(f"tw_done_{l}")
        self.tw_ready = sem(f"tw_ready_{l}")
        self.tw_evac = sem(f"tw_evac_{l}")
        self.q_ready = sem(f"q_ready_{l}")
        self.q_evac = sem(f"q_evac_{l}")
        self.q_max = sem(f"q_max_{l}")
        self.shift = sem(f"shift_{l}")
        self.values = sem(f"values_{l}")
        self.z_sum = sem(f"z_sum_{l}")
        self.z_leaky = sem(f"z_leaky_{l}")
        self.z_done = sem(f"z_done_{l}")
        self.p_exp = sem(f"p_exp_{l}")
        self.p_done = sem(f"p_done_{l}")
        self.mm_done = sem(f"mm_done_{l}")
        self.acc_done = sem(f"acc_done_{l}")


def each_head(eng, H, body):
    body(0, 0)
    with eng.Fori(0, H // 2 - 1) as pair:
        body(2 * pair + 1, 1)
        body(2 * pair + 2, 0)
    body(H - 1, 1)


def build(nc, x, adj, a0, a10, a11, a12, a13, w2, b2, src2, dst2, w3, a3, out):
    ctx = ExitStack()
    with ctx:
        def sb(name, shape, dt=F32):
            return ctx.enter_context(nc.sbuf_tensor(name, shape, dt))

        def sem(name):
            return ctx.enter_context(nc.semaphore(name))

        identf = sb("identf", [128, 128])
        identb = sb("identb", [128, 128], BF16)
        ones = sb("ones", [128, 128])
        neg_half = sb("neg_half", [128, 1])
        glob01 = sb("glob01", [128, 1])
        decay_bias = sb("decay_bias", [128, 1])
        exponent = sb("exponent", [128, T])
        a01 = sb("a01", [128, 8])
        w2_nat = sb("w2_nat", [128, 128])
        w3_cat = sb("w3_cat", [128, 128])
        w3_nat = sb("w3_nat", [128, 128])
        b2_row = sb("b2_row", [1, 128])
        b2_col = sb("b2_col", [128, 1])
        b2_rep = sb("b2_rep", [128, 128])
        att = {2: sb("att2", [128, 8]), 3: sb("att3", [128, 16])}
        wall = {2: sb("wall2", [128, 136]), 3: sb("wall3", [128, 144])}
        bias2 = sb("bias2", [128, 136])
        sel = sb("sel", [128, 8, 128], BF16)
        kmax = sb("kmax", [128, 16])
        ksq = sb("ksq", [128, 16])
        stat = sb("stat", [128, 2])
        srep = sb("srep", [128, 2, 128])
        glob = sb("glob", [128, 2])
        flagf = sb("flagf", [128, 1])
        flag = sb("flag", [128, 1], I32)
        tau = sb("tau", [128, 1])
        adj_in = sb("adj_in", [128, T, N], I32)
        code = sb("code", [128, T, N], BF16)
        codeT = sb("codeT", [128, T, N], BF16)
        mask = sb("mask", [128, T, N], BF16)
        x_in = sb("x_in", [128, T, D])
        X = [sb("X0", [128, T, D]), sb("X1", [128, T, D]), sb("y_out", [128, T, D])]
        xT = sb("xT", [128, N])
        aT = sb("aT", [128, N])
        G = sb("G", [128, 2, T, N], BF16)
        scratch = G[:, :, :, :].rearrange("p a t n -> p (a t n)").bitcast(F32)
        E = [scratch[:, 0:N], scratch[:, N:2 * N]]
        P = [scratch[:, 2 * N:3 * N], scratch[:, 3 * N:4 * N]]
        PT = [scratch[:, 4 * N:5 * N], scratch[:, 5 * N:6 * N]]
        EK = scratch[:, 6 * N:7 * N]
        NK = scratch[:, 7 * N:7 * N + HALF].bitcast(BF16)
        aK = scratch[:, 7 * N + HALF:7 * N + HALF + 128]
        twT = scratch.rearrange("p (t n) -> p t n", t=T)
        squares = scratch[:, 0:4 * N]
        rmax = sb("rmax", [128, T])
        nmax = sb("nmax", [128, T])
        den = sb("den", [128, T])
        rden = sb("rden", [128, T])
        Z = sb("Z", [128, T, D])
        stats = sb("stats", [128, T, 6])
        mv = sb("mv", [128, T, 2])
        vare = sb("vare", [128, T])
        rstd = sb("rstd", [128, T])
        XP = sb("XP", [128, T, 144])
        q_parts = sb("q_parts", [128, N], BF16)
        q_mid = sb("q_mid", [8, N], BF16)
        q_res = sb("q_res", [8, N])
        QB = [sb("QB0", [128, N]), sb("QB1", [128, N])]
        kml = sb("kml", [128, 8])
        krep = aT[:, :].rearrange("p (h n) -> p h n", h=8)
        Mb = sb("Mb", [128, 8])
        nkey = sb("nkey", [128, T, 8])
        thr = sb("thr", [128, T, 8])
        kbig = sb("kbig", [128, T, 8])
        R = sb("R", [128, T, 8])
        UVf = sb("UVf", [128, T * 272])
        RSf = sb("RSf", [128, T * 272])
        PCf = sb("PCf", [128, T * 3 * 272], BF16)
        parts_f = PCf[:, 0:6 * N].bitcast(F32)
        ZT, PX, PM = (parts_f[:, k * N:(k + 1) * N] for k in range(3))
        VG = UVf[:, 0:T * L3.W].rearrange("p (t c) -> p t c", t=T)
        adj_row = QB[1][:, :].bitcast(I32)
        q_most = sb("q_most", [128, 1])
        neg_most = sb("neg_most", [128, 1])
        MVf = sb("MVf", [128, T * 136])
        TTf = RSf
        O = UVf[:, 0:N].rearrange("p (t c) -> p t c", t=T)
        OE = UVf[:, N:2 * N].rearrange("p (t c) -> p t c", t=T)
        rd = sb("rd", [128, T * 8])

        bank = [ctx.enter_context(nc.psum_tensor(f"bank{i}", [128, 2, HALF], F32)) for i in range(4)]
        SP = [bank[0][:, :, :].rearrange("p a n -> p (a n)"), bank[1][:, :, :].rearrange("p a n -> p (a n)")]
        PTP = bank[2][:, :, :].rearrange("p a n -> p (a n)")
        ps_proj = [bank[1][:, 0, :], bank[1][:, 1, :]]
        ps_one = [bank[3][:, 0, :], bank[3][:, 1, :]]
        ct_ps = [p.bitcast(BF16) for p in ps_one]
        OP = [bank[2][:, 0, :], bank[2][:, 1, :], bank[3][:, 0, :], bank[3][:, 1, :]]

        def views(L):
            W, H = L.W, L.H
            uv = UVf[:, 0:T * H * 2 * W].rearrange("p (t h k c) -> p t h k c", t=T, h=H, k=2)
            rs = RSf[:, 0:T * H * 2 * W].rearrange("p (t h k) -> p t h k", t=T, h=H)
            pc = PCf[:, 0:T * H * NP * 2 * W].rearrange("p (t h n k) -> p t h n k", t=T, h=H, n=NP)
            mvv = MVf[:, 0:T * H * W].rearrange("p (t h c) -> p t h c", t=T, h=H)
            tt = TTf[:, 0:T * H * 2 * W].rearrange("p (t h k) -> p t h k", t=T, h=H)
            return uv, rs, pc, mvv, tt

        weights_in = sem("weights_in")
        const_done = sem("const_done")
        ident_done = sem("ident_done")
        sel_done = sem("sel_done")
        att_zero = sem("att_zero")
        att_in = sem("att_in")
        setup_pe = sem("setup_pe")
        setup_dve = sem("setup_dve")
        setup_act = sem("setup_act")
        adj_loaded = [sem("adj_loaded0"), sem("adj_loaded1")]
        scan_max = sem("scan_max")
        scan_sq = sem("scan_sq")
        x_loaded = sem("x_loaded")
        x0_room = sem("x0_room")
        x0_ready = sem("x0_ready")
        code_done = sem("code_done")
        neg_done = sem("neg_done")
        ct_ready = sem("ct_ready")
        ct_evac = sem("ct_evac")
        out_ready = sem("out_ready")
        out_stored = sem("out_stored")
        out_room = sem("out_room")
        wait_taken = sem("wait_taken")
        dve_steps = sem("dve_steps")
        act_steps = sem("act_steps")
        DVE_PER, ACT_PER = 256, 64

        s01 = [AttentionSems(sem, l) for l in range(2)]
        s23 = {l: HeadsSems(sem, l) for l in (2, 3)}
        kinds = [KindSems(sem, l) for l in range(2)]
        gen = GeneralSems(sem, 3)

        block = ctx.enter_context(nc.Block())
        x_v = x.rearrange("b (t p) d -> b p t d", p=128)
        out_v = out.rearrange("b (t p) d -> b p t d", p=128)
        adj_v = adj.rearrange("b (t p) n -> b p t n", p=128)

        n_weight_dmas = 13
        n_att_dmas = 24

        @block.sync
        def _(sp):
            for k in range(4):
                sp.dma_start(a01[:, k:k + 1], a0[k, :].rearrange("(d a) -> d a", a=1)).then_inc(weights_in, 16)
            for k, v in enumerate((a10, a11, a12, a13)):
                sp.dma_start(a01[:, 4 + k:5 + k], v).then_inc(weights_in, 16)
            sp.dma_start(w2_nat[:, :], w2).then_inc(weights_in, 16)
            sp.dma_start(w3_cat[:, :].rearrange("i (h o) -> i h o", h=8),
                         w3.rearrange("h i o -> i h o")).then_inc(weights_in, 16)
            sp.dma_start(wall[3][:, 0:128].rearrange("i (h o) -> i h o", h=8),
                         w3.rearrange("h i o -> i h o")).then_inc(weights_in, 16)
            sp.dma_start(b2_row[:, :], b2.rearrange("(a n) -> a n", a=1)).then_inc(weights_in, 16)
            sp.dma_start(b2_col[:, :], b2.rearrange("(n a) -> n a", a=1)).then_inc(weights_in, 16)
            sp.wait_ge(att_zero, 2)
            for h in range(4):
                sp.dma_start(att[2][32 * h:32 * h + 32, h:h + 1],
                             src2[0, h, :].rearrange("(c a) -> c a", a=1)).then_inc(att_in, 16)
                sp.dma_start(att[2][32 * h:32 * h + 32, 4 + h:5 + h],
                             dst2[0, h, :].rearrange("(c a) -> c a", a=1)).then_inc(att_in, 16)
            for h in range(8):
                sp.dma_start(att[3][16 * h:16 * h + 16, h:h + 1], a3[h, 16:32, :]).then_inc(att_in, 16)
                sp.dma_start(att[3][16 * h:16 * h + 16, 8 + h:9 + h], a3[h, 0:16, :]).then_inc(att_in, 16)
            with sp.Fori(0, B) as b:
                for h in range(2):
                    sp.wait_ge(scan_max, 2 * b + CREDIT)
                    sp.wait_ge(scan_sq, 2 * b + CREDIT)
                    sp.dma_start(adj_in[:, 4 * h:4 * h + 4, :], adj_v[b, :, 4 * h:4 * h + 4, :])\
                      .then_inc(adj_loaded[h], 16)
            sp.wait_ge(scan_max, 2 * B + CREDIT)
            sp.wait_ge(scan_sq, 2 * B + CREDIT)
            sp.wait_ge(setup_dve, 17)
            general = sp.value_load(flag[0:1, 0:1], min_val=0, max_val=1)
            with sp.Fori(0, B) as b:
                sp.wait_ge(x0_ready, b + CREDIT)
                sp.dma_start(x_in[:, :, :], x_v[b]).then_inc(x_loaded, 16)
                sp.wait_ge(code_done, T * b + CREDIT)
                for h in range(2):
                    sp.dma_start(adj_in[:, 4 * h:4 * h + 4, :], adj_v[b, :, 4 * h:4 * h + 4, :])\
                      .then_inc(adj_loaded[h], 16)
                with sp.If(general != 0):
                    for i in range(T):
                        if i == 0:
                            sp.wait_ge(gen.q_evac, L3.H * b + CREDIT)
                            sp.wait_ge(s23[2].x_done, b + 1)
                        else:
                            sp.wait_ge(gen.row_less, T * b + i)
                        sp.dma_start(adj_row, adj_v[b, :, i, :]).then_inc(gen.row_loaded, 16)
                with sp.Else():
                    sp.nop()
                sp.nop()

        @block.gpsimd
        def _(pool):
            for s in (scan_max, scan_sq, x0_ready, code_done, s23[3].t_ready, s23[3].x_done,
                      gen.q_evac, out_room, s23[2].o_ready, s23[3].o_ready, s23[2].cmp_done, s23[3].cmp_done):
                pool.sem_inc(s, CREDIT)
            pool.memset(att[2][:, :], 0.0).then_inc(att_zero, 1)
            pool.memset(att[3][:, :], 0.0).then_inc(att_zero, 1)
            pool.memset(identf[:, :], 0.0).then_inc(const_done, 1)
            pool.memset(identb[:, :], 0.0).then_inc(const_done, 1)
            pool.memset(ones[:, :], 1.0).then_inc(const_done, 1)
            pool.memset(neg_half[:, :], -0.5).then_inc(const_done, 1)
            pool.memset(exponent[:, :], -0.5).then_inc(const_done, 1)
            pool.memset(sel[:, :, :], 0.0).then_inc(const_done, 1)
            pool.memset(q_parts[:, :], 0.0).then_inc(const_done, 1)
            pool.wait_ge(const_done, 7)
            for n in range(NP):
                pool.affine_select(out=sel[:, :, :], in_=sel[:, :, :], compare_op=ALU.not_equal, fill=1.0,
                                   base=-32 * n, pattern=[[-1, 8], [0, 128]], channel_multiplier=1)\
                    .then_inc(sel_done, 1)
                pool.wait_ge(sel_done, n + 1)
            for m in (identf, identb):
                pool.affine_select(out=m[:, :], in_=m[:, :], compare_op=ALU.not_equal, fill=1.0, base=0,
                                   pattern=[[-1, 128]], channel_multiplier=1).then_inc(ident_done, 1)

            def inverse_root(s, want, c0, c1):
                pool.wait_ge(s.var_ready, want)
                pool.tensor_tensor(rstd[:, c0:c1], vare[:, c0:c1], exponent[:, c0:c1], ALU.pow)\
                    .then_inc(s.rstd_ready, 1)

            with pool.Fori(0, B) as b:
                pool.wait_ge(x_loaded, 16 * (b + 1))
                pool.wait_ge(s23[3].t_ready, b + CREDIT)
                pool.sem_inc(x0_room, 1)
                pool.tensor_copy(X[0][:, :, :], x_in[:, :, :]).then_inc(x0_ready, 1)
                for l in range(2):
                    for i in range(T):
                        inverse_root(s01[l], T * b + i + 1, i, i + 1)
                for l in (2, 3):
                    inverse_root(s23[l], b + 1, 0, T)
                pool.wait_ge(s23[3].x_done, b + 1 + CREDIT)
                pool.dma_start(out_v[b], X[2][:, :, :]).then_inc(out_stored, 16)
                pool.wait_ge(out_stored, 16 * (b + 1))
                pool.sem_inc(out_room, 1)

        @block.scalar
        def _(act):
            act.wait_ge(const_done, 7)
            with act.Fori(0, B) as b:
                for h in range(2):
                    act.wait_ge(adj_loaded[h], 16 * (b + 1))
                    act.wait_ge(scan_sq, 2 * b + h + CREDIT)
                    act.activation(squares, adj_in[:, 4 * h:4 * h + 4, :].rearrange("p t n -> p (t n)"),
                                   ACT.Square, bias=neg_half[:, 0:1],
                                   accum_out=ksq[:, bass.ds(2 * b + h, 1)]).then_inc(scan_sq, 1)
            act.wait_ge(setup_dve, 7)
            act.activation(tau[:, :], glob01[:, 0:1], ACT.Exp, bias=decay_bias[:, 0:1], scale=-DECAY)\
               .then_inc(setup_act, 1)

            act.wait_ge(setup_dve, 17)
            general = act.value_load(flag[0:1, 0:1], min_val=0, max_val=1)

            def attention(l, b):
                s = s01[l]
                act.wait_ge(s.t_ready, b + 1)
                act.activation(xT[:, :], SP[0], ACT.Copy).then_inc(s.xt_done, 1)

                def leaky(i):
                    act.wait_ge(s.s_ready, T * b + i + 1)
                    act.activation(E[i % 2], SP[i % 2], ACT.Relu, scale=SLOPE - 1.0).then_inc(s.lift_done, 1)
                    with act.If(general != 0):
                        for k in range(3):
                            act.wait_ge(kinds[l].kind_ready, 3 * (T * b + i) + k + 1)
                            if k >= 1:
                                act.wait_ge(kinds[l].kind_max, 3 * (T * b + i) + k)
                            act.activation(EK, SP[i % 2], ACT.Relu, scale=SLOPE - 1.0).then_inc(kinds[l].kind_lift, 1)
                    with act.Else():
                        act.nop()
                    act.nop()

                def expo(i):
                    act.wait_ge(s.nm_ready, T * b + i + 1)
                    if i >= 2:
                        act.wait_ge(s.pt_ready, T * b + i - 1)
                    act.activation(P[i % 2], E[i % 2], ACT.Exp, bias=nmax[:, i:i + 1],
                                   accum_out=den[:, i:i + 1]).then_inc(s.p_ready, 1)

                leaky(0)
                leaky(1)
                expo(0)
                for i in range(T):
                    if i + 2 < T:
                        act.wait_ge(s.p_ready, T * b + i + 1)
                        leaky(i + 2)
                    if i + 1 < T:
                        expo(i + 1)
                    act.wait_ge(s.pt_ready, T * b + i + 1)
                    if i >= 2:
                        act.wait_ge(s.pv_ready, T * b + i - 1)
                    act.activation(PT[i % 2][:, 0:HALF], PTP[:, 0:HALF], ACT.Copy).then_inc(s.pt_act, 1)

            def heads_layer(L, b):
                s, H, C, W, l = s23[L.layer], L.H, L.C, L.W, L.layer
                uv, rs, pc, mvv, tt = views(L)
                act.wait_ge(s.t_ready, b + 1 + (CREDIT if l == 3 else 0))
                act.activation(xT[:, :], SP[0], ACT.Copy).then_inc(s.xt_done, 1)

                def query_rows(h, par):
                    act.wait_ge(s.qb_ready, H * b + h + 1)
                    if l == 2:
                        act.activation(QB[par][:, :], SP[0], ACT.Identity,
                                       bias=bias2[:, bass.ds(L.QCOL + h, 1)]).then_inc(s.qb_evac, 1)
                    else:
                        act.activation(QB[par][:, :], SP[0], ACT.Copy).then_inc(s.qb_evac, 1)

                act.wait_ge(s.qr_ready, b + 1)
                act.activation(q_parts[0:H, :], SP[0][0:H, :], ACT.Copy).then_inc(s.q_hi, 1)
                act.wait_ge(s.q_res, b + 1)
                act.activation(q_mid[0:H, :], q_res[0:H, :], ACT.Copy).then_inc(s.q_mid, 1)
                act.activation(q_parts[32:32 + H, :], q_res[0:H, :], ACT.Copy).then_inc(s.q_mid, 1)
                query_rows(0, 0)
                act.wait_ge(s.shift_done, b + 1)
                act.activation(uv[:, :, :, 0, C], nkey[:, :, 0:H], ACT.Exp).then_inc(s.ac_done, 1)
                act.activation(uv[:, :, :, 1, C], nkey[:, :, 0:H], ACT.Exp, scale=SLOPE).then_inc(s.ac_done, 1)
                act.activation(R[:, :, 0:H], R[:, :, 0:H], ACT.Exp, scale=SLOPE - 1.0).then_inc(s.ac_done, 1)
                act.wait_ge(s.uv_done, b + 1)
                uvk = uv.rearrange("p t h k c -> p (t h) (k c)")
                act.activation(pc[:, :, :, 0, :].rearrange("p t h k -> p (t h) k"), uvk, ACT.Copy)\
                   .then_inc(s.cast1, 1)
                act.wait_ge(s.res1, b + 1)
                act.activation(pc[:, :, :, 1, :].rearrange("p t h k -> p (t h) k"),
                               rs.rearrange("p t h k -> p (t h) k"), ACT.Copy).then_inc(s.cast2, 1)

                def body(h, par):
                    act.wait_ge(s.qb_evac, H * b + h + 1)
                    if not is_first(h):
                        act.wait_ge(s.o_ready, 4 * (H * b + h - 1) + CREDIT)
                    for j in RELU_TILES:
                        act.activation(G[:, par, j, :], QB[par][:, :], ACT.Relu, scale=STEEP,
                                       bias=kbig[:, j, bass.ds(h, 1)]).then_inc(s.relu_done, 1)
                    if not is_last(h, H):
                        act.wait_ge(s.cmp_done, (T - RELUS) * (H * b + h) + CREDIT)
                        query_rows(h + 1, 1 - par)

                if l == 2:
                    each_head(act, H, body)
                else:
                    with act.If(general != 0):
                        general_weights(b)
                    with act.Else():
                        each_head(act, H, body)
                    act.nop()
                    act.wait_ge(s.neg_out, b + 1)
                    act.activation(OE[:, :, :], OE[:, :, :], ACT.Exp).then_inc(s.exp_out, 1)

            def general_weights(b):
                act.sem_inc(s23[3].qb_evac, L3.H - 1)
                for i in range(T):
                    act.wait_ge(gen.row_less, T * b + i + 1)
                    if i >= 1:
                        act.wait_ge(gen.tw_ready, T * b + i)
                    act.activation(PX, ZT, ACT.Exp, scale=DECAY).then_inc(gen.tw_done, 1)
                with act.Fori(0, L3.H) as h:
                    n = L3.H * b + h
                    act.wait_ge(gen.q_ready, n + 1)
                    act.activation(QB[0][:, :], SP[0], ACT.Copy).then_inc(gen.q_evac, 1)
                    for j in range(T):
                        act.wait_ge(gen.z_done, T * n + j + 1)
                        act.activation(PX, ZT, ACT.Exp, bias=neg_most[:, 0:1]).then_inc(gen.p_exp, 1)

            with act.Fori(0, B) as b:
                for j in range(T):
                    act.wait_ge(ct_ready, T * b + j + 1)
                    act.activation(codeT[:, j, :], ct_ps[j % 2], ACT.Copy).then_inc(ct_evac, 1)
                attention(0, b)
                attention(1, b)
                heads_layer(L2, b)
                heads_layer(L3, b)

        @block.vector
        def _(dve):
            with dve.Fori(0, B) as b:
                for h in range(2):
                    dve.wait_ge(adj_loaded[h], 16 * (b + 1))
                    dve.tensor_reduce(kmax[:, bass.ds(2 * b + h, 1)],
                                      adj_in[:, 4 * h:4 * h + 4, :].rearrange("p t n -> p (t n)"),
                                      AX.X, ALU.max).then_inc(scan_max, 1)
            dve.wait_ge(scan_max, 2 * B + CREDIT)
            dve.wait_ge(scan_sq, 2 * B + CREDIT)
            dve.tensor_reduce(stat[:, 0:1], kmax[:, :], AX.X, ALU.max).then_inc(setup_dve, 1)
            dve.tensor_reduce(stat[:, 1:2], ksq[:, :], AX.X, ALU.max).then_inc(setup_dve, 1)
            dve.wait_ge(setup_dve, 2)
            dve.tensor_copy(srep[:, :, :], stat[:, :].unsqueeze(2).to_broadcast([128, 2, 128]))\
               .then_inc(setup_dve, 1)
            dve.wait_ge(setup_pe, 1)
            dve.tensor_reduce(glob[:, :], ps_one[0][:, 0:256].rearrange("p (k n) -> p k n", k=2), AX.X, ALU.max)\
               .then_inc(setup_dve, 1)
            dve.wait_ge(setup_dve, 4)
            dve.tensor_scalar(flagf[:, :], glob[:, 1:2], 4 * N * 0.25, None, ALU.is_gt).then_inc(setup_dve, 1)
            dve.memset(decay_bias[:, :], DECAY).then_inc(setup_dve, 1)
            dve.tensor_scalar(glob01[:, :], glob[:, 0:1], 0.0, 1.0, ALU.max, ALU.min).then_inc(setup_dve, 1)
            dve.wait_ge(setup_dve, 7)
            dve.tensor_copy(flag[:, :], flagf[:, :]).then_inc(setup_dve, 1)
            dve.wait_ge(setup_act, 1)
            dve.tensor_scalar(tau[:, :], tau[:, :], -1.0, None, ALU.add).then_inc(setup_dve, 1)
            dve.tensor_scalar(flagf[:, :], flagf[:, :], -1.0, 1.0, ALU.mult, ALU.add).then_inc(setup_dve, 1)
            dve.wait_ge(setup_dve, 10)
            dve.tensor_tensor(tau[:, :], tau[:, :], flagf[:, :], ALU.mult).then_inc(setup_dve, 1)
            dve.wait_ge(setup_dve, 11)
            dve.tensor_scalar(tau[:, :], tau[:, :], 1.0, None, ALU.add).then_inc(setup_dve, 1)
            dve.wait_ge(setup_pe, 2)
            dve.tensor_copy(wall[2][:, 0:128], ps_one[1][:, 128:256])
            dve.tensor_copy(w3_nat[:, :], ps_one[1][:, 0:128]).then_inc(setup_dve, 1)
            dve.wait_ge(weights_in, 16 * n_weight_dmas)
            dve.tensor_copy(b2_rep[:, :], b2_col[:, 0:1].to_broadcast([128, 128])).then_inc(setup_dve, 1)
            dve.wait_ge(setup_dve, 14)
            dve.wait_ge(setup_pe, 3)
            dve.tensor_copy(wall[2][:, 128:136], SP[0][:, 0:8]).then_inc(setup_dve, 1)
            dve.tensor_scalar(wall[3][:, 128:144], SP[0][:, 8:24], tau[:, 0:1], None, ALU.mult).then_inc(setup_dve, 1)
            dve.tensor_copy(bias2[:, 0:136], SP[0][:, 32:168]).then_inc(setup_dve, 1)
            dve.wait_ge(setup_dve, 17)
            general = dve.value_load(flag[0:1, 0:1], min_val=0, max_val=1)

            def further_kinds(l, b, i):
                s, n = kinds[l], 3 * (T * b + i)
                for k in range(3):
                    dve.tensor_scalar(NK, code[:, i, :], float(k + 2), -BIG, ALU.not_equal, ALU.mult)\
                       .then_inc(s.kind_mask, 1)
                    dve.tensor_scalar(aK, xT[:, 128 * i:128 * i + 128], a01[:, 4 * l + k + 1:4 * l + k + 2], None,
                                      ALU.mult).then_inc(s.kind_mask, 1)
                    dve.wait_ge(s.kind_lift, n + k + 1)
                    dve.tensor_tensor(EK, SP[i % 2], EK, ALU.add).then_inc(s.kind_sum, 1)
                    dve.wait_ge(s.kind_sum, n + k + 1)
                    dve.tensor_tensor(E[i % 2], E[i % 2], EK, ALU.max).then_inc(s.kind_max, 1)
                    dve.wait_ge(s.kind_max, n + k + 1)
                dve.tensor_reduce(rmax[:, i:i + 1], E[i % 2], AX.X, ALU.max).then_inc(s.kind_mask, 1)
                dve.wait_ge(s.kind_mask, 7 * (T * b + i + 1))
                dve.sem_inc(wait_taken, 1)

            def attention(l, b, st):
                s = s01[l]
                src, dst = X[l], X[1 - l]
                dve.wait_ge(s.xt_done, b + 1)
                dve.tensor_scalar(aT[:, :], xT[:, :], a01[:, 4 * l:4 * l + 1], None, ALU.mult).then_inc(s.at_done, 1)

                def row_max(i):
                    dve.wait_ge(s.lift_done, T * b + i + 1)
                    st.carry()
                    dve.tensor_tensor_reduce(out=E[i % 2], in0=SP[i % 2], in1=E[i % 2], scale=1.0, scalar=-3e38,
                                             op0=ALU.add, op1=ALU.max, accum_out=rmax[:, i:i + 1])\
                       .then_inc(s.e_done, 1)
                    dve.wait_ge(s.e_done, T * b + i + 1)
                    dve.sem_inc(wait_taken, 1)
                    with dve.If(general != 0):
                        further_kinds(l, b, i)
                    with dve.Else():
                        dve.nop()
                    dve.tensor_scalar(nmax[:, i:i + 1], rmax[:, i:i + 1], -1.0, None, ALU.mult)\
                       .then_inc(s.nm_ready, 1)

                def finish(i):
                    dve.wait_ge(s.pv_ready, T * b + i + 1)
                    dve.wait_ge(s.p_ready, T * b + i + 1)
                    st.done(dve.reciprocal(rden[:, i:i + 1], den[:, i:i + 1]))
                    st.wait()
                    st.done(dve.scalar_tensor_tensor(Z[:, i, :], ps_one[i % 2][:, 0:D], rden[:, i:i + 1],
                                                     src[:, i, :], ALU.mult, ALU.add))
                    st.wait()
                    st.done(dve.bn_stats(stats[:, i, :], Z[:, i, :]))
                    st.wait()
                    st.carry()
                    st.done(dve.bn_aggr(mv[:, i, :], stats[:, i, :]))
                    st.wait()
                    dve.tensor_scalar(vare[:, i:i + 1], mv[:, i, 1:2], EPS, None, ALU.add).then_inc(s.var_ready, 1)

                def normal(i):
                    dve.wait_ge(s.rstd_ready, T * b + i + 1)
                    dve.tensor_scalar(dst[:, i, :], Z[:, i, :], mv[:, i, 0:1], rstd[:, i:i + 1],
                                      ALU.subtract, ALU.mult).then_inc(s.x_done, 1)

                row_max(0)
                row_max(1)
                for i in range(T):
                    if i + 2 < T:
                        row_max(i + 2)
                    dve.wait_ge(s.pt_ready, T * b + i + 1)
                    if i >= 2:
                        dve.wait_ge(s.pv_ready, T * b + i - 1)
                    dve.tensor_copy(PT[i % 2][:, HALF:N], PTP[:, HALF:N]).then_inc(s.pt_dve, 1)
                    if i >= 1:
                        finish(i - 1)
                    if i >= 2:
                        normal(i - 2)
                finish(T - 1)
                normal(T - 2)
                normal(T - 1)

            def general_heads(b, sums):
                s = s23[3]
                dve.wait_ge(s.mv_evac, T * (b + 1))
                dve.wait_ge(s.mask_done, T * (b + 1))
                dve.wait_ge(s.qb_evac, L3.H * b + 1)
                for i in range(T):
                    dve.wait_ge(gen.row_loaded, 16 * (T * b + i + 1))
                    if i >= 1:
                        dve.wait_ge(gen.tw_done, T * b + i)
                    dve.tensor_scalar(ZT, adj_row, glob[:, 0:1], None, ALU.subtract).then_inc(gen.row_less, 1)
                    dve.wait_ge(gen.tw_ready, T * b + i + 1)
                    dve.tensor_copy(twT[:, :, 128 * i:128 * i + 128], PTP.rearrange("p (t n) -> p t n", t=T))\
                       .then_inc(gen.tw_evac, 1)
                dve.wait_ge(gen.tw_evac, T * (b + 1))
                dve.sem_inc(wait_taken, 1)
                with dve.Fori(0, L3.H) as h:
                    n = L3.H * b + h
                    dve.memset(VG[:, :, L3.C:L3.W], 1.0).then_inc(gen.values, 1)
                    dve.tensor_copy(VG[:, :, 0:L3.C], XP[:, :, bass.ds(L3.C * h, L3.C)]).then_inc(gen.values, 1)
                    dve.wait_ge(gen.q_evac, n + 1 + CREDIT)
                    dve.tensor_reduce(q_most[:, :], QB[0][:, :], AX.X, ALU.max).then_inc(gen.q_max, 1)
                    dve.wait_ge(gen.q_max, n + 1)
                    dve.tensor_scalar(neg_most[:, :], q_most[:, :], Mb[:, bass.ds(h, 1)], 0.0, ALU.add, ALU.max)\
                       .then_inc(gen.shift, 1)
                    dve.wait_ge(gen.shift, 2 * n + 1)
                    dve.tensor_scalar(neg_most[:, :], neg_most[:, :], -1.0, None, ALU.mult).then_inc(gen.shift, 1)
                    dve.wait_ge(gen.shift, 2 * n + 2)
                    for j in range(T):
                        m = T * n + j
                        dve.tensor_scalar(PM, QB[0][:, :], XP[:, j, bass.ds(D + h, 1)], None, ALU.add)\
                           .then_inc(gen.z_sum, 1)
                        dve.wait_ge(gen.z_sum, m + 1)
                        dve.scalar_tensor_tensor(ZT, PM, SLOPE, PM, ALU.mult, ALU.max).then_inc(gen.z_leaky, 1)
                        dve.wait_ge(gen.z_leaky, m + 1)
                        dve.tensor_tensor(ZT, ZT, twT[:, j, :], ALU.mult).then_inc(gen.z_done, 1)
                        dve.wait_ge(gen.p_exp, m + 1)
                        dve.tensor_tensor(PM, PX, mask[:, j, :], ALU.mult).then_inc(gen.p_done, 1)
                        dve.wait_ge(gen.mm_done, m + 1)
                        part = PTP[:, 0:T * 32].rearrange("p (t c) -> p t c", t=T)[:, :, 0:L3.W]
                        whole = sums[:, :, bass.ds(h, 1), :].rearrange("p t h c -> p t (h c)")
                        if j == 0:
                            dve.tensor_copy(whole, part).then_inc(gen.acc_done, 1)
                        else:
                            dve.tensor_tensor(whole, whole, part, ALU.add).then_inc(gen.acc_done, 1)
                        dve.wait_ge(gen.acc_done, m + 1)
                    dve.sem_inc(wait_taken, 1)

            def heads_layer(L, b, st):
                s, H, C, W, l = s23[L.layer], L.H, L.C, L.W, L.layer
                uv, rs, pc, mvv, tt = views(L)
                src, dst = X[l - 2], X[l - 1]
                for j in range(T):
                    if l == 2:
                        if j == 0:
                            dve.wait_ge(ct_evac, T * b + T)
                        m = dve.tensor_scalar(mask[:, j, :], codeT[:, j, :], 0.0, None, ALU.is_gt)
                    else:
                        m = dve.tensor_scalar(mask[:, j, :], codeT[:, j, :], 0.0, None, ALU.not_equal)
                    if l == 3:
                        m.then_inc(s.mask_done, 1)
                if l == 2:
                    st.done(m)
                    st.wait()
                    for j in range(T):
                        dve.tensor_tensor(mask[:, j, 128 * j:128 * j + 128], mask[:, j, 128 * j:128 * j + 128],
                                          identb[:, :], ALU.max).then_inc(s.mask_done, 1)
                for j in range(T):
                    dve.wait_ge(s.pj_ready, T * b + j + 1)
                    ps = ps_proj[j % 2][:, 0:L.cols]
                    if l == 2:
                        dve.tensor_tensor(XP[:, j, 0:L.cols], ps, bias2[:, :], ALU.add).then_inc(s.xp_done, 1)
                    else:
                        dve.tensor_copy(XP[:, j, 0:L.cols], ps).then_inc(s.xp_done, 1)
                dve.wait_ge(s.qr_ready, b + 1)
                dve.wait_ge(s.q_hi, b + 1)
                dve.tensor_tensor(q_res[0:H, :], SP[0][0:H, :], q_parts[0:H, :], ALU.subtract).then_inc(s.q_res, 1)
                dve.wait_ge(s.q_res, b + 1)
                dve.wait_ge(s.q_mid, 2 * b + 2)
                dve.tensor_tensor(q_parts[64:64 + H, :], q_res[0:H, :], q_mid[0:H, :], ALU.subtract)\
                   .then_inc(s.q_split, 1)
                dve.wait_ge(s.xp_done, T * b + T)
                key = XP[:, :, D:D + H]
                qry = XP[:, :, D + H:D + 2 * H]
                st.done(dve.tensor_reduce(kml[:, 0:H], key.rearrange("p t h -> p h t"), AX.X, ALU.max))
                dve.tensor_scalar(thr[:, :, 0:H], key, -1.0, None, ALU.mult)
                dve.tensor_scalar(kbig[:, :, 0:H], key, STEEP, None, ALU.mult)
                st.wait()
                dve.tensor_copy(krep[:, 0:H, :], kml[:, 0:H].unsqueeze(2).to_broadcast([128, H, 128]))\
                   .then_inc(s.krep_done, 1)
                dve.wait_ge(s.mb_ready, b + 1)
                st.done(dve.tensor_reduce(Mb[:, 0:H], SP[1][:, 0:H * 128].rearrange("p (h n) -> p h n", h=H),
                                          AX.X, ALU.max))
                st.wait()
                mb_all = Mb[:, 0:H].unsqueeze(1).to_broadcast([128, T, H])
                st.done(dve.tensor_tensor(nkey[:, :, 0:H], key, mb_all, ALU.subtract))
                st.done(dve.tensor_tensor(R[:, :, 0:H], qry, mb_all, ALU.add))
                st.wait()
                dve.tensor_scalar(R[:, :, 0:H], R[:, :, 0:H], 0.0, None, ALU.max).then_inc(s.shift_done, 1)
                dve.wait_ge(s.ac_done, 3 * b + 2)
                xph = XP[:, :, 0:D].rearrange("p t (h c) -> p t h c", h=H)
                for k in range(2):
                    u = dve.tensor_tensor(uv[:, :, :, k, 0:C], xph,
                                          uv[:, :, :, k, C:W].to_broadcast([128, T, H, C]), ALU.mult)
                u.then_inc(s.uv_done, 1)
                uvk = uv.rearrange("p t h k c -> p (t h) (k c)")
                rsk = rs.rearrange("p t h k -> p (t h) k")
                part = [pc[:, :, :, n, :].rearrange("p t h k -> p (t h) k") for n in range(NP)]
                dve.wait_ge(s.uv_done, b + 1)
                dve.wait_ge(s.cast1, b + 1)
                dve.tensor_tensor(rsk, uvk, part[0], ALU.subtract).then_inc(s.res1, 1)
                dve.wait_ge(s.res1, b + 1)
                dve.wait_ge(s.cast2, b + 1)
                dve.tensor_tensor(part[2], rsk, part[1], ALU.subtract).then_inc(s.parts_done, 1)

                def mask_sums(i):
                    dve.wait_ge(s.mv_ready, T * b + i + 1)
                    dve.tensor_reduce(mvv[:, i, :, :], ps_proj[i % 2][:, 0:H * NP * W]
                                      .rearrange("p (h n c) -> p h c n", h=H, n=NP), AX.X, ALU.add)\
                       .then_inc(s.mv_evac, 1)

                for i in range(T):
                    mask_sums(i)

                def take(h, q):
                    dve.wait_ge(s.o_ready, 4 * (H * b + h) + q + 1 + CREDIT)
                    dve.tensor_reduce(tt[:, 2 * q:2 * q + 2, bass.ds(h, 1), :].rearrange("p i h k -> p i (h k)"),
                                      OP[q].rearrange("p (i c) -> p i c", i=2)[:, :, 0:NP * 2 * W]
                                      .rearrange("p i (n k) -> p i k n", n=NP), AX.X, ALU.add)\
                       .then_inc(s.o_evac, 1)

                def body(h, par):
                    first = is_first(h)
                    dve.wait_ge(s.qb_evac, H * b + h + 1)
                    if not first:
                        dve.wait_ge(s.o_ready, 4 * (H * b + h - 1) + CREDIT)
                    for j in CMP_TILES:
                        dve.tensor_scalar(G[:, par, j, :], QB[par][:, :], thr[:, j, bass.ds(h, 1)], None,
                                          ALU.is_ge).then_inc(s.cmp_done, 1)
                    seen = 0
                    cmps = 0
                    for j in range(T):
                        if j in RELU_TILES:
                            seen += 1
                            dve.wait_ge(s.relu_done, RELUS * (H * b + h) + seen)
                        else:
                            cmps += 1
                            dve.wait_ge(s.cmp_done, (T - RELUS) * (H * b + h) + cmps + CREDIT)
                        dve.tensor_tensor(G[:, par, j, :], G[:, par, j, :], mask[:, j, :], ALU.min)\
                           .then_inc(s.g_ready, 1)
                        if j % 2 and not first:
                            take(h - 1, j // 2)

                def fast():
                    each_head(dve, H, body)
                    for q in range(4):
                        take(H - 1, q)
                    dve.wait_ge(s.o_evac, 4 * H * (b + 1))
                    dve.wait_ge(s.mv_evac, T * (b + 1))
                    dve.wait_ge(s.ac_done, 3 * b + 3)
                    ttv, ttu = tt[:, :, :, W:2 * W], tt[:, :, :, 0:W]
                    dve.tensor_tensor(mvv, mvv, ttv, ALU.subtract).then_inc(s.combined, 1)
                    dve.wait_ge(s.combined, 3 * b + 1)
                    dve.tensor_tensor(mvv, mvv, R[:, :, 0:H].unsqueeze(3).to_broadcast([128, T, H, W]), ALU.mult)\
                       .then_inc(s.combined, 1)
                    dve.wait_ge(s.combined, 3 * b + 2)
                    dve.tensor_tensor(mvv, mvv, ttu, ALU.add).then_inc(s.combined, 1)
                    dve.wait_ge(s.combined, 3 * b + 3)
                    dve.sem_inc(wait_taken, 1)

                if l == 2:
                    fast()
                else:
                    with dve.If(general != 0):
                        general_heads(b, mvv)
                    with dve.Else():
                        fast()
                rdh = rd[:, 0:T * H].rearrange("p (t h) -> p t h", t=T)
                st.done(dve.reciprocal(rdh, mvv[:, :, :, C]))
                st.wait()
                st.done(dve.tensor_tensor(O[:, :, :].rearrange("p t (h c) -> p t h c", h=H), mvv[:, :, :, 0:C],
                                          rdh.unsqueeze(3).to_broadcast([128, T, H, C]), ALU.mult))
                st.wait()
                if l == 3:
                    dve.tensor_scalar(OE[:, :, :], O[:, :, :], 0.0, None, ALU.min).then_inc(s.neg_out, 1)
                    st.done(dve.tensor_scalar(O[:, :, :], O[:, :, :], 0.0, -1.0, ALU.max, ALU.add))
                    st.wait()
                    dve.wait_ge(s.exp_out, b + 1)
                    st.done(dve.tensor_tensor(O[:, :, :], O[:, :, :], OE[:, :, :], ALU.add))
                    st.wait()
                st.done(dve.tensor_tensor(Z[:, :, :], O[:, :, :], src[:, :, :], ALU.add))
                st.wait()
                for i in range(T):
                    m = dve.bn_stats(stats[:, i, :], Z[:, i, :])
                st.done(m)
                st.wait()
                st.carry()
                for i in range(T):
                    m = dve.bn_aggr(mv[:, i, :], stats[:, i, :])
                st.done(m)
                st.wait()
                dve.tensor_scalar(vare[:, :], mv[:, :, 1], EPS, None, ALU.add).then_inc(s.var_ready, 1)
                dve.wait_ge(s.rstd_ready, b + 1)
                if l == 3:
                    dve.wait_ge(out_room, b + CREDIT)
                for i in range(T):
                    m = dve.tensor_scalar(dst[:, i, :], Z[:, i, :], mv[:, i, 0:1], rstd[:, i:i + 1],
                                          ALU.subtract, ALU.mult)
                m.then_inc(s.x_done, 1)

            with dve.Fori(0, B) as b:
                for i in range(T):
                    if i % 4 == 0:
                        dve.wait_ge(adj_loaded[i // 4], 16 * (B + b + 1))
                    dve.tensor_scalar(code[:, i, :], adj_in[:, i, :], -1.0, 5.0, ALU.max, ALU.min)\
                       .then_inc(code_done, 1)
                for i in range(T):
                    dve.wait_ge(code_done, T * b + i + 1 + CREDIT)
                    dve.tensor_scalar(mask[:, i, :], code[:, i, :], 1.0, -BIG, ALU.not_equal, ALU.mult)\
                       .then_inc(neg_done, 1)
                st = Steps(dve, dve_steps, DVE_PER * b)
                attention(0, b, st)
                attention(1, b, st)
                heads_layer(L2, b, st)
                heads_layer(L3, b, st)
                dve.sem_inc(dve_steps, DVE_PER - st.n)

        @block.tensor
        def _(pe):
            pe.wait_ge(ident_done, 2)
            pe.wait_ge(setup_dve, 3)
            for k in range(2):
                mm = pe.matmul(ps_one[0][:, 128 * k:128 * k + 128], srep[:, k, :], identf[:, :], start=True, stop=True)
            mm.then_inc(setup_pe, 1)
            pe.wait_ge(weights_in, 16 * n_weight_dmas)
            pe.wait_ge(att_in, 16 * n_att_dmas)
            pe.transpose(ps_one[1][:, 0:128], w3_cat[:, :], identf[:, :])
            pe.transpose(ps_one[1][:, 128:256], w2_nat[:, :], identf[:, :]).then_inc(setup_pe, 1)
            pe.wait_ge(setup_dve, 14)
            pe.matmul(SP[0][:, 0:8], w2_nat[:, :], att[2][:, :], start=True, stop=True)
            pe.matmul(SP[0][:, 8:24], w3_nat[:, :], att[3][:, :], start=True, stop=True)
            pe.matmul(SP[0][:, 32:160], ones[0:1, :], b2_row[:, :], start=True, stop=True)
            pe.matmul(SP[0][:, 160:168], b2_rep[:, :], att[2][:, :], start=True, stop=True).then_inc(setup_pe, 1)
            pe.wait_ge(setup_dve, 17)
            pe.wait_ge(sel_done, NP)

            general = pe.value_load(flag[0:1, 0:1], min_val=0, max_val=1)

            def further_kinds(l, b, i):
                s, n = kinds[l], 3 * (T * b + i)
                pe.wait_ge(s01[l].e_done, T * b + i + 1)
                for k in range(3):
                    pe.wait_ge(s.kind_mask, 7 * (T * b + i) + 2 * k + 2)
                    if k >= 1:
                        pe.wait_ge(s.kind_sum, n + k)
                    for c in range(2):
                        o = SP[i % 2][:, c * HALF:(c + 1) * HALF]
                        pe.matmul(o, aK, xT[:, c * HALF:(c + 1) * HALF], start=True, stop=False)
                        mm = pe.matmul(o, identb[:, :], NK[:, c * HALF:(c + 1) * HALF], start=False, stop=True)
                    mm.then_inc(s.kind_ready, 1)
                pe.wait_ge(s.kind_sum, n + 3)

            def general_heads(b):
                pe.sem_inc(s23[3].qb_ready, L3.H - 1)
                for i in range(T):
                    pe.wait_ge(gen.tw_done, T * b + i + 1)
                    if i >= 1:
                        pe.wait_ge(gen.tw_evac, T * b + i)
                    for j in range(T):
                        mm = pe.transpose(PTP[:, 128 * j:128 * j + 128], PX[:, 128 * j:128 * j + 128], identf[:, :])
                    mm.then_inc(gen.tw_ready, 1)
                with pe.Fori(0, L3.H) as h:
                    n = L3.H * b + h
                    pe.wait_ge(gen.q_evac, n + CREDIT)
                    for c in range(2):
                        mm = pe.matmul(SP[0][:, c * HALF:(c + 1) * HALF],
                                       sel[:, bass.ds(h, 1), :].rearrange("p h n -> p (h n)"),
                                       q_parts[:, c * HALF:(c + 1) * HALF], start=True, stop=True)
                    mm.then_inc(gen.q_ready, 1)
                    for j in range(T):
                        pe.wait_ge(gen.p_done, T * n + j + 1)
                        pe.wait_ge(gen.values, 2 * n + 2)
                        for i in range(T):
                            mm = pe.matmul(PTP[:, 32 * i:32 * i + L3.W], PM[:, 128 * i:128 * i + 128], VG[:, j, :],
                                           start=True, stop=True)
                        mm.then_inc(gen.mm_done, 1)

            def transposes(s, src, b):
                for i in range(T):
                    mm = pe.transpose(SP[0][:, 128 * i:128 * i + 128], src[:, i, :], identf[:, :])
                mm.then_inc(s.t_ready, 1)

            def attention(l, b):
                s = s01[l]
                src = X[l]
                if l == 0:
                    pe.wait_ge(x0_ready, b + 1 + CREDIT)
                else:
                    pe.wait_ge(s01[0].x_done, T * (b + 1))
                transposes(s, src, b)

                def scores(i):
                    if i >= 2:
                        pe.wait_ge(s.e_done, T * b + i - 1)
                    if i == 0:
                        pe.wait_ge(s.xt_done, b + 1)
                        pe.wait_ge(s.at_done, b + 1)
                    if l == 0:
                        pe.wait_ge(neg_done, T * b + i + 1)
                    for n in range(2):
                        o = SP[i % 2][:, n * HALF:(n + 1) * HALF]
                        pe.matmul(o, aT[:, 128 * i:128 * i + 128], xT[:, n * HALF:(n + 1) * HALF],
                                  start=True, stop=False)
                        mm = pe.matmul(o, identb[:, :], mask[:, i, n * HALF:(n + 1) * HALF], start=False, stop=True)
                    mm.then_inc(s.s_ready, 1)
                    with pe.If(general != 0):
                        further_kinds(l, b, i)
                    with pe.Else():
                        pe.nop()
                    pe.nop()

                scores(0)
                scores(1)
                for i in range(T):
                    pe.wait_ge(s.p_ready, T * b + i + 1)
                    if i >= 1:
                        pe.wait_ge(s.pt_act, T * b + i)
                        pe.wait_ge(s.pt_dve, T * b + i)
                    for j in range(T):
                        mm = pe.transpose(PTP[:, 128 * j:128 * j + 128], P[i % 2][:, 128 * j:128 * j + 128],
                                          identf[:, :])
                    mm.then_inc(s.pt_ready, 1)
                    if i + 2 < T:
                        scores(i + 2)
                    pe.wait_ge(s.pt_act, T * b + i + 1)
                    pe.wait_ge(s.pt_dve, T * b + i + 1)
                    if i >= 2:
                        pe.wait_ge(s.var_ready, T * b + i - 1)
                    for j in range(T):
                        mm = pe.matmul(ps_one[i % 2][:, 0:D], PT[i % 2][:, 128 * j:128 * j + 128], src[:, j, :],
                                       start=(j == 0), stop=(j == T - 1))
                    mm.then_inc(s.pv_ready, 1)

            def heads_layer(L, b):
                s, H, C, W, l = s23[L.layer], L.H, L.C, L.W, L.layer
                uv, rs, pc, mvv, tt = views(L)
                if l == 2:
                    pe.wait_ge(s01[1].x_done, T * (b + 1))
                else:
                    pe.wait_ge(s23[2].x_done, b + 1)
                transposes(s, X[l - 2], b)
                pe.wait_ge(s.xt_done, b + 1)

                for j in range(T):
                    if j >= 2:
                        pe.wait_ge(s.xp_done, T * b + j - 1)
                    pe.matmul(ps_proj[j % 2][:, 0:L.cols], xT[:, 128 * j:128 * j + 128], wall[l][:, :],
                              start=True, stop=True).then_inc(s.pj_ready, 1)
                for n in range(2):
                    mm = pe.matmul(SP[0][0:H, n * HALF:(n + 1) * HALF], wall[l][:, L.QCOL:L.QCOL + H],
                                   xT[:, n * HALF:(n + 1) * HALF], start=True, stop=True)
                mm.then_inc(s.qr_ready, 1)

                def query_rows(h):
                    for n in range(2):
                        mm = pe.matmul(SP[0][:, n * HALF:(n + 1) * HALF],
                                       sel[:, bass.ds(h, 1), :].rearrange("p h n -> p (h n)"),
                                       q_parts[:, n * HALF:(n + 1) * HALF], start=True, stop=True)
                    mm.then_inc(s.qb_ready, 1)

                pe.wait_ge(s.q_mid, 2 * b + 2)
                pe.wait_ge(s.q_split, b + 1)
                query_rows(0)
                pe.wait_ge(s.xp_done, T * b + T)
                pe.wait_ge(s.krep_done, b + 1)
                for h in range(H):
                    mm = pe.matmul(SP[1][:, 128 * h:128 * h + 128], krep[:, h, :], identf[:, :], start=True, stop=True)
                mm.then_inc(s.mb_ready, 1)
                pe.wait_ge(s.parts_done, b + 1)
                pe.wait_ge(s.shift_done, b + 1)
                pe.wait_ge(s.mask_done, T * (b + 1))
                for i in range(T):
                    if i >= 2:
                        pe.wait_ge(s.mv_evac, T * b + i - 1)
                    for j in range(T):
                        mm = pe.matmul(ps_proj[i % 2][:, 0:H * NP * W], mask[:, j, 128 * i:128 * i + 128],
                                       pc[:, j, :, :, W:2 * W].rearrange("p h n c -> p (h n) c"),
                                       start=(j == 0), stop=(j == T - 1))
                    mm.then_inc(s.mv_ready, 1)

                def body(h, par):
                    if not is_last(h, H):
                        pe.wait_ge(s.qb_evac, H * b + h + 1)
                        query_rows(h + 1)
                    for i in range(T):
                        if i == 0:
                            pe.wait_ge(s.g_ready, T * (H * b + h + 1))
                        if i % 2 == 0 and not is_first(h):
                            pe.wait_ge(s.o_evac, 4 * (H * b + h - 1) + i // 2 + 1)
                        for j in range(T):
                            mm = pe.matmul(OP[i // 2].rearrange("p (i c) -> p i c", i=2)[:, i % 2, 0:NP * 2 * W],
                                           G[:, par, j, 128 * i:128 * i + 128],
                                           pc[:, j, bass.ds(h, 1), :, :].rearrange("p h n k -> p (h n k)"),
                                           start=(j == 0), stop=(j == T - 1))
                        if i % 2:
                            mm.then_inc(s.o_ready, 1)

                if l == 2:
                    each_head(pe, H, body)
                else:
                    with pe.If(general != 0):
                        general_heads(b)
                    with pe.Else():
                        each_head(pe, H, body)
                    pe.nop()

            with pe.Fori(0, B) as b:
                pe.wait_ge(s23[3].x_done, b + CREDIT)
                for j in range(T):
                    if j >= 2:
                        pe.wait_ge(ct_evac, T * b + j - 1)
                    for i in range(T):
                        if j == 0:
                            pe.wait_ge(code_done, T * b + i + 1 + CREDIT)
                        mm = pe.transpose(ct_ps[j % 2][:, 128 * i:128 * i + 128], code[:, i, 128 * j:128 * j + 128],
                                          identb[:, :])
                    mm.then_inc(ct_ready, 1)
                attention(0, b)
                attention(1, b)
                heads_layer(L2, b)
                heads_layer(L3, b)


_INS = ["x", "adj", "L0_gnn_a", "L1_gnn_a_0", "L1_gnn_a_1", "L1_gnn_a_2", "L1_gnn_a_3", "L2_gnn_W", "L2_gnn_b",
        "L2_gnn_att_src", "L2_gnn_att_dst", "L3_gnn_W", "L3_gnn_a"]


def kernel(**inputs):
    import numpy as _np
    import concourse.bacc as _bacc
    from concourse import mybir as _mybir
    from concourse.bass_utils import run_bass_kernel_spmd as _run

    nc = _bacc.Bacc("TRN2", target_bir_lowering=False, num_devices=1)
    arrays, args = {}, []
    for name in _INS:
        a = _np.ascontiguousarray(inputs[name])
        arrays[f"in_{name}_dram"] = a
        args.append(nc.dram_tensor(f"in_{name}_dram", a.shape, _mybir.dt.from_np(a.dtype), kind="ExternalInput").ap())
    out = nc.dram_tensor("out_dram", (B, N, D), F32, kind="ExternalOutput").ap()
    build(nc, *args, out)
    r = _run(nc, [arrays], core_ids=[0])
    return r.results[0]["out_dram"]
```

```python
import concourse.bass as bass
from concourse import mybir
from concourse.alu_op_type import AluOpType as ALU
from contextlib import ExitStack

F32 = mybir.dt.float32
BF16 = mybir.dt.bfloat16
I32 = mybir.dt.int32
ACT = mybir.ActivationFunctionType
AX = mybir.AxisListType

B, N, D = 8, 1024, 128
T = N // 128
HALF = N // 2
SLOPE = 0.2
DECAY = 0.1
EPS = 1e-5
BIG = 4.5e16
STEEP = 1e30
NP = 3


SCANNED = 2
CODED = 3
CREDIT = 1


class Steps:

    def __init__(self, eng, sem, base):
        self.eng, self.sem, self.base, self.n = eng, sem, base, 0

    def done(self, ins):
        ins.then_inc(self.sem, 1)
        self.n += 1

    def carry(self):
        self.eng.sem_inc(self.sem, 1)
        self.n += 1

    def wait(self):
        self.eng.wait_ge(self.sem, self.base + self.n)


class Heads:

    def __init__(self, layer, heads):
        self.layer, self.H, self.C = layer, heads, D // heads
        self.W = self.C + 1
        self.QCOL = D + heads
        self.cols = D + 2 * heads


L2, L3 = Heads(2, 4), Heads(3, 8)


CT = 2
CHUNKS = T // CT
def is_first(h):
    return isinstance(h, int) and h == 0


def is_last(h, H):
    return isinstance(h, int) and h == H - 1


class AttentionSems:

    def __init__(self, sem, l):
        self.t_ready = sem(f"t_ready_{l}")
        self.xt_done = sem(f"xt_done_{l}")
        self.at_done = sem(f"at_done_{l}")
        self.s_ready = sem(f"s_ready_{l}")
        self.lift_done = sem(f"lift_done_{l}")
        self.e_done = sem(f"e_done_{l}")
        self.nm_ready = sem(f"nm_ready_{l}")
        self.p_ready = sem(f"p_ready_{l}")
        self.pt_ready = sem(f"pt_ready_{l}")
        self.pt_act = sem(f"pt_act_{l}")
        self.pt_dve = sem(f"pt_dve_{l}")
        self.pv_ready = sem(f"pv_ready_{l}")
        self.var_ready = sem(f"var_ready_{l}")
        self.rstd_ready = sem(f"rstd_ready_{l}")
        self.x_done = sem(f"x_done_{l}")


class HeadsSems:

    def __init__(self, sem, l):
        self.t_ready = sem(f"t_ready_{l}")
        self.xt_done = sem(f"xt_done_{l}")
        self.pj_ready = sem(f"pj_ready_{l}")
        self.xp_done = sem(f"xp_done_{l}")
        self.qr_ready = sem(f"qr_ready_{l}")
        self.q_hi = sem(f"q_hi_{l}")
        self.q_res = sem(f"q_res_{l}")
        self.q_mid = sem(f"q_mid_{l}")
        self.q_split = sem(f"q_split_{l}")
        self.qb_ready = sem(f"qb_ready_{l}")
        self.krep_done = sem(f"krep_done_{l}")
        self.mb_ready = sem(f"mb_ready_{l}")
        self.shift_done = sem(f"shift_done_{l}")
        self.ac_done = sem(f"ac_done_{l}")
        self.cast1 = sem(f"cast1_{l}")
        self.res1 = sem(f"res1_{l}")
        self.cast2 = sem(f"cast2_{l}")
        self.parts_done = sem(f"parts_done_{l}")
        self.uv_done = sem(f"uv_done_{l}")
        self.mask_done = sem(f"mask_done_{l}")
        self.mv_ready = sem(f"mv_ready_{l}")
        self.mv_evac = sem(f"mv_evac_{l}")
        self.relu_done = sem(f"relu_done_{l}")
        self.g_ready = sem(f"g_ready_{l}")
        self.o_ready = sem(f"o_ready_{l}")
        self.o_evac = sem(f"o_evac_{l}")
        self.combined = sem(f"combined_{l}")
        self.neg_out = sem(f"neg_out_{l}")
        self.exp_out = sem(f"exp_out_{l}")
        self.var_ready = sem(f"var_ready_{l}")
        self.rstd_ready = sem(f"rstd_ready_{l}")
        self.x_done = sem(f"x_done_{l}")


class KindSems:

    def __init__(self, sem, l):
        self.kind_mask = sem(f"kind_mask_{l}")
        self.kind_ready = sem(f"kind_ready_{l}")
        self.kind_lift = sem(f"kind_lift_{l}")
        self.kind_sum = sem(f"kind_sum_{l}")
        self.kind_max = sem(f"kind_max_{l}")


class GeneralSems:

    def __init__(self, sem, l):
        self.row_loaded = sem(f"row_loaded_{l}")
        self.row_less = sem(f"row_less_{l}")
        self.tw_done = sem(f"tw_done_{l}")
        self.tw_ready = sem(f"tw_ready_{l}")
        self.tw_evac = sem(f"tw_evac_{l}")
        self.q_ready = sem(f"q_ready_{l}")
        self.q_evac = sem(f"q_evac_{l}")
        self.q_max = sem(f"q_max_{l}")
        self.shift = sem(f"shift_{l}")
        self.values = sem(f"values_{l}")
        self.z_sum = sem(f"z_sum_{l}")
        self.z_leaky = sem(f"z_leaky_{l}")
        self.z_done = sem(f"z_done_{l}")
        self.p_exp = sem(f"p_exp_{l}")
        self.p_done = sem(f"p_done_{l}")
        self.mm_done = sem(f"mm_done_{l}")
        self.acc_done = sem(f"acc_done_{l}")


def each_head(eng, H, body):
    body(0, 0)
    with eng.Fori(0, H // 2 - 1) as pair:
        body(2 * pair + 1, 1)
        body(2 * pair + 2, 0)
    body(H - 1, 1)


def build(nc, x, adj, a0, a10, a11, a12, a13, w2, b2, src2, dst2, w3, a3, out):
    ctx = ExitStack()
    with ctx:
        def sb(name, shape, dt=F32):
            return ctx.enter_context(nc.sbuf_tensor(name, shape, dt))

        def sem(name):
            return ctx.enter_context(nc.semaphore(name))

        identf = sb("identf", [128, 128])
        identb = sb("identb", [128, 128], BF16)
        ones = sb("ones", [128, 128])
        neg_half = sb("neg_half", [128, 1])
        glob01 = sb("glob01", [128, 1])
        decay_bias = sb("decay_bias", [128, 1])
        exponent = sb("exponent", [128, T])
        a01 = sb("a01", [128, 8])
        w2_nat = sb("w2_nat", [128, 128])
        w3_cat = sb("w3_cat", [128, 128])
        w3_nat = sb("w3_nat", [128, 128])
        b2_row = sb("b2_row", [1, 128])
        b2_col = sb("b2_col", [128, 1])
        b2_rep = sb("b2_rep", [128, 128])
        att = {2: sb("att2", [128, 8]), 3: sb("att3", [128, 16])}
        wall = {2: sb("wall2", [128, 136]), 3: sb("wall3", [128, 144])}
        bias2 = sb("bias2", [128, 136])
        sel = sb("sel", [128, 9, 128], BF16)
        kmax = sb("kmax", [128, B * CHUNKS])
        ksq = sb("ksq", [128, B * CHUNKS])
        stat = sb("stat", [128, 2])
        srep = sb("srep", [128, 2, 128])
        glob = sb("glob", [128, 2])
        flagf = sb("flagf", [128, 1])
        flag = sb("flag", [128, 1], I32)
        tau = sb("tau", [128, 1])
        adj_in = sb("adj_in", [128, 2, CT, N], I32)
        code = sb("code", [128, T, N], BF16)
        codeT = sb("codeT", [128, T, N], BF16)
        other = sb("other", [128, T, N], BF16)
        mask = sb("mask", [128, T, N], BF16)
        x_in = sb("x_in", [128, T, D])
        X = [sb("X0", [128, T, D]), sb("X1", [128, T, D]), sb("y_out", [128, T, D])]
        xT = sb("xT", [128, N])
        aT = sb("aT", [128, N])
        G = sb("G", [128, 2, T, N], BF16)
        scratch = G[:, :, :, :].rearrange("p a t n -> p (a t n)").bitcast(F32)
        E = [scratch[:, 0:N], scratch[:, N:2 * N]]
        P = [scratch[:, 2 * N:3 * N], scratch[:, 3 * N:4 * N]]
        PT = [scratch[:, 4 * N:5 * N], scratch[:, 5 * N:6 * N]]
        EK = scratch[:, 6 * N:7 * N]
        NK = scratch[:, 7 * N:7 * N + HALF].bitcast(BF16)
        aK = scratch[:, 7 * N + HALF:7 * N + HALF + 128]
        twT = scratch.rearrange("p (t n) -> p t n", t=T)
        squares = scratch[:, 0:CT * N]
        rmax = sb("rmax", [128, T])
        nmax = sb("nmax", [128, T])
        den = sb("den", [128, T])
        rden = sb("rden", [128, T])
        Z = sb("Z", [128, T, D])
        stats = sb("stats", [128, T, 6])
        mv = sb("mv", [128, T, 2])
        vare = sb("vare", [128, T])
        rstd = sb("rstd", [128, T])
        XP = sb("XP", [128, T, 144])
        q_parts = sb("q_parts", [128, N], BF16)
        q_mid = sb("q_mid", [8, N], BF16)
        q_res = sb("q_res", [8, N])
        QB = [sb("QB0", [128, N]), sb("QB1", [128, N])]
        kml = sb("kml", [128, 8])
        krep = aT[:, :].rearrange("p (h n) -> p h n", h=8)
        Mb = sb("Mb", [128, 8])
        nkey = sb("nkey", [128, T, 8])
        kbig = sb("kbig", [128, T, 8])
        R = sb("R", [128, T, 8])
        UVf = sb("UVf", [128, T * 272])
        RSf = sb("RSf", [128, T * 272])
        PCf = sb("PCf", [128, T * 3 * 272], BF16)
        parts_f = PCf[:, 0:6 * N].bitcast(F32)
        ZT, PX, PM = (parts_f[:, k * N:(k + 1) * N] for k in range(3))
        VG = UVf[:, 0:T * L3.W].rearrange("p (t c) -> p t c", t=T)
        adj_row = QB[1][:, :].bitcast(I32)
        q_most = sb("q_most", [128, 1])
        neg_most = sb("neg_most", [128, 1])
        MVf = sb("MVf", [128, T * 136])
        TTf = RSf
        O = UVf[:, 0:N].rearrange("p (t c) -> p t c", t=T)
        OE = UVf[:, N:2 * N].rearrange("p (t c) -> p t c", t=T)
        rd = sb("rd", [128, T * 8])

        bank = [ctx.enter_context(nc.psum_tensor(f"bank{i}", [128, 2, HALF], F32)) for i in range(4)]
        SP = [bank[0][:, :, :].rearrange("p a n -> p (a n)"), bank[1][:, :, :].rearrange("p a n -> p (a n)")]
        PTP = bank[2][:, :, :].rearrange("p a n -> p (a n)")
        ps_one = [bank[3][:, 0, :], bank[3][:, 1, :]]
        ps_proj = ps_one
        ct_ps = [p.bitcast(BF16) for p in ps_one]
        OP = [bank[2][:, 0, :], bank[2][:, 1, :], bank[3][:, 0, :], bank[3][:, 1, :]]

        def views(L):
            W, H = L.W, L.H
            uv = UVf[:, 0:T * H * 2 * W].rearrange("p (t h k c) -> p t h k c", t=T, h=H, k=2)
            rs = RSf[:, 0:T * H * 2 * W].rearrange("p (t h k) -> p t h k", t=T, h=H)
            pc = PCf[:, 0:T * H * NP * 2 * W].rearrange("p (t h n k) -> p t h n k", t=T, h=H, n=NP)
            mvv = MVf[:, 0:T * H * W].rearrange("p (t h c) -> p t h c", t=T, h=H)
            tt = TTf[:, 0:T * H * 2 * W].rearrange("p (t h k) -> p t h k", t=T, h=H)
            return uv, rs, pc, mvv, tt

        weights_in = sem("weights_in")
        const_done = sem("const_done")
        ident_done = sem("ident_done")
        sel_done = sem("sel_done")
        att_zero = sem("att_zero")
        att_in = sem("att_in")
        setup_pe = sem("setup_pe")
        setup_dve = sem("setup_dve")
        setup_act = sem("setup_act")
        adj_loaded = [sem("adj_loaded0"), sem("adj_loaded1")]
        scan_max = sem("scan_max")
        scan_sq = sem("scan_sq")
        x_loaded = sem("x_loaded")
        x0_room = sem("x0_room")
        x0_ready = sem("x0_ready")
        code_done = sem("code_done")
        neg_done = sem("neg_done")
        ct_ready = sem("ct_ready")
        ct_evac = sem("ct_evac")
        out_ready = sem("out_ready")
        out_stored = sem("out_stored")
        out_room = sem("out_room")
        wait_taken = sem("wait_taken")
        dve_steps = sem("dve_steps")
        act_steps = sem("act_steps")
        DVE_PER, ACT_PER = 256, 64

        s01 = [AttentionSems(sem, l) for l in range(2)]
        s23 = {l: HeadsSems(sem, l) for l in (2, 3)}
        kinds = [KindSems(sem, l) for l in range(2)]
        gen = GeneralSems(sem, 3)

        block = ctx.enter_context(nc.Block())
        x_v = x.rearrange("b (t p) d -> b p t d", p=128)
        out_v = out.rearrange("b (t p) d -> b p t d", p=128)
        adj_v = adj.rearrange("b (t p) n -> b p t n", p=128)

        n_weight_dmas = 13
        n_att_dmas = 24

        @block.sync
        def _(sp):
            for k in range(4):
                sp.dma_start(a01[:, k:k + 1], a0[k, :].rearrange("(d a) -> d a", a=1)).then_inc(weights_in, 16)
            for k, v in enumerate((a10, a11, a12, a13)):
                sp.dma_start(a01[:, 4 + k:5 + k], v).then_inc(weights_in, 16)
            sp.dma_start(w2_nat[:, :], w2).then_inc(weights_in, 16)
            sp.dma_start(w3_cat[:, :].rearrange("i (h o) -> i h o", h=8),
                         w3.rearrange("h i o -> i h o")).then_inc(weights_in, 16)
            sp.dma_start(wall[3][:, 0:128].rearrange("i (h o) -> i h o", h=8),
                         w3.rearrange("h i o -> i h o")).then_inc(weights_in, 16)
            sp.dma_start(b2_row[:, :], b2.rearrange("(a n) -> a n", a=1)).then_inc(weights_in, 16)
            sp.dma_start(b2_col[:, :], b2.rearrange("(n a) -> n a", a=1)).then_inc(weights_in, 16)
            sp.wait_ge(att_zero, 2)
            for h in range(4):
                sp.dma_start(att[2][32 * h:32 * h + 32, h:h + 1],
                             src2[0, h, :].rearrange("(c a) -> c a", a=1)).then_inc(att_in, 16)
                sp.dma_start(att[2][32 * h:32 * h + 32, 4 + h:5 + h],
                             dst2[0, h, :].rearrange("(c a) -> c a", a=1)).then_inc(att_in, 16)
            for h in range(8):
                sp.dma_start(att[3][16 * h:16 * h + 16, h:h + 1], a3[h, 16:32, :]).then_inc(att_in, 16)
                sp.dma_start(att[3][16 * h:16 * h + 16, 8 + h:9 + h], a3[h, 0:16, :]).then_inc(att_in, 16)
            def load_chunk(b, c):
                sp.sem_inc(wait_taken, 1)
                sp.dma_start(adj_in[:, c % 2, :, :], adj_v[b, :, CT * c:CT * c + CT, :]).then_inc(adj_loaded[c % 2], 16)

            with sp.Fori(0, B) as b:
                for c in range(CHUNKS):
                    sp.wait_ge(scan_max, CHUNKS * b + c - 1 + SCANNED)
                    sp.wait_ge(scan_sq, CHUNKS * b + c - 1 + SCANNED)
                    load_chunk(b, c)
            sp.wait_ge(scan_max, CHUNKS * B + SCANNED)
            sp.wait_ge(scan_sq, CHUNKS * B + SCANNED)
            sp.wait_ge(setup_dve, 17)
            general = sp.value_load(flag[0:1, 0:1], min_val=0, max_val=1)
            with sp.Fori(0, B) as b:
                sp.wait_ge(x0_ready, b + CREDIT)
                sp.dma_start(x_in[:, :, :], x_v[b]).then_inc(x_loaded, 16)
                for c in range(CHUNKS):
                    sp.wait_ge(code_done, T * b + CT * (c - 1) + CODED)
                    load_chunk(b, c)
                with sp.If(general != 0):
                    for i in range(T):
                        if i == 0:
                            sp.wait_ge(gen.q_evac, L3.H * b + CREDIT)
                            sp.sem_inc(wait_taken, 1)
                            sp.wait_ge(s23[2].x_done, T * (b + 1))
                        else:
                            sp.wait_ge(gen.row_less, T * b + i)
                        sp.dma_start(adj_row, adj_v[b, :, i, :]).then_inc(gen.row_loaded, 16)
                with sp.Else():
                    sp.nop()
                sp.nop()

        @block.gpsimd
        def _(pool):
            pool.sem_inc(scan_max, SCANNED)
            pool.sem_inc(scan_sq, SCANNED)
            pool.sem_inc(code_done, CODED)
            for s in (x0_ready, s23[3].t_ready, s23[3].x_done,
                      gen.q_evac, out_room, s23[2].o_ready, s23[3].o_ready):
                pool.sem_inc(s, CREDIT)
            pool.memset(att[2][:, :], 0.0).then_inc(att_zero, 1)
            pool.memset(att[3][:, :], 0.0).then_inc(att_zero, 1)
            pool.memset(identf[:, :], 0.0).then_inc(const_done, 1)
            pool.memset(identb[:, :], 0.0).then_inc(const_done, 1)
            pool.memset(ones[:, :], 1.0).then_inc(const_done, 1)
            pool.memset(neg_half[:, :], -0.5).then_inc(const_done, 1)
            pool.memset(exponent[:, :], -0.5).then_inc(const_done, 1)
            pool.memset(sel[:, :, :], 0.0).then_inc(const_done, 1)
            pool.memset(q_parts[:, :], 0.0).then_inc(const_done, 1)
            pool.wait_ge(const_done, 7)
            for n in range(NP):
                pool.affine_select(out=sel[:, :, :], in_=sel[:, :, :], compare_op=ALU.not_equal, fill=1.0,
                                   base=-32 * n, pattern=[[-1, 9], [0, 128]], channel_multiplier=1)\
                    .then_inc(sel_done, 1)
                pool.wait_ge(sel_done, n + 1)
            for m in (identf, identb):
                pool.affine_select(out=m[:, :], in_=m[:, :], compare_op=ALU.not_equal, fill=1.0, base=0,
                                   pattern=[[-1, 128]], channel_multiplier=1).then_inc(ident_done, 1)

            def inverse_root(s, want, c0, c1):
                pool.wait_ge(s.var_ready, want)
                pool.tensor_tensor(rstd[:, c0:c1], vare[:, c0:c1], exponent[:, c0:c1], ALU.pow)\
                    .then_inc(s.rstd_ready, 1)

            with pool.Fori(0, B) as b:
                pool.wait_ge(x_loaded, 16 * (b + 1))
                pool.wait_ge(s23[3].t_ready, b + CREDIT)
                pool.sem_inc(x0_room, 1)
                pool.tensor_copy(X[0][:, :, :], x_in[:, :, :]).then_inc(x0_ready, 1)
                for l in range(2):
                    for i in range(T):
                        inverse_root(s01[l], T * b + i + 1, i, i + 1)
                for l in (2, 3):
                    inverse_root(s23[l], b + 1, 0, T)
                pool.wait_ge(s23[3].x_done, T * (b + 1) + CREDIT)
                pool.dma_start(out_v[b], X[2][:, :, :]).then_inc(out_stored, 16)
                pool.wait_ge(out_stored, 16 * (b + 1))
                pool.sem_inc(out_room, 1)

        @block.scalar
        def _(act):
            act.wait_ge(const_done, 7)
            with act.Fori(0, B) as b:
                for c in range(CHUNKS):
                    act.wait_ge(adj_loaded[c % 2], 16 * (CHUNKS // 2 * b + c // 2 + 1))
                    act.wait_ge(scan_sq, CHUNKS * b + c + SCANNED)
                    act.activation(squares, adj_in[:, c % 2, :, :].rearrange("p t n -> p (t n)"),
                                   ACT.Square, bias=neg_half[:, 0:1],
                                   accum_out=ksq[:, bass.ds(CHUNKS * b + c, 1)]).then_inc(scan_sq, 1)
            act.wait_ge(setup_dve, 7)
            act.activation(tau[:, :], glob01[:, 0:1], ACT.Exp, bias=decay_bias[:, 0:1], scale=-DECAY)\
               .then_inc(setup_act, 1)

            act.wait_ge(setup_dve, 17)
            general = act.value_load(flag[0:1, 0:1], min_val=0, max_val=1)

            def codes(b, tiles):
                for j in tiles:
                    act.wait_ge(ct_ready, T * b + j + 1)
                    act.activation(codeT[:, j, :], ct_ps[j % 2], ACT.Copy).then_inc(ct_evac, 1)

            def attention(l, b):
                s = s01[l]
                if l == 1:
                    codes(b, range(4))
                act.wait_ge(s.t_ready, b + 1)
                act.activation(xT[:, :], SP[0], ACT.Copy).then_inc(s.xt_done, 1)
                if l == 1:
                    codes(b, range(4, T))

                def leaky(i):
                    act.wait_ge(s.s_ready, T * b + i + 1)
                    act.activation(E[i % 2], SP[i % 2], ACT.Relu, scale=SLOPE - 1.0).then_inc(s.lift_done, 1)
                    with act.If(general != 0):
                        for k in range(3):
                            act.wait_ge(kinds[l].kind_ready, 3 * (T * b + i) + k + 1)
                            if k >= 1:
                                act.wait_ge(kinds[l].kind_max, 3 * (T * b + i) + k)
                            act.activation(EK, SP[i % 2], ACT.Relu, scale=SLOPE - 1.0).then_inc(kinds[l].kind_lift, 1)
                    with act.Else():
                        act.nop()
                    act.nop()

                def expo(i):
                    act.wait_ge(s.nm_ready, T * b + i + 1)
                    if i >= 2:
                        act.wait_ge(s.pt_ready, T * b + i - 1)
                    act.activation(P[i % 2], E[i % 2], ACT.Exp, bias=nmax[:, i:i + 1],
                                   accum_out=den[:, i:i + 1]).then_inc(s.p_ready, 1)

                leaky(0)
                leaky(1)
                expo(0)
                for i in range(T):
                    if i + 1 < T:
                        expo(i + 1)
                    act.wait_ge(s.pt_ready, T * b + i + 1)
                    if i >= 2:
                        act.wait_ge(s.pv_ready, T * b + i - 1)
                    act.activation(PT[i % 2][:, 0:HALF], PTP[:, 0:HALF], ACT.Copy).then_inc(s.pt_act, 1)
                    if i + 2 < T:
                        act.wait_ge(s.p_ready, T * b + i + 1)
                        leaky(i + 2)

            def heads_layer(L, b):
                s, H, C, W, l = s23[L.layer], L.H, L.C, L.W, L.layer
                uv, rs, pc, mvv, tt = views(L)
                act.wait_ge(s.t_ready, b + 1 + (CREDIT if l == 3 else 0))
                act.activation(xT[:, :], SP[0], ACT.Copy).then_inc(s.xt_done, 1)
                act.wait_ge(s.qr_ready, b + 1)
                act.activation(q_parts[0:H, :], SP[0][0:H, :], ACT.Copy).then_inc(s.q_hi, 1)
                act.wait_ge(s.q_res, b + 1)
                act.activation(q_mid[0:H, :], q_res[0:H, :], ACT.Copy).then_inc(s.q_mid, 1)
                act.activation(q_parts[32:32 + H, :], q_res[0:H, :], ACT.Copy).then_inc(s.q_mid, 1)
                act.wait_ge(s.shift_done, b + 1)
                act.activation(uv[:, :, :, 0, C], nkey[:, :, 0:H], ACT.Exp).then_inc(s.ac_done, 1)
                act.activation(uv[:, :, :, 1, C], nkey[:, :, 0:H], ACT.Exp, scale=SLOPE).then_inc(s.ac_done, 1)
                act.activation(R[:, :, 0:H], R[:, :, 0:H], ACT.Exp, scale=SLOPE - 1.0).then_inc(s.ac_done, 1)

                def steps(h, par, tiles):
                    for j in tiles:
                        act.activation(G[:, par, j, :], SP[par], ACT.Relu, scale=STEEP,
                                       bias=kbig[:, j, bass.ds(h, 1)]).then_inc(s.relu_done, 1)

                def body(h, par):
                    act.wait_ge(s.qb_ready, (H + 1) * b + h + 1)
                    if is_first(h):
                        steps(h, par, range(2))
                        act.wait_ge(s.uv_done, b + 1)
                        act.activation(pc[:, :, :, 0, :].rearrange("p t h k -> p (t h) k"),
                                       uv.rearrange("p t h k c -> p (t h) (k c)"), ACT.Copy).then_inc(s.cast1, 1)
                        steps(h, par, range(2, 4))
                        act.wait_ge(s.res1, b + 1)
                        act.activation(pc[:, :, :, 1, :].rearrange("p t h k -> p (t h) k"),
                                       rs.rearrange("p t h k -> p (t h) k"), ACT.Copy).then_inc(s.cast2, 1)
                        steps(h, par, range(4, T))
                    else:
                        act.wait_ge(s.o_ready, 4 * (H * b + h - 1) + CREDIT)
                        steps(h, par, range(T))

                if l == 2:
                    each_head(act, H, body)
                else:
                    with act.If(general != 0):
                        general_weights(b)
                    with act.Else():
                        each_head(act, H, body)
                    act.nop()
                    act.wait_ge(s.neg_out, b + 1)
                    act.activation(OE[:, :, :], OE[:, :, :], ACT.Exp).then_inc(s.exp_out, 1)

            def general_weights(b):
                s, L = s23[3], L3
                uv, rs, pc, mvv, tt = views(L)
                act.wait_ge(s.uv_done, b + 1)
                act.activation(pc[:, :, :, 0, :].rearrange("p t h k -> p (t h) k"),
                               uv.rearrange("p t h k c -> p (t h) (k c)"), ACT.Copy).then_inc(s.cast1, 1)
                act.wait_ge(s.res1, b + 1)
                act.activation(pc[:, :, :, 1, :].rearrange("p t h k -> p (t h) k"),
                               rs.rearrange("p t h k -> p (t h) k"), ACT.Copy).then_inc(s.cast2, 1)
                for i in range(T):
                    act.wait_ge(gen.row_less, T * b + i + 1)
                    if i >= 1:
                        act.wait_ge(gen.tw_ready, T * b + i)
                    act.activation(PX, ZT, ACT.Exp, scale=DECAY).then_inc(gen.tw_done, 1)
                with act.Fori(0, L3.H) as h:
                    n = L3.H * b + h
                    act.wait_ge(gen.q_ready, n + 1)
                    act.activation(QB[0][:, :], SP[0], ACT.Copy).then_inc(gen.q_evac, 1)
                    for j in range(T):
                        act.wait_ge(gen.z_done, T * n + j + 1)
                        act.activation(PX, ZT, ACT.Exp, bias=neg_most[:, 0:1]).then_inc(gen.p_exp, 1)

            with act.Fori(0, B) as b:
                attention(0, b)
                attention(1, b)
                heads_layer(L2, b)
                heads_layer(L3, b)

        @block.vector
        def _(dve):
            with dve.Fori(0, B) as b:
                for c in range(CHUNKS):
                    dve.wait_ge(adj_loaded[c % 2], 16 * (CHUNKS // 2 * b + c // 2 + 1))
                    dve.tensor_reduce(kmax[:, bass.ds(CHUNKS * b + c, 1)],
                                      adj_in[:, c % 2, :, :].rearrange("p t n -> p (t n)"),
                                      AX.X, ALU.max).then_inc(scan_max, 1)
            dve.wait_ge(scan_max, CHUNKS * B + SCANNED)
            dve.wait_ge(scan_sq, CHUNKS * B + SCANNED)
            dve.tensor_reduce(stat[:, 0:1], kmax[:, :], AX.X, ALU.max).then_inc(setup_dve, 1)
            dve.tensor_reduce(stat[:, 1:2], ksq[:, :], AX.X, ALU.max).then_inc(setup_dve, 1)
            dve.wait_ge(setup_dve, 2)
            dve.tensor_copy(srep[:, :, :], stat[:, :].unsqueeze(2).to_broadcast([128, 2, 128]))\
               .then_inc(setup_dve, 1)
            dve.wait_ge(setup_pe, 1)
            dve.tensor_reduce(glob[:, :], ps_one[0][:, 0:256].rearrange("p (k n) -> p k n", k=2), AX.X, ALU.max)\
               .then_inc(setup_dve, 1)
            dve.wait_ge(setup_dve, 4)
            dve.tensor_scalar(flagf[:, :], glob[:, 1:2], CT * N * 0.25, None, ALU.is_gt).then_inc(setup_dve, 1)
            dve.memset(decay_bias[:, :], DECAY).then_inc(setup_dve, 1)
            dve.tensor_scalar(glob01[:, :], glob[:, 0:1], 0.0, 1.0, ALU.max, ALU.min).then_inc(setup_dve, 1)
            dve.wait_ge(setup_dve, 7)
            dve.tensor_copy(flag[:, :], flagf[:, :]).then_inc(setup_dve, 1)
            dve.wait_ge(setup_act, 1)
            dve.tensor_scalar(tau[:, :], tau[:, :], -1.0, None, ALU.add).then_inc(setup_dve, 1)
            dve.tensor_scalar(flagf[:, :], flagf[:, :], -1.0, 1.0, ALU.mult, ALU.add).then_inc(setup_dve, 1)
            dve.wait_ge(setup_dve, 10)
            dve.tensor_tensor(tau[:, :], tau[:, :], flagf[:, :], ALU.mult).then_inc(setup_dve, 1)
            dve.wait_ge(setup_dve, 11)
            dve.tensor_scalar(tau[:, :], tau[:, :], 1.0, None, ALU.add).then_inc(setup_dve, 1)
            dve.wait_ge(setup_pe, 2)
            dve.tensor_copy(wall[2][:, 0:128], ps_one[1][:, 128:256])
            dve.tensor_copy(w3_nat[:, :], ps_one[1][:, 0:128]).then_inc(setup_dve, 1)
            dve.wait_ge(weights_in, 16 * n_weight_dmas)
            dve.tensor_copy(b2_rep[:, :], b2_col[:, 0:1].to_broadcast([128, 128])).then_inc(setup_dve, 1)
            dve.wait_ge(setup_dve, 14)
            dve.wait_ge(setup_pe, 3)
            dve.tensor_copy(wall[2][:, 128:136], SP[0][:, 0:8]).then_inc(setup_dve, 1)
            dve.tensor_scalar(wall[3][:, 128:144], SP[0][:, 8:24], tau[:, 0:1], None, ALU.mult).then_inc(setup_dve, 1)
            dve.tensor_copy(bias2[:, 0:136], SP[0][:, 32:168]).then_inc(setup_dve, 1)
            dve.wait_ge(setup_dve, 17)
            general = dve.value_load(flag[0:1, 0:1], min_val=0, max_val=1)

            def further_kinds(l, b, i):
                s, n = kinds[l], 3 * (T * b + i)
                for k in range(3):
                    dve.tensor_scalar(NK, code[:, i, :], float(k + 2), -BIG, ALU.not_equal, ALU.mult)\
                       .then_inc(s.kind_mask, 1)
                    dve.tensor_scalar(aK, xT[:, 128 * i:128 * i + 128], a01[:, 4 * l + k + 1:4 * l + k + 2], None,
                                      ALU.mult).then_inc(s.kind_mask, 1)
                    dve.wait_ge(s.kind_lift, n + k + 1)
                    dve.tensor_tensor(EK, SP[i % 2], EK, ALU.add).then_inc(s.kind_sum, 1)
                    dve.wait_ge(s.kind_sum, n + k + 1)
                    dve.tensor_tensor(E[i % 2], E[i % 2], EK, ALU.max).then_inc(s.kind_max, 1)
                    dve.wait_ge(s.kind_max, n + k + 1)
                dve.tensor_reduce(rmax[:, i:i + 1], E[i % 2], AX.X, ALU.max).then_inc(s.kind_mask, 1)
                dve.wait_ge(s.kind_mask, 7 * (T * b + i + 1))
                dve.sem_inc(wait_taken, 1)

            def code_tile(b, i):
                c = i // CT
                dve.wait_ge(adj_loaded[c % 2], 16 * (CHUNKS // 2 * (B + b) + c // 2 + 1))
                dve.tensor_scalar(code[:, i, :], adj_in[:, c % 2, i % CT, :], -1.0, 5.0, ALU.max, ALU.min)\
                   .then_inc(code_done, 1)
                dve.wait_ge(code_done, T * b + i + 1 + CODED)
                dve.tensor_scalar(other[:, i, :], code[:, i, :], 1.0, -BIG, ALU.not_equal, ALU.mult)\
                   .then_inc(neg_done, 1)

            def mask_tile(b, j, st):
                dve.wait_ge(ct_evac, T * b + j + 1)
                st.done(dve.tensor_scalar(mask[:, j, :], codeT[:, j, :], 0.0, None, ALU.is_gt))
                st.wait()
                own = mask[:, j, 128 * j:128 * j + 128]
                dve.tensor_tensor(own, own, identb[:, :], ALU.max).then_inc(s23[2].mask_done, 1)

            def attention(l, b, st):
                s = s01[l]
                src, dst = X[l], X[1 - l]
                dve.wait_ge(s.xt_done, b + 1)
                dve.tensor_scalar(aT[:, :], xT[:, :], a01[:, 4 * l:4 * l + 1], None, ALU.mult).then_inc(s.at_done, 1)

                def row_max(i):
                    dve.wait_ge(s.lift_done, T * b + i + 1)
                    st.carry()
                    dve.tensor_tensor_reduce(out=E[i % 2], in0=SP[i % 2], in1=E[i % 2], scale=1.0, scalar=-3e38,
                                             op0=ALU.add, op1=ALU.max, accum_out=rmax[:, i:i + 1])\
                       .then_inc(s.e_done, 1)
                    dve.wait_ge(s.e_done, T * b + i + 1)
                    dve.sem_inc(wait_taken, 1)
                    with dve.If(general != 0):
                        further_kinds(l, b, i)
                    with dve.Else():
                        dve.nop()
                    dve.tensor_scalar(nmax[:, i:i + 1], rmax[:, i:i + 1], -1.0, None, ALU.mult)\
                       .then_inc(s.nm_ready, 1)

                def finish(i):
                    dve.wait_ge(s.pv_ready, T * b + i + 1)
                    dve.wait_ge(s.p_ready, T * b + i + 1)
                    st.done(dve.reciprocal(rden[:, i:i + 1], den[:, i:i + 1]))
                    st.wait()
                    st.done(dve.scalar_tensor_tensor(Z[:, i, :], ps_one[i % 2][:, 0:D], rden[:, i:i + 1],
                                                     src[:, i, :], ALU.mult, ALU.add))
                    st.wait()
                    st.done(dve.bn_stats(stats[:, i, :], Z[:, i, :]))
                    st.wait()
                    st.carry()
                    st.done(dve.bn_aggr(mv[:, i, :], stats[:, i, :]))
                    st.wait()
                    dve.tensor_scalar(vare[:, i:i + 1], mv[:, i, 1:2], EPS, None, ALU.add).then_inc(s.var_ready, 1)

                def normal(i):
                    dve.wait_ge(s.rstd_ready, T * b + i + 1)
                    dve.tensor_scalar(dst[:, i, :], Z[:, i, :], mv[:, i, 0:1], rstd[:, i:i + 1],
                                      ALU.subtract, ALU.mult).then_inc(s.x_done, 1)

                if l == 0:
                    code_tile(b, 0)
                    code_tile(b, 1)
                row_max(0)
                if l == 0:
                    code_tile(b, 2)
                row_max(1)
                for i in range(T):
                    dve.wait_ge(s.pt_ready, T * b + i + 1)
                    if i >= 2:
                        dve.wait_ge(s.pv_ready, T * b + i - 1)
                    dve.tensor_copy(PT[i % 2][:, HALF:N], PTP[:, HALF:N]).then_inc(s.pt_dve, 1)
                    if i + 2 < T:
                        row_max(i + 2)
                    if l == 0 and i + 3 < T:
                        code_tile(b, i + 3)
                    if i >= 1:
                        finish(i - 1)
                    if i >= 2:
                        normal(i - 2)
                    if l == 1:
                        mask_tile(b, i, st)
                finish(T - 1)
                normal(T - 2)
                normal(T - 1)

            def general_heads(b, sums):
                s = s23[3]
                dve.wait_ge(s.mv_evac, T * (b + 1))
                dve.wait_ge(s.mask_done, T * (b + 1))
                for i in range(T):
                    dve.wait_ge(gen.row_loaded, 16 * (T * b + i + 1))
                    if i >= 1:
                        dve.wait_ge(gen.tw_done, T * b + i)
                    dve.tensor_scalar(ZT, adj_row, glob[:, 0:1], None, ALU.subtract).then_inc(gen.row_less, 1)
                    dve.wait_ge(gen.tw_ready, T * b + i + 1)
                    dve.tensor_copy(twT[:, :, 128 * i:128 * i + 128], PTP.rearrange("p (t n) -> p t n", t=T))\
                       .then_inc(gen.tw_evac, 1)
                dve.wait_ge(gen.tw_evac, T * (b + 1))
                dve.sem_inc(wait_taken, 1)
                with dve.Fori(0, L3.H) as h:
                    n = L3.H * b + h
                    dve.memset(VG[:, :, L3.C:L3.W], 1.0).then_inc(gen.values, 1)
                    dve.tensor_copy(VG[:, :, 0:L3.C], XP[:, :, bass.ds(L3.C * h, L3.C)]).then_inc(gen.values, 1)
                    dve.wait_ge(gen.q_evac, n + 1 + CREDIT)
                    dve.tensor_reduce(q_most[:, :], QB[0][:, :], AX.X, ALU.max).then_inc(gen.q_max, 1)
                    dve.wait_ge(gen.q_max, n + 1)
                    dve.tensor_scalar(neg_most[:, :], q_most[:, :], Mb[:, bass.ds(h, 1)], 0.0, ALU.add, ALU.max)\
                       .then_inc(gen.shift, 1)
                    dve.wait_ge(gen.shift, 2 * n + 1)
                    dve.tensor_scalar(neg_most[:, :], neg_most[:, :], -1.0, None, ALU.mult).then_inc(gen.shift, 1)
                    dve.wait_ge(gen.shift, 2 * n + 2)
                    for j in range(T):
                        m = T * n + j
                        dve.tensor_scalar(PM, QB[0][:, :], XP[:, j, bass.ds(D + h, 1)], None, ALU.add)\
                           .then_inc(gen.z_sum, 1)
                        dve.wait_ge(gen.z_sum, m + 1)
                        dve.scalar_tensor_tensor(ZT, PM, SLOPE, PM, ALU.mult, ALU.max).then_inc(gen.z_leaky, 1)
                        dve.wait_ge(gen.z_leaky, m + 1)
                        dve.tensor_tensor(ZT, ZT, twT[:, j, :], ALU.mult).then_inc(gen.z_done, 1)
                        dve.wait_ge(gen.p_exp, m + 1)
                        dve.tensor_tensor(PM, PX, mask[:, j, :], ALU.mult).then_inc(gen.p_done, 1)
                        dve.wait_ge(gen.mm_done, m + 1)
                        part = PTP[:, 0:T * 32].rearrange("p (t c) -> p t c", t=T)[:, :, 0:L3.W]
                        whole = sums[:, :, bass.ds(h, 1), :].rearrange("p t h c -> p t (h c)")
                        if j == 0:
                            dve.tensor_copy(whole, part).then_inc(gen.acc_done, 1)
                        else:
                            dve.tensor_tensor(whole, whole, part, ALU.add).then_inc(gen.acc_done, 1)
                        dve.wait_ge(gen.acc_done, m + 1)
                    dve.sem_inc(wait_taken, 1)

            def heads_layer(L, b, st):
                s, H, C, W, l = s23[L.layer], L.H, L.C, L.W, L.layer
                uv, rs, pc, mvv, tt = views(L)
                src, dst = X[l - 2], X[l - 1]
                if l == 3:
                    with dve.If(general != 0):
                        for j in range(T):
                            dve.tensor_scalar(mask[:, j, :], codeT[:, j, :], 0.0, None, ALU.not_equal)\
                               .then_inc(s.mask_done, 1)
                    with dve.Else():
                        for j in range(T):
                            own = slice(128 * j, 128 * j + 128)
                            dve.tensor_scalar(mask[:, j, own], codeT[:, j, own], 0.0, None, ALU.not_equal)\
                               .then_inc(s.mask_done, 1)
                def projected(j):
                    dve.wait_ge(s.pj_ready, T * b + j + 1)
                    ps = ps_proj[j % 2][:, 0:L.cols]
                    if l == 2:
                        dve.tensor_tensor(XP[:, j, 0:L.cols], ps, bias2[:, :], ALU.add).then_inc(s.xp_done, 1)
                    else:
                        dve.tensor_copy(XP[:, j, 0:L.cols], ps).then_inc(s.xp_done, 1)

                projected(0)
                projected(1)
                dve.wait_ge(s.qr_ready, b + 1)
                dve.wait_ge(s.q_hi, b + 1)
                dve.tensor_tensor(q_res[0:H, :], SP[0][0:H, :], q_parts[0:H, :], ALU.subtract).then_inc(s.q_res, 1)
                for j in range(2, T):
                    projected(j)
                dve.wait_ge(s.xp_done, T * b + T)
                key = XP[:, :, D:D + H]
                qry = XP[:, :, D + H:D + 2 * H]
                st.done(dve.tensor_reduce(kml[:, 0:H], key.rearrange("p t h -> p h t"), AX.X, ALU.max))
                st.wait()
                dve.tensor_copy(krep[:, 0:H, :], kml[:, 0:H].unsqueeze(2).to_broadcast([128, H, 128]))\
                   .then_inc(s.krep_done, 1)
                dve.wait_ge(s.q_res, b + 1)
                dve.wait_ge(s.q_mid, 2 * b + 2)
                dve.tensor_tensor(q_parts[64:64 + H, :], q_res[0:H, :], q_mid[0:H, :], ALU.subtract)\
                   .then_inc(s.q_split, 1)
                if l == 2:
                    st.done(dve.tensor_tensor(kbig[:, :, 0:H], key, bias2[:, D + H:D + 2 * H].unsqueeze(1)
                                              .to_broadcast([128, T, H]), ALU.add))
                    st.wait()
                    dve.tensor_scalar(kbig[:, :, 0:H], kbig[:, :, 0:H], STEEP, None, ALU.mult)
                else:
                    dve.tensor_scalar(kbig[:, :, 0:H], key, STEEP, None, ALU.mult)
                dve.wait_ge(s.mb_ready, b + 1)
                st.done(dve.tensor_reduce(Mb[:, 0:H], SP[1][:, 0:H * 128].rearrange("p (h n) -> p h n", h=H),
                                          AX.X, ALU.max))
                st.wait()
                mb_all = Mb[:, 0:H].unsqueeze(1).to_broadcast([128, T, H])
                st.done(dve.tensor_tensor(nkey[:, :, 0:H], key, mb_all, ALU.subtract))
                st.done(dve.tensor_tensor(R[:, :, 0:H], qry, mb_all, ALU.add))
                st.wait()
                dve.tensor_scalar(R[:, :, 0:H], R[:, :, 0:H], 0.0, None, ALU.max).then_inc(s.shift_done, 1)

                def products():
                    dve.wait_ge(s.ac_done, 3 * b + 2)
                    xph = XP[:, :, 0:D].rearrange("p t (h c) -> p t h c", h=H)
                    for k in range(2):
                        u = dve.tensor_tensor(uv[:, :, :, k, 0:C], xph,
                                              uv[:, :, :, k, C:W].to_broadcast([128, T, H, C]), ALU.mult)
                    u.then_inc(s.uv_done, 1)

                uvk = uv.rearrange("p t h k c -> p (t h) (k c)")
                rsk = rs.rearrange("p t h k -> p (t h) k")
                part = [pc[:, :, :, n, :].rearrange("p t h k -> p (t h) k") for n in range(NP)]

                def residue():
                    dve.wait_ge(s.uv_done, b + 1)
                    dve.wait_ge(s.cast1, b + 1)
                    dve.tensor_tensor(rsk, uvk, part[0], ALU.subtract).then_inc(s.res1, 1)

                def last_part():
                    dve.wait_ge(s.res1, b + 1)
                    dve.wait_ge(s.cast2, b + 1)
                    dve.tensor_tensor(part[2], rsk, part[1], ALU.subtract).then_inc(s.parts_done, 1)

                def mask_sums(i):
                    dve.wait_ge(s.mv_ready, T * b + i + 1)
                    dve.tensor_reduce(mvv[:, i, :, :], ps_proj[i % 2][:, 0:H * NP * W]
                                      .rearrange("p (h n c) -> p h c n", h=H, n=NP), AX.X, ALU.add)\
                       .then_inc(s.mv_evac, 1)

                def take(h, q):
                    dve.wait_ge(s.o_ready, 4 * (H * b + h) + q + 1 + CREDIT)
                    dve.tensor_reduce(tt[:, 2 * q:2 * q + 2, bass.ds(h, 1), :].rearrange("p i h k -> p i (h k)"),
                                      OP[q].rearrange("p (i c) -> p i c", i=2)[:, :, 0:NP * 2 * W]
                                      .rearrange("p i (n k) -> p i k n", n=NP), AX.X, ALU.add)\
                       .then_inc(s.o_evac, 1)

                def combine(h):
                    n = H * b + h
                    own = mvv[:, :, bass.ds(h, 1), :].rearrange("p t h c -> p t (h c)")
                    tth = tt[:, :, bass.ds(h, 1), :].rearrange("p t h k -> p t (h k)")
                    dve.wait_ge(s.o_evac, 4 * n + 4)
                    dve.tensor_tensor(own, own, tth[:, :, W:2 * W], ALU.subtract).then_inc(s.combined, 1)
                    dve.wait_ge(s.combined, 3 * n + 1)
                    dve.tensor_tensor(own, own, R[:, :, bass.ds(h, 1)].to_broadcast([128, T, W]), ALU.mult)\
                       .then_inc(s.combined, 1)
                    dve.wait_ge(s.combined, 3 * n + 2)
                    dve.tensor_tensor(own, own, tth[:, :, 0:W], ALU.add).then_inc(s.combined, 1)

                def cut(h, par, j):
                    dve.wait_ge(s.relu_done, T * (H * b + h) + j + 1)
                    dve.tensor_tensor(G[:, par, j, :], G[:, par, j, :], mask[:, j, :], ALU.min)\
                       .then_inc(s.g_ready, 1)

                def body(h, par):
                    if is_first(h):
                        products()
                        cut(h, par, 0)
                        cut(h, par, 1)
                        residue()
                        cut(h, par, 2)
                        cut(h, par, 3)
                        last_part()
                        for j in range(4, T):
                            cut(h, par, j)
                            mask_sums(j - 4)
                        for i in range(4, T):
                            mask_sums(i)
                        dve.wait_ge(s.mv_evac, T * (b + 1))
                        dve.wait_ge(s.ac_done, 3 * b + 3)
                        dve.sem_inc(wait_taken, 1)
                    else:
                        for j in range(T):
                            cut(h, par, j)
                            if j % 2:
                                take(h - 1, j // 2)
                        combine(h - 1)
                        if not is_last(h, H):
                            dve.sem_inc(wait_taken, 1)

                def fast():
                    each_head(dve, H, body)
                    for q in range(4):
                        take(H - 1, q)
                    combine(H - 1)
                    dve.wait_ge(s.combined, 3 * H * (b + 1))
                    dve.sem_inc(wait_taken, 1)

                def general_layer():
                    products()
                    residue()
                    last_part()
                    for i in range(T):
                        mask_sums(i)
                    general_heads(b, mvv)

                if l == 2:
                    fast()
                else:
                    with dve.If(general != 0):
                        general_layer()
                    with dve.Else():
                        fast()
                rdh = rd[:, 0:T * H].rearrange("p (t h) -> p t h", t=T)
                st.done(dve.reciprocal(rdh, mvv[:, :, :, C]))
                st.wait()
                st.done(dve.tensor_tensor(O[:, :, :].rearrange("p t (h c) -> p t h c", h=H), mvv[:, :, :, 0:C],
                                          rdh.unsqueeze(3).to_broadcast([128, T, H, C]), ALU.mult))
                st.wait()
                if l == 3:
                    dve.tensor_scalar(OE[:, :, :], O[:, :, :], 0.0, None, ALU.min).then_inc(s.neg_out, 1)
                    st.done(dve.tensor_scalar(O[:, :, :], O[:, :, :], 0.0, -1.0, ALU.max, ALU.add))
                    st.wait()
                    dve.wait_ge(s.exp_out, b + 1)
                    st.done(dve.tensor_tensor(O[:, :, :], O[:, :, :], OE[:, :, :], ALU.add))
                    st.wait()
                st.done(dve.tensor_tensor(Z[:, :, :], O[:, :, :], src[:, :, :], ALU.add))
                st.wait()
                for i in range(T):
                    m = dve.bn_stats(stats[:, i, :], Z[:, i, :])
                st.done(m)
                st.wait()
                st.carry()
                for i in range(T):
                    m = dve.bn_aggr(mv[:, i, :], stats[:, i, :])
                st.done(m)
                st.wait()
                dve.tensor_scalar(vare[:, :], mv[:, :, 1], EPS, None, ALU.add).then_inc(s.var_ready, 1)
                dve.wait_ge(s.rstd_ready, b + 1)
                if l == 3:
                    dve.wait_ge(out_room, b + CREDIT)
                for i in range(T):
                    dve.tensor_scalar(dst[:, i, :], Z[:, i, :], mv[:, i, 0:1], rstd[:, i:i + 1],
                                      ALU.subtract, ALU.mult).then_inc(s.x_done, 1)

            with dve.Fori(0, B) as b:
                st = Steps(dve, dve_steps, DVE_PER * b)
                attention(0, b, st)
                attention(1, b, st)
                heads_layer(L2, b, st)
                heads_layer(L3, b, st)
                dve.sem_inc(dve_steps, DVE_PER - st.n)

        @block.tensor
        def _(pe):
            pe.wait_ge(ident_done, 2)
            pe.wait_ge(setup_dve, 3)
            for k in range(2):
                mm = pe.matmul(ps_one[0][:, 128 * k:128 * k + 128], srep[:, k, :], identf[:, :], start=True, stop=True)
            mm.then_inc(setup_pe, 1)
            pe.wait_ge(weights_in, 16 * n_weight_dmas)
            pe.wait_ge(att_in, 16 * n_att_dmas)
            pe.transpose(ps_one[1][:, 0:128], w3_cat[:, :], identf[:, :])
            pe.transpose(ps_one[1][:, 128:256], w2_nat[:, :], identf[:, :]).then_inc(setup_pe, 1)
            pe.wait_ge(setup_dve, 14)
            pe.matmul(SP[0][:, 0:8], w2_nat[:, :], att[2][:, :], start=True, stop=True)
            pe.matmul(SP[0][:, 8:24], w3_nat[:, :], att[3][:, :], start=True, stop=True)
            pe.matmul(SP[0][:, 32:160], ones[0:1, :], b2_row[:, :], start=True, stop=True)
            pe.matmul(SP[0][:, 160:168], b2_rep[:, :], att[2][:, :], start=True, stop=True).then_inc(setup_pe, 1)
            pe.wait_ge(setup_dve, 17)
            pe.wait_ge(sel_done, NP)

            general = pe.value_load(flag[0:1, 0:1], min_val=0, max_val=1)

            def further_kinds(l, b, i):
                s, n = kinds[l], 3 * (T * b + i)
                pe.wait_ge(s01[l].e_done, T * b + i + 1)
                for k in range(3):
                    pe.wait_ge(s.kind_mask, 7 * (T * b + i) + 2 * k + 2)
                    if k >= 1:
                        pe.wait_ge(s.kind_sum, n + k)
                    for c in range(2):
                        o = SP[i % 2][:, c * HALF:(c + 1) * HALF]
                        pe.matmul(o, aK, xT[:, c * HALF:(c + 1) * HALF], start=True, stop=False)
                        mm = pe.matmul(o, identb[:, :], NK[:, c * HALF:(c + 1) * HALF], start=False, stop=True)
                    mm.then_inc(s.kind_ready, 1)
                pe.wait_ge(s.kind_sum, n + 3)

            def general_heads(b):
                pe.wait_ge(s23[3].q_mid, 2 * b + 2)
                pe.wait_ge(s23[3].q_split, b + 1)
                for i in range(T):
                    pe.wait_ge(gen.tw_done, T * b + i + 1)
                    if i >= 1:
                        pe.wait_ge(gen.tw_evac, T * b + i)
                    for j in range(T):
                        mm = pe.transpose(PTP[:, 128 * j:128 * j + 128], PX[:, 128 * j:128 * j + 128], identf[:, :])
                    mm.then_inc(gen.tw_ready, 1)
                with pe.Fori(0, L3.H) as h:
                    n = L3.H * b + h
                    pe.wait_ge(gen.q_evac, n + CREDIT)
                    for c in range(2):
                        mm = pe.matmul(SP[0][:, c * HALF:(c + 1) * HALF],
                                       sel[:, bass.ds(h, 1), :].rearrange("p h n -> p (h n)"),
                                       q_parts[:, c * HALF:(c + 1) * HALF], start=True, stop=True)
                    mm.then_inc(gen.q_ready, 1)
                    for j in range(T):
                        pe.wait_ge(gen.p_done, T * n + j + 1)
                        pe.wait_ge(gen.values, 2 * n + 2)
                        for i in range(T):
                            mm = pe.matmul(PTP[:, 32 * i:32 * i + L3.W], PM[:, 128 * i:128 * i + 128], VG[:, j, :],
                                           start=True, stop=True)
                        mm.then_inc(gen.mm_done, 1)

            def codes(b, tiles):
                for j in tiles:
                    if j < 2:
                        pe.wait_ge(s01[0].x_done, T * b + T - 1 + j)
                        if j == 0:
                            pe.wait_ge(code_done, T * b + T + CODED)
                    else:
                        pe.wait_ge(ct_evac, T * b + j - 1)
                    for i in range(T):
                        mm = pe.transpose(ct_ps[j % 2][:, 128 * i:128 * i + 128], code[:, i, 128 * j:128 * j + 128],
                                          identb[:, :])
                    mm.then_inc(ct_ready, 1)

            def transposes(s, src, b, done, credit=0):
                for i in range(T):
                    if done is not None:
                        pe.wait_ge(done, T * b + i + 1 + credit)
                    mm = pe.transpose(SP[0][:, 128 * i:128 * i + 128], src[:, i, :], identf[:, :])
                mm.then_inc(s.t_ready, 1)

            def attention(l, b):
                s = s01[l]
                src = X[l]
                if l == 0:
                    pe.wait_ge(x0_ready, b + 1 + CREDIT)
                    pe.wait_ge(s23[3].x_done, T * b + CREDIT)
                    transposes(s, src, b, None)
                else:
                    codes(b, range(4))
                    transposes(s, src, b, s01[0].x_done)
                    codes(b, range(4, T))

                def scores(i):
                    if i >= 2:
                        pe.wait_ge(s.e_done, T * b + i - 1)
                    if i == 0:
                        pe.wait_ge(s.xt_done, b + 1)
                        pe.wait_ge(s.at_done, b + 1)
                    if l == 1 and i == 0:
                        pe.wait_ge(ct_evac, T * b + T)
                    if l == 0:
                        pe.wait_ge(neg_done, T * b + i + 1)
                    for n in range(2):
                        o = SP[i % 2][:, n * HALF:(n + 1) * HALF]
                        pe.matmul(o, aT[:, 128 * i:128 * i + 128], xT[:, n * HALF:(n + 1) * HALF],
                                  start=True, stop=False)
                        mm = pe.matmul(o, identb[:, :], other[:, i, n * HALF:(n + 1) * HALF], start=False, stop=True)
                    mm.then_inc(s.s_ready, 1)
                    with pe.If(general != 0):
                        further_kinds(l, b, i)
                    with pe.Else():
                        pe.nop()
                    pe.nop()

                scores(0)
                scores(1)
                for i in range(T):
                    pe.wait_ge(s.p_ready, T * b + i + 1)
                    if i >= 1:
                        pe.wait_ge(s.pt_act, T * b + i)
                        pe.wait_ge(s.pt_dve, T * b + i)
                    for j in range(T):
                        mm = pe.transpose(PTP[:, 128 * j:128 * j + 128], P[i % 2][:, 128 * j:128 * j + 128],
                                          identf[:, :])
                    mm.then_inc(s.pt_ready, 1)
                    if i + 2 < T:
                        scores(i + 2)
                    pe.wait_ge(s.pt_act, T * b + i + 1)
                    pe.wait_ge(s.pt_dve, T * b + i + 1)
                    if i >= 2:
                        pe.wait_ge(s.var_ready, T * b + i - 1)
                    for j in range(T):
                        mm = pe.matmul(ps_one[i % 2][:, 0:D], PT[i % 2][:, 128 * j:128 * j + 128], src[:, j, :],
                                       start=(j == 0), stop=(j == T - 1))
                    mm.then_inc(s.pv_ready, 1)

            def heads_layer(L, b):
                s, H, C, W, l = s23[L.layer], L.H, L.C, L.W, L.layer
                uv, rs, pc, mvv, tt = views(L)
                transposes(s, X[l - 2], b, s01[1].x_done if l == 2 else s23[2].x_done)
                pe.wait_ge(s.xt_done, b + 1)

                for n in range(2):
                    mm = pe.matmul(SP[0][0:H, n * HALF:(n + 1) * HALF], wall[l][:, L.QCOL:L.QCOL + H],
                                   xT[:, n * HALF:(n + 1) * HALF], start=True, stop=True)
                mm.then_inc(s.qr_ready, 1)
                for j in range(T):
                    if j >= 2:
                        pe.wait_ge(s.xp_done, T * b + j - 1)
                    pe.matmul(ps_proj[j % 2][:, 0:L.cols], xT[:, 128 * j:128 * j + 128], wall[l][:, :],
                              start=True, stop=True).then_inc(s.pj_ready, 1)
                pe.wait_ge(s.krep_done, b + 1)
                for h in range(H):
                    mm = pe.matmul(SP[1][:, 128 * h:128 * h + 128], krep[:, h, :], identf[:, :], start=True, stop=True)
                mm.then_inc(s.mb_ready, 1)

                def query_row(h, par):
                    for n in range(2):
                        mm = pe.matmul(SP[par][:, n * HALF:(n + 1) * HALF],
                                       sel[:, bass.ds(h, 1), :].rearrange("p h n -> p (h n)"),
                                       q_parts[:, n * HALF:(n + 1) * HALF], start=True, stop=True)
                    mm.then_inc(s.qb_ready, 1)

                def mask_products():
                    pe.wait_ge(s.parts_done, b + 1)
                    pe.wait_ge(s.mask_done, T * (b + 1))
                    for i in range(T):
                        if i >= 2:
                            pe.wait_ge(s.mv_evac, T * b + i - 1)
                        for j in range(T):
                            mm = pe.matmul(ps_proj[i % 2][:, 0:H * NP * W], mask[:, j, 128 * i:128 * i + 128],
                                           pc[:, j, :, :, W:2 * W].rearrange("p h n c -> p (h n) c"),
                                           start=(j == 0), stop=(j == T - 1))
                        mm.then_inc(s.mv_ready, 1)

                def body(h, par):
                    pe.wait_ge(s.g_ready, T * (H * b + h + 1))
                    if not is_last(h, H):
                        query_row(h + 2, par)
                    for i in range(T):
                        if i == 4 and is_first(h):
                            pe.wait_ge(s.mv_evac, T * (b + 1))
                        if i % 2 == 0 and not is_first(h):
                            pe.wait_ge(s.o_evac, 4 * (H * b + h - 1) + i // 2 + 1)
                        for j in range(T):
                            mm = pe.matmul(OP[i // 2].rearrange("p (i c) -> p i c", i=2)[:, i % 2, 0:NP * 2 * W],
                                           G[:, par, j, 128 * i:128 * i + 128],
                                           pc[:, j, bass.ds(h, 1), :, :].rearrange("p h n k -> p (h n k)"),
                                           start=(j == 0), stop=(j == T - 1))
                        if i % 2:
                            mm.then_inc(s.o_ready, 1)

                def fast():
                    pe.wait_ge(s.q_res, b + 1)
                    pe.wait_ge(s.q_mid, 2 * b + 2)
                    pe.wait_ge(s.q_split, b + 1)
                    query_row(0, 0)
                    pe.wait_ge(s.shift_done, b + 1)
                    query_row(1, 1)
                    mask_products()
                    each_head(pe, H, body)

                def general_layer():
                    mask_products()
                    general_heads(b)

                if l == 2:
                    fast()
                else:
                    with pe.If(general != 0):
                        general_layer()
                    with pe.Else():
                        fast()
                    pe.nop()

            with pe.Fori(0, B) as b:
                attention(0, b)
                attention(1, b)
                heads_layer(L2, b)
                heads_layer(L3, b)


_INS = ["x", "adj", "L0_gnn_a", "L1_gnn_a_0", "L1_gnn_a_1", "L1_gnn_a_2", "L1_gnn_a_3", "L2_gnn_W", "L2_gnn_b",
        "L2_gnn_att_src", "L2_gnn_att_dst", "L3_gnn_W", "L3_gnn_a"]


def kernel(**inputs):
    import numpy as _np
    import concourse.bacc as _bacc
    from concourse import mybir as _mybir
    from concourse.bass_utils import run_bass_kernel_spmd as _run

    nc = _bacc.Bacc("TRN2", target_bir_lowering=False, num_devices=1)
    arrays, args = {}, []
    for name in _INS:
        a = _np.ascontiguousarray(inputs[name])
        arrays[f"in_{name}_dram"] = a
        args.append(nc.dram_tensor(f"in_{name}_dram", a.shape, _mybir.dt.from_np(a.dtype), kind="ExternalInput").ap())
    out = nc.dram_tensor("out_dram", (B, N, D), F32, kind="ExternalOutput").ap()
    build(nc, *args, out)
    r = _run(nc, [arrays], core_ids=[0])
    return r.results[0]["out_dram"]
```

```python
import concourse.bass as bass
from concourse import mybir
from concourse.alu_op_type import AluOpType as ALU
from contextlib import ExitStack

F32 = mybir.dt.float32
BF16 = mybir.dt.bfloat16
I32 = mybir.dt.int32
ACT = mybir.ActivationFunctionType
AX = mybir.AxisListType

B, N, D = 8, 1024, 128
T = N // 128
HALF = N // 2
SLOPE = 0.2
DECAY = 0.1
EPS = 1e-5
BIG = 4.5e16
STEEP = 1e30
NP = 3


SCANNED = 2
CODED = 3
CREDIT = 1


class Steps:

    def __init__(self, eng, sem, base):
        self.eng, self.sem, self.base, self.n = eng, sem, base, 0

    def done(self, ins):
        ins.then_inc(self.sem, 1)
        self.n += 1

    def carry(self):
        self.eng.sem_inc(self.sem, 1)
        self.n += 1

    def wait(self):
        self.eng.wait_ge(self.sem, self.base + self.n)


class Heads:

    def __init__(self, layer, heads):
        self.layer, self.H, self.C = layer, heads, D // heads
        self.W = self.C + 1
        self.QCOL = D + heads
        self.cols = D + 2 * heads


L2, L3 = Heads(2, 4), Heads(3, 8)


CT = 2
CHUNKS = T // CT


MV_BEFORE = 5
MV_BETWEEN = 2


STEPPED = 6


def is_head(h, n):
    return isinstance(h, int) and h == n


def is_last(h, H):
    return isinstance(h, int) and h == H - 1


class AttentionSems:

    def __init__(self, sem, l):
        self.t_ready = sem(f"t_ready_{l}")
        self.xt_done = sem(f"xt_done_{l}")
        self.at_done = sem(f"at_done_{l}")
        self.s_ready = sem(f"s_ready_{l}")
        self.lift_done = sem(f"lift_done_{l}")
        self.e_done = sem(f"e_done_{l}")
        self.nm_ready = sem(f"nm_ready_{l}")
        self.p_ready = sem(f"p_ready_{l}")
        self.pt_ready = sem(f"pt_ready_{l}")
        self.pt_act = sem(f"pt_act_{l}")
        self.pt_dve = sem(f"pt_dve_{l}")
        self.pv_ready = sem(f"pv_ready_{l}")
        self.var_ready = sem(f"var_ready_{l}")
        self.rstd_ready = sem(f"rstd_ready_{l}")
        self.x_done = sem(f"x_done_{l}")


class HeadsSems:

    def __init__(self, sem, l):
        self.t_ready = sem(f"t_ready_{l}")
        self.xt_done = sem(f"xt_done_{l}")
        self.pj_ready = sem(f"pj_ready_{l}")
        self.xp_done = sem(f"xp_done_{l}")
        self.qr_ready = sem(f"qr_ready_{l}")
        self.q_hi = sem(f"q_hi_{l}")
        self.q_res = sem(f"q_res_{l}")
        self.q_mid = sem(f"q_mid_{l}")
        self.q_split = sem(f"q_split_{l}")
        self.qb_ready = sem(f"qb_ready_{l}")
        self.kq_ready = sem(f"kq_ready_{l}")
        self.kq_done = sem(f"kq_done_{l}")
        self.kbig_done = sem(f"kbig_done_{l}")
        self.kdiag_done = sem(f"kdiag_done_{l}")
        self.mb_ready = sem(f"mb_ready_{l}")
        self.shift_done = sem(f"shift_done_{l}")
        self.ac_done = sem(f"ac_done_{l}")
        self.cast1 = sem(f"cast1_{l}")
        self.res1 = sem(f"res1_{l}")
        self.cast2 = sem(f"cast2_{l}")
        self.parts_done = sem(f"parts_done_{l}")
        self.uv_done = sem(f"uv_done_{l}")
        self.mask_done = sem(f"mask_done_{l}")
        self.mv_ready = sem(f"mv_ready_{l}")
        self.mv_evac = sem(f"mv_evac_{l}")
        self.q3_ready = sem(f"q3_ready_{l}")
        self.relu_done = sem(f"relu_done_{l}")
        self.g_ready = sem(f"g_ready_{l}")
        self.o_ready = sem(f"o_ready_{l}")
        self.o_evac = sem(f"o_evac_{l}")
        self.combined = sem(f"combined_{l}")
        self.neg_out = sem(f"neg_out_{l}")
        self.exp_out = sem(f"exp_out_{l}")
        self.var_ready = sem(f"var_ready_{l}")
        self.rstd_ready = sem(f"rstd_ready_{l}")
        self.x_done = sem(f"x_done_{l}")


class KindSems:

    def __init__(self, sem, l):
        self.kind_mask = sem(f"kind_mask_{l}")
        self.kind_ready = sem(f"kind_ready_{l}")
        self.kind_lift = sem(f"kind_lift_{l}")
        self.kind_sum = sem(f"kind_sum_{l}")
        self.kind_max = sem(f"kind_max_{l}")


class GeneralSems:

    def __init__(self, sem, l):
        self.row_loaded = sem(f"row_loaded_{l}")
        self.row_less = sem(f"row_less_{l}")
        self.tw_done = sem(f"tw_done_{l}")
        self.tw_ready = sem(f"tw_ready_{l}")
        self.tw_evac = sem(f"tw_evac_{l}")
        self.q_ready = sem(f"q_ready_{l}")
        self.q_evac = sem(f"q_evac_{l}")
        self.q_max = sem(f"q_max_{l}")
        self.shift = sem(f"shift_{l}")
        self.values = sem(f"values_{l}")
        self.z_sum = sem(f"z_sum_{l}")
        self.z_leaky = sem(f"z_leaky_{l}")
        self.z_done = sem(f"z_done_{l}")
        self.p_exp = sem(f"p_exp_{l}")
        self.p_done = sem(f"p_done_{l}")
        self.mm_done = sem(f"mm_done_{l}")
        self.acc_done = sem(f"acc_done_{l}")


def each_head(eng, H, body):
    for pair in range(H // 2):
        with eng.Fori(0, 1):
            body(2 * pair, 0)
            body(2 * pair + 1, 1)


def build(nc, x, adj, a0, a10, a11, a12, a13, w2, b2, src2, dst2, w3, a3, out):
    ctx = ExitStack()
    with ctx:
        def sb(name, shape, dt=F32):
            return ctx.enter_context(nc.sbuf_tensor(name, shape, dt))

        def sem(name):
            return ctx.enter_context(nc.semaphore(name))

        identf = sb("identf", [128, 128])
        identb = sb("identb", [128, 128], BF16)
        ones = sb("ones", [128, 128])
        neg_half = sb("neg_half", [128, 1])
        exponent = sb("exponent", [128, T])
        a01 = sb("a01", [128, 8])
        w2_nat = sb("w2_nat", [128, 128])
        w3_cat = sb("w3_cat", [128, 128])
        w3_nat = sb("w3_nat", [128, 128])
        b2_row = sb("b2_row", [1, 128])
        b2_col = sb("b2_col", [128, 1])
        b2_rep = sb("b2_rep", [128, 128])
        att = {2: sb("att2", [128, 8]), 3: sb("att3", [128, 16])}
        wall = {2: sb("wall2", [128, 136]), 3: sb("wall3", [128, 144])}
        bias2 = sb("bias2", [128, 136])
        wq_rep = {2: sb("wq_rep2", [128, 2, 128]), 3: sb("wq_rep3", [128, 2, 128])}
        sel = sb("sel", [128, 9, 128], BF16)
        ksq = sb("ksq", [128, B])
        kmax = sb("kmax", [128, B * CHUNKS])
        stat = sb("stat", [128, 2])
        srep = sb("srep", [128, 2, 128])
        glob = sb("glob", [128, 2])
        flag = sb("flag", [128, 1], I32)
        adj_in = sb("adj_in", [128, 2, CT, N], I32)
        code = sb("code", [128, T, N], BF16)
        codeT = sb("codeT", [128, T, N], BF16)
        other = sb("other", [128, T, N], BF16)
        mask = sb("mask", [128, T, N], BF16)
        x_in = sb("x_in", [128, T, D])
        X = [sb("X0", [128, T, D]), sb("X1", [128, T, D]), sb("y_out", [128, T, D])]
        xT = sb("xT", [128, N])
        aT = sb("aT", [128, N])
        G = sb("G", [128, 2, T, N], BF16)
        scratch = G[:, :, :, :].rearrange("p a t n -> p (a t n)").bitcast(F32)
        E = [scratch[:, 0:N], scratch[:, N:2 * N]]
        P = [scratch[:, 2 * N:3 * N], scratch[:, 3 * N:4 * N]]
        PT = [scratch[:, 4 * N:5 * N], scratch[:, 5 * N:6 * N]]
        EK = scratch[:, 6 * N:7 * N]
        NK = scratch[:, 7 * N:7 * N + HALF].bitcast(BF16)
        aK = scratch[:, 7 * N + HALF:7 * N + HALF + 128]
        twT = scratch.rearrange("p (t n) -> p t n", t=T)
        squares = G[:, 0, :, :].rearrange("p t n -> p (t n)")
        rmax = sb("rmax", [128, T])
        nmax = sb("nmax", [128, T])
        den = sb("den", [128, T])
        rden = sb("rden", [128, T])
        Z = sb("Z", [128, T, D])
        stats = sb("stats", [128, T, 6])
        mv = sb("mv", [128, T, 2])
        vare = sb("vare", [128, T])
        rstd = sb("rstd", [128, T])
        XP = sb("XP", [128, T, 144])
        q_parts = sb("q_parts", [128, N], BF16)
        q_mid = sb("q_mid", [8, N], BF16)
        q_res = sb("q_res", [8, N])
        QB = [sb("QB0", [128, N]), sb("QB1", [128, N])]
        kml = sb("kml", [128, 8])
        kcol = sb("kcol", [8, 1])
        kdiag = sb("kdiag", [8, 8])
        Mb = sb("Mb", [128, 8])
        nkey = sb("nkey", [128, T, 8])
        kbig = sb("kbig", [128, T, 8])
        kneg = sb("kneg", [128, T, 8])
        R = sb("R", [128, T, 8])
        UVf = sb("UVf", [128, T * 272])
        RSf = sb("RSf", [128, T * 272])
        PCf = sb("PCf", [128, T * 3 * 272], BF16)
        parts_f = PCf[:, 0:6 * N].bitcast(F32)
        ZT, PX, PM = (parts_f[:, k * N:(k + 1) * N] for k in range(3))
        VG = UVf[:, 0:T * L3.W].rearrange("p (t c) -> p t c", t=T)
        adj_row = QB[1][:, :].bitcast(I32)
        q_most = sb("q_most", [128, 1])
        neg_most = sb("neg_most", [128, 1])
        MVf = sb("MVf", [128, T * 136])
        TTf = RSf
        O = UVf[:, 0:N].rearrange("p (t c) -> p t c", t=T)
        OE = UVf[:, N:2 * N].rearrange("p (t c) -> p t c", t=T)
        rd = sb("rd", [128, T * 8])

        bank = [ctx.enter_context(nc.psum_tensor(f"bank{i}", [128, 2, HALF], F32)) for i in range(4)]
        SP = [bank[0][:, :, :].rearrange("p a n -> p (a n)"), bank[1][:, :, :].rearrange("p a n -> p (a n)")]
        PTP = bank[2][:, :, :].rearrange("p a n -> p (a n)")
        ps_one = [bank[3][:, 0, :], bank[3][:, 1, :]]
        ps_proj = ps_one
        ct_ps = [p.bitcast(BF16) for p in 2 * [SP[0][:, HALF:N], SP[1][:, HALF:N]] + 2 * ps_one]
        OP = [bank[2][:, 0, :], bank[2][:, 1, :]]
        Q3 = bank[3][:, :, :].rearrange("p a n -> p (a n)")

        def views(L):
            W, H = L.W, L.H
            uv = UVf[:, 0:T * H * 2 * W].rearrange("p (t h k c) -> p t h k c", t=T, h=H, k=2)
            rs = RSf[:, 0:T * H * 2 * W].rearrange("p (t h k) -> p t h k", t=T, h=H)
            pc = PCf[:, 0:T * H * NP * 2 * W].rearrange("p (t h n k) -> p t h n k", t=T, h=H, n=NP)
            mvv = MVf[:, 0:T * H * W].rearrange("p (t h c) -> p t h c", t=T, h=H)
            tt = TTf[:, 0:T * H * 2 * W].rearrange("p (t h k) -> p t h k", t=T, h=H)
            return uv, rs, pc, mvv, tt

        weights_in = sem("weights_in")
        const_done = sem("const_done")
        ident_done = sem("ident_done")
        sel_done = sem("sel_done")
        att_zero = sem("att_zero")
        att_in = sem("att_in")
        setup_pe = sem("setup_pe")
        setup_dve = sem("setup_dve")
        adj_loaded = [sem("adj_loaded0"), sem("adj_loaded1")]
        scan_loaded = [sem("scan_loaded0"), sem("scan_loaded1")]
        scan_max = sem("scan_max")
        scan_sq = sem("scan_sq")
        flag_steps = sem("flag_steps")
        flag_rep = sem("flag_rep")
        x_loaded = sem("x_loaded")
        x0_ready = sem("x0_ready")
        code_done = sem("code_done")
        neg_done = sem("neg_done")
        others_done = sem("others_done")
        rden_done = sem("rden_done")
        resid_done = sem("resid_done")
        stats_done = sem("stats_done")
        mv_done = sem("mv_done")
        ct_ready = sem("ct_ready")
        ct_evac = sem("ct_evac")
        out_stored = sem("out_stored")
        wait_taken = sem("wait_taken")
        dve_steps = sem("dve_steps")
        DVE_PER = 256

        s01 = [AttentionSems(sem, l) for l in range(2)]
        s23 = {l: HeadsSems(sem, l) for l in (2, 3)}
        kind = KindSems(sem, "kinds")
        gen = GeneralSems(sem, 3)

        block = ctx.enter_context(nc.Block())
        x_v = x.rearrange("b (t p) d -> b p t d", p=128)
        out_v = out.rearrange("b (t p) d -> b p t d", p=128)
        adj_v = adj.rearrange("b (t p) n -> b p t n", p=128)

        n_weight_dmas = 13
        n_att_dmas = 24

        def combine(eng, L, b, h):
            s, H, C, W = s23[L.layer], L.H, L.C, L.W
            uv, rs, pc, mvv, tt = views(L)
            n = (H - 1) * b + h
            own = mvv[:, :, bass.ds(h, 1), :].rearrange("p t h c -> p t (h c)")
            tth = tt[:, :, bass.ds(h, 1), :].rearrange("p t h k -> p t (h k)")
            eng.wait_ge(s.mv_evac, T * (b + 1))
            eng.wait_ge(s.ac_done, 3 * b + 3)
            eng.wait_ge(s.o_evac, 2 * (H * b + h) + 2)
            eng.tensor_tensor(own, own, tth[:, :, W:2 * W], ALU.subtract).then_inc(s.combined, 1)
            eng.wait_ge(s.combined, 3 * n + 1)
            eng.tensor_tensor(own, own, R[:, :, bass.ds(h, 1)].to_broadcast([128, T, W]), ALU.mult)\
               .then_inc(s.combined, 1)
            eng.wait_ge(s.combined, 3 * n + 2)
            eng.tensor_tensor(own, own, tth[:, :, 0:W], ALU.add).then_inc(s.combined, 1)

        @block.sync
        def _(sp):
            sp.dma_start(x_in[:, :, :], x_v[0]).then_inc(x_loaded, 16)
            for c in range(2):
                sp.dma_start(adj_in[:, c, :, :], adj_v[0, :, CT * c:CT * c + CT, :]).then_inc(adj_loaded[c], 16)
            for k in range(4):
                sp.dma_start(a01[:, k:k + 1], a0[k, :].rearrange("(d a) -> d a", a=1)).then_inc(weights_in, 16)
            for k, v in enumerate((a10, a11, a12, a13)):
                sp.dma_start(a01[:, 4 + k:5 + k], v).then_inc(weights_in, 16)
            sp.dma_start(w2_nat[:, :], w2).then_inc(weights_in, 16)
            sp.dma_start(w3_cat[:, :].rearrange("i (h o) -> i h o", h=8),
                         w3.rearrange("h i o -> i h o")).then_inc(weights_in, 16)
            sp.dma_start(wall[3][:, 0:128].rearrange("i (h o) -> i h o", h=8),
                         w3.rearrange("h i o -> i h o")).then_inc(weights_in, 16)
            sp.dma_start(b2_row[:, :], b2.rearrange("(a n) -> a n", a=1)).then_inc(weights_in, 16)
            sp.dma_start(b2_col[:, :], b2.rearrange("(n a) -> n a", a=1)).then_inc(weights_in, 16)
            sp.wait_ge(att_zero, 2)
            for h in range(4):
                sp.dma_start(att[2][32 * h:32 * h + 32, h:h + 1],
                             src2[0, h, :].rearrange("(c a) -> c a", a=1)).then_inc(att_in, 16)
                sp.dma_start(att[2][32 * h:32 * h + 32, 4 + h:5 + h],
                             dst2[0, h, :].rearrange("(c a) -> c a", a=1)).then_inc(att_in, 16)
            for h in range(8):
                sp.dma_start(att[3][16 * h:16 * h + 16, h:h + 1], a3[h, 16:32, :]).then_inc(att_in, 16)
                sp.dma_start(att[3][16 * h:16 * h + 16, 8 + h:9 + h], a3[h, 0:16, :]).then_inc(att_in, 16)

            def load_x(b, g):
                sp.wait_ge(x0_ready, b + CREDIT)
                sp.sem_inc(wait_taken, 1)
                sp.dma_start(x_in[:, :, :], x_v[g]).then_inc(x_loaded, 16)

            def load_chunk(b, g, c):
                sp.wait_ge(code_done, T * b + CT * (c - 1) + CODED)
                sp.sem_inc(wait_taken, 1)
                sp.dma_start(adj_in[:, c % 2, :, :], adj_v[g, :, CT * c:CT * c + CT, :]).then_inc(adj_loaded[c % 2], 16)

            def rest(b, g, general):
                for c in range(2, CHUNKS):
                    load_chunk(b, g, c)
                if general:
                    for i in range(T):
                        if i == 0:
                            sp.wait_ge(gen.q_evac, L3.H * g + CREDIT)
                            sp.sem_inc(wait_taken, 1)
                            sp.wait_ge(s23[2].x_done, T * (b + 1))
                        else:
                            sp.wait_ge(gen.row_less, T * g + i)
                        sp.sem_inc(wait_taken, 1)
                        sp.dma_start(adj_row, adj_v[g, :, i, :]).then_inc(gen.row_loaded, 16)

            def graphs(base, general):
                with sp.Fori(0, B - 1) as g:
                    b = base + g if base else g
                    rest(b, g, general)
                    load_x(b + 1, g + 1)
                    load_chunk(b + 1, g + 1, 0)
                    load_chunk(b + 1, g + 1, 1)
                rest(base + B - 1, B - 1, general)

            graphs(0, False)
            sp.wait_ge(flag_steps, 5)
            general = sp.value_load(flag[0:1, 0:1], min_val=0, max_val=1)
            with sp.If(general != 0):
                with sp.Fori(0, B) as g:
                    for c in range(CHUNKS):
                        sp.wait_ge(scan_max, CHUNKS * g + c - 1 + SCANNED)
                        sp.sem_inc(wait_taken, 1)
                        sp.dma_start(adj_in[:, c % 2, :, :], adj_v[g, :, CT * c:CT * c + CT, :])\
                          .then_inc(scan_loaded[c % 2], 16)
                sp.wait_ge(scan_max, CHUNKS * B + SCANNED)
                load_x(B, 0)
                load_chunk(B, 0, 0)
                load_chunk(B, 0, 1)
                graphs(B, True)
            with sp.Else():
                sp.nop()
            sp.nop()

        @block.gpsimd
        def _(pool):
            pool.sem_inc(scan_max, SCANNED)
            pool.sem_inc(code_done, CODED)
            for s in (x0_ready, s23[3].t_ready, s23[3].x_done,
                      gen.q_evac, s23[2].o_ready, s23[3].o_ready):
                pool.sem_inc(s, CREDIT)
            pool.memset(att[2][:, :], 0.0).then_inc(att_zero, 1)
            pool.memset(att[3][:, :], 0.0).then_inc(att_zero, 1)
            pool.memset(identf[:, :], 0.0).then_inc(const_done, 1)
            pool.memset(identb[:, :], 0.0).then_inc(const_done, 1)
            pool.memset(ones[:, :], 1.0).then_inc(const_done, 1)
            pool.memset(neg_half[:, :], -0.5).then_inc(const_done, 1)
            pool.memset(exponent[:, :], -0.5).then_inc(const_done, 1)
            pool.memset(sel[:, :, :], 0.0).then_inc(const_done, 1)
            pool.memset(q_parts[:, :], 0.0).then_inc(const_done, 1)
            pool.wait_ge(const_done, 7)
            for n in range(NP):
                pool.affine_select(out=sel[:, :, :], in_=sel[:, :, :], compare_op=ALU.not_equal, fill=1.0,
                                   base=-32 * n, pattern=[[-1, 9], [0, 128]], channel_multiplier=1)\
                    .then_inc(sel_done, 1)
                pool.wait_ge(sel_done, n + 1)
            for m in (identf, identb):
                pool.affine_select(out=m[:, :], in_=m[:, :], compare_op=ALU.not_equal, fill=1.0, base=0,
                                   pattern=[[-1, 128]], channel_multiplier=1).then_inc(ident_done, 1)

            def inverse_root(s, want, c0, c1):
                pool.wait_ge(s.var_ready, want)
                pool.tensor_tensor(rstd[:, c0:c1], vare[:, c0:c1], exponent[:, c0:c1], ALU.pow)\
                    .then_inc(s.rstd_ready, 1)

            def copy_x(b):
                pool.wait_ge(x_loaded, 16 * (b + 1))
                pool.wait_ge(s23[3].t_ready, 2 * b + CREDIT)
                pool.sem_inc(wait_taken, 1)
                pool.tensor_copy(X[0][:, :, :], x_in[:, :, :]).then_inc(x0_ready, 1)

            def combine_heads(L, b):
                with pool.Fori(0, L.H - 1) as h:
                    combine(pool, L, b, h)
                    pool.wait_ge(s23[L.layer].combined, 3 * ((L.H - 1) * b + h + 1))
                    pool.sem_inc(wait_taken, 1)

            def graph(b, g, last, general):
                for l in range(2):
                    for i in range(T):
                        inverse_root(s01[l], T * b + i + 1, i, i + 1)
                combine_heads(L2, b)
                for hf in range(2):
                    inverse_root(s23[2], 2 * b + hf + 1, T // 2 * hf, T // 2 * (hf + 1))
                if not last:
                    copy_x(b + 1)
                if not general:
                    combine_heads(L3, b)
                for hf in range(2):
                    inverse_root(s23[3], 2 * b + hf + 1, T // 2 * hf, T // 2 * (hf + 1))
                    pool.wait_ge(s23[3].rstd_ready, 2 * b + hf + 1)
                    pool.sem_inc(wait_taken, 1)
                    for i in range(4 * hf, 4 * hf + 4):
                        pool.tensor_scalar(X[2][:, i, :], Z[:, i, :], mv[:, i, 0:1], rstd[:, i:i + 1],
                                           ALU.subtract, ALU.mult).then_inc(s23[3].x_done, 1)
                pool.wait_ge(s23[3].x_done, T * (b + 1) + CREDIT)
                pool.dma_start(out_v[g], X[2][:, :, :]).then_inc(out_stored, 16)
                pool.wait_ge(out_stored, 16 * (b + 1))

            def graphs(base, general):
                copy_x(base)
                with pool.Fori(0, B - 1) as g:
                    graph(base + g, g, False, general)
                graph(base + B - 1, B - 1, True, general)

            graphs(0, False)
            pool.wait_ge(flag_steps, 5)
            general = pool.value_load(flag[0:1, 0:1], min_val=0, max_val=1)
            with pool.If(general != 0):
                graphs(B, True)
            with pool.Else():
                pool.nop()
            pool.nop()

        @block.scalar
        def _(act):
            act.wait_ge(const_done, 7)
            act.wait_ge(weights_in, 16 * n_weight_dmas)

            def codes(b, tiles):
                for j in tiles:
                    act.wait_ge(ct_ready, T * b + j + 1)
                    act.activation(codeT[:, j, :], ct_ps[j], ACT.Copy).then_inc(ct_evac, 1)

            def transposed(s, want, hf):
                act.wait_ge(s.t_ready, want)
                act.activation(xT[:, hf * HALF:(hf + 1) * HALF], SP[hf][:, 0:HALF], ACT.Copy).then_inc(s.xt_done, 1)

            def attention(l, b, g, general):
                s = s01[l]
                for hf in range(2):
                    transposed(s, 2 * b + hf + 1, hf)
                    if l == 0:
                        act.activation(aT[:, hf * HALF:(hf + 1) * HALF], SP[hf][:, 0:HALF], ACT.Copy,
                                       scale=a01[:, 0:1]).then_inc(s.at_done, 1)
                    else:
                        codes(b, (4,) if hf == 0 else (5, 6))

                def leaky(i):
                    act.wait_ge(s.s_ready, T * b + i + 1)
                    act.activation(E[i % 2], SP[i % 2], ACT.Relu, scale=SLOPE - 1.0).then_inc(s.lift_done, 1)
                    if general:
                        for k in range(3):
                            act.wait_ge(kind.kind_ready, 3 * (T * (2 * g + l) + i) + k + 1)
                            if k >= 1:
                                act.wait_ge(kind.kind_max, 3 * (T * (2 * g + l) + i) + k)
                            act.activation(EK, SP[i % 2], ACT.Relu, scale=SLOPE - 1.0).then_inc(kind.kind_lift, 1)

                def expo(i):
                    act.wait_ge(s.nm_ready, T * b + i + 1)
                    if i >= 2:
                        act.wait_ge(s.pt_ready, T * b + i - 1)
                    act.activation(P[i % 2], E[i % 2], ACT.Exp, bias=nmax[:, i:i + 1],
                                   accum_out=den[:, i:i + 1]).then_inc(s.p_ready, 1)

                leaky(0)
                if l == 1:
                    codes(b, (7,))
                leaky(1)
                expo(0)
                for i in range(T):
                    if i + 1 < T:
                        expo(i + 1)
                    act.wait_ge(s.pt_ready, T * b + i + 1)
                    if i >= 2:
                        act.wait_ge(s.pv_ready, T * b + i - 1)
                    act.activation(PT[i % 2][:, 0:HALF], PTP[:, 0:HALF], ACT.Copy).then_inc(s.pt_act, 1)
                    if i + 2 < T:
                        act.wait_ge(s.p_ready, T * b + i + 1)
                        leaky(i + 2)
                    elif l == 0:
                        codes(b, (i + 2 - T,))
                if l == 0:
                    codes(b, (2, 3))

            def heads_layer(L, b, g, general):
                s, H, C, W, l = s23[L.layer], L.H, L.C, L.W, L.layer
                uv, rs, pc, mvv, tt = views(L)
                for hf in range(2):
                    transposed(s, 2 * b + hf + 1 + (CREDIT if l == 3 else 0), hf)

                def exponentials():
                    act.wait_ge(s.shift_done, b + 1)
                    act.activation(uv[:, :, :, 1, C], nkey[:, :, 0:H], ACT.Exp, scale=SLOPE).then_inc(s.ac_done, 1)
                    act.activation(uv[:, :, :, 0, C], nkey[:, :, 0:H], ACT.Exp).then_inc(s.ac_done, 1)
                    act.activation(R[:, :, 0:H], R[:, :, 0:H], ACT.Exp, scale=SLOPE - 1.0).then_inc(s.ac_done, 1)

                def cast(n, k):
                    act.wait_ge(s.uv_done if n == 0 else s.res1, 2 * b + 2 - k)
                    whole = uv[:, :, :, k, :] if n == 0 else rs[:, :, :, k * W:(k + 1) * W]
                    act.activation(pc[:, :, :, n, k * W:(k + 1) * W], whole, ACT.Copy)\
                       .then_inc(s.cast1 if n == 0 else s.cast2, 1)

                def query_high():
                    act.wait_ge(s.qr_ready, b + 1)
                    act.activation(q_parts[0:H, :], PTP[0:H, :], ACT.Copy).then_inc(s.q_hi, 1)

                def query_middle():
                    act.wait_ge(s.q_res, b + 1)
                    act.activation(q_mid[0:H, :], q_res[0:H, :], ACT.Copy).then_inc(s.q_mid, 1)
                    act.activation(q_parts[32:32 + H, :], q_res[0:H, :], ACT.Copy).then_inc(s.q_mid, 1)

                def steps(h, par, tiles):
                    for j in tiles:
                        act.activation(G[:, par, j, :], SP[par], ACT.Relu, scale=STEEP,
                                       bias=kbig[:, j, h:h + 1]).then_inc(s.relu_done, 1)

                def body(h, par):
                    if is_head(h, 0):
                        cast(0, 1)
                        cast(0, 0)
                    act.wait_ge(s.qb_ready, (H + 1) * b + h + 1)
                    if is_head(h, 0):
                        act.wait_ge(s.kbig_done, b + 1)
                        steps(h, par, range(1))
                        cast(1, 1)
                        cast(1, 0)
                        steps(h, par, range(1, 4))
                        query_high()
                        steps(h, par, range(4, T))
                    elif is_head(h, 1):
                        steps(h, par, range(2))
                        query_middle()
                        steps(h, par, range(2, T))
                    else:
                        act.wait_ge(s.o_ready, 2 * (H * b + h - 1) + CREDIT)
                        steps(h, par, range(STEPPED))

                if l == 3 and general:
                    exponentials()
                    query_high()
                    query_middle()
                    for n in range(2):
                        cast(n, 1)
                        cast(n, 0)
                    general_weights(b, g)
                else:
                    if l == 3:
                        act.wait_ge(scan_sq, b + 1)
                    exponentials()
                    each_head(act, H, body)
                if l == 2 and not general:
                    act.wait_ge(s.o_ready, 2 * (H * b + H - 1) + CREDIT)
                    act.activation(squares, code[:, :, :].rearrange("p t n -> p (t n)"), ACT.Square,
                                   bias=neg_half[:, 0:1], accum_out=ksq[:, bass.ds(g, 1)]).then_inc(scan_sq, 1)
                if l == 3:
                    for hf in range(2):
                        act.wait_ge(s.neg_out, 2 * b + hf + 1)
                        act.activation(OE[:, 4 * hf:4 * hf + 4, :], OE[:, 4 * hf:4 * hf + 4, :], ACT.Exp)\
                           .then_inc(s.exp_out, 1)

            def general_weights(b, g):
                for i in range(T):
                    act.wait_ge(gen.row_less, T * g + i + 1)
                    if i >= 1:
                        act.wait_ge(gen.tw_ready, T * g + i)
                    act.activation(PX, ZT, ACT.Exp, scale=DECAY).then_inc(gen.tw_done, 1)
                with act.Fori(0, L3.H) as h:
                    n = L3.H * g + h
                    act.wait_ge(gen.q_ready, n + 1)
                    act.activation(QB[0][:, :], SP[0], ACT.Copy).then_inc(gen.q_evac, 1)
                    for j in range(T):
                        act.wait_ge(gen.z_done, T * n + j + 1)
                        act.activation(PX, ZT, ACT.Exp, bias=neg_most[:, 0:1]).then_inc(gen.p_exp, 1)

            def graphs(base, general):
                with act.Fori(0, B) as g:
                    b = base + g if base else g
                    with act.Fori(0, 1):
                        attention(0, b, g, general)
                    attention(1, b, g, general)
                    heads_layer(L2, b, g, general)
                    heads_layer(L3, b, g, general)

            graphs(0, False)
            act.wait_ge(flag_steps, 5)
            general = act.value_load(flag[0:1, 0:1], min_val=0, max_val=1)
            with act.If(general != 0):
                graphs(B, True)
            with act.Else():
                act.nop()
            act.nop()

        @block.vector
        def _(dve):
            dve.wait_ge(setup_pe, 1)
            dve.tensor_copy(wall[2][:, 0:128], ps_one[1][:, 128:256])
            dve.tensor_copy(w3_nat[:, :], ps_one[1][:, 0:128]).then_inc(setup_dve, 1)
            dve.wait_ge(weights_in, 16 * n_weight_dmas)
            dve.tensor_copy(b2_rep[:, :], b2_col[:, 0:1].to_broadcast([128, 128])).then_inc(setup_dve, 1)
            dve.wait_ge(setup_pe, 2)
            dve.tensor_copy(wall[2][:, 128:136], SP[0][:, 0:8]).then_inc(setup_dve, 1)
            dve.tensor_copy(wall[3][:, 128:144], SP[0][:, 8:24]).then_inc(setup_dve, 1)
            dve.tensor_copy(bias2[:, 0:136], SP[0][:, 32:168]).then_inc(setup_dve, 1)
            dve.tensor_copy(wq_rep[2][:, :, :], SP[0][:, 4:6].unsqueeze(2).to_broadcast([128, 2, 128]))\
               .then_inc(setup_dve, 1)
            dve.tensor_copy(wq_rep[3][:, :, :], SP[0][:, 16:18].unsqueeze(2).to_broadcast([128, 2, 128]))\
               .then_inc(setup_dve, 1)

            def further_kinds(l, g, i):
                s, n = kind, 3 * (T * (2 * g + l) + i)
                for k in range(3):
                    dve.tensor_scalar(NK, code[:, i, :], float(k + 2), -BIG, ALU.not_equal, ALU.mult)\
                       .then_inc(s.kind_mask, 1)
                    dve.tensor_scalar(aK, xT[:, 128 * i:128 * i + 128], a01[:, 4 * l + k + 1:4 * l + k + 2], None,
                                      ALU.mult).then_inc(s.kind_mask, 1)
                    dve.wait_ge(s.kind_lift, n + k + 1)
                    dve.tensor_tensor(EK, SP[i % 2], EK, ALU.add).then_inc(s.kind_sum, 1)
                    dve.wait_ge(s.kind_sum, n + k + 1)
                    dve.tensor_tensor(E[i % 2], E[i % 2], EK, ALU.max).then_inc(s.kind_max, 1)
                    dve.wait_ge(s.kind_max, n + k + 1)
                dve.tensor_reduce(rmax[:, i:i + 1], E[i % 2], AX.X, ALU.max).then_inc(s.kind_mask, 1)
                dve.wait_ge(s.kind_mask, 7 * (T * (2 * g + l) + i + 1))
                dve.sem_inc(wait_taken, 1)

            def code_tile(b, i):
                c = i // CT
                dve.wait_ge(adj_loaded[c % 2], 16 * (CHUNKS // 2 * b + c // 2 + 1))
                dve.tensor_scalar(code[:, i, :], adj_in[:, c % 2, i % CT, :], -1.0, 5.0, ALU.max, ALU.min)\
                   .then_inc(code_done, 1)
                dve.wait_ge(code_done, T * b + i + 1 + CODED)
                dve.tensor_scalar(other[:, i, :], code[:, i, :], 1.0, -BIG, ALU.not_equal, ALU.mult)\
                   .then_inc(neg_done, 1)

            def mask_tile(b, j, st):
                dve.wait_ge(ct_evac, T * b + j + 1)
                dve.tensor_scalar(mask[:, j, :], codeT[:, j, :], 0.0, None, ALU.is_gt).then_inc(others_done, 1)
                dve.wait_ge(others_done, T * b + j + 1)
                own = mask[:, j, 128 * j:128 * j + 128]
                dve.tensor_tensor(own, own, identb[:, :], ALU.max).then_inc(s23[2].mask_done, 1)

            def attention(l, b, g, general, st):
                s = s01[l]
                src, dst = X[l], X[1 - l]
                if l == 1:
                    for hf in range(2):
                        half = slice(hf * HALF, (hf + 1) * HALF)
                        dve.wait_ge(s.xt_done, 2 * b + hf + 1)
                        dve.tensor_scalar(aT[:, half], xT[:, half], a01[:, 4:5], None, ALU.mult)\
                           .then_inc(s.at_done, 1)

                def row_max(i):
                    dve.wait_ge(s.lift_done, T * b + i + 1)
                    dve.sem_inc(wait_taken, 1)
                    dve.tensor_tensor_reduce(out=E[i % 2], in0=SP[i % 2], in1=E[i % 2], scale=1.0, scalar=-3e38,
                                             op0=ALU.add, op1=ALU.max, accum_out=rmax[:, i:i + 1])\
                       .then_inc(s.e_done, 1)
                    dve.wait_ge(s.e_done, T * b + i + 1)
                    if general:
                        dve.sem_inc(wait_taken, 1)
                        further_kinds(l, g, i)
                    dve.tensor_scalar(nmax[:, i:i + 1], rmax[:, i:i + 1], -1.0, None, ALU.mult)\
                       .then_inc(s.nm_ready, 1)

                def finish(i):
                    if l == 0 and i == 0:
                        dve.wait_ge(s23[3].x_done, T * b + CREDIT)
                    dve.wait_ge(s.pv_ready, T * b + i + 1)
                    dve.wait_ge(s.p_ready, T * b + i + 1)
                    m = T * (2 * b + l) + i + 1
                    dve.reciprocal(rden[:, i:i + 1], den[:, i:i + 1]).then_inc(rden_done, 1)
                    dve.wait_ge(rden_done, m)
                    dve.scalar_tensor_tensor(Z[:, i, :], ps_one[i % 2][:, 0:D], rden[:, i:i + 1],
                                             src[:, i, :], ALU.mult, ALU.add).then_inc(resid_done, 1)
                    dve.wait_ge(resid_done, m)
                    dve.bn_stats(stats[:, i, :], Z[:, i, :]).then_inc(stats_done, 1)
                    dve.wait_ge(stats_done, m)
                    dve.sem_inc(wait_taken, 1)
                    dve.bn_aggr(mv[:, i, :], stats[:, i, :]).then_inc(mv_done, 1)
                    dve.wait_ge(mv_done, m)
                    dve.tensor_scalar(vare[:, i:i + 1], mv[:, i, 1:2], EPS, None, ALU.add).then_inc(s.var_ready, 1)

                def normal(i):
                    dve.wait_ge(s.rstd_ready, T * b + i + 1)
                    dve.tensor_scalar(dst[:, i, :], Z[:, i, :], mv[:, i, 0:1], rstd[:, i:i + 1],
                                      ALU.subtract, ALU.mult).then_inc(s.x_done, 1)

                if l == 0:
                    code_tile(b, 0)
                    code_tile(b, 1)
                row_max(0)
                if l == 0:
                    code_tile(b, 2)
                row_max(1)
                for i in range(T):
                    dve.wait_ge(s.pt_ready, T * b + i + 1)
                    if i >= 2:
                        dve.wait_ge(s.pv_ready, T * b + i - 1)
                    dve.tensor_copy(PT[i % 2][:, HALF:N], PTP[:, HALF:N]).then_inc(s.pt_dve, 1)
                    if i >= 2:
                        normal(i - 2)
                    if l == 1 and i >= 1:
                        mask_tile(b, i - 1, st)
                    if l == 0 and i + 3 < T:
                        code_tile(b, i + 3)
                    if i + 2 < T:
                        row_max(i + 2)
                    if i >= 1:
                        finish(i - 1)
                normal(T - 2)
                if l == 1:
                    mask_tile(b, T - 1, st)
                finish(T - 1)
                normal(T - 1)

            def general_heads(b, g, sums):
                s = s23[3]
                dve.wait_ge(s.mv_evac, T * (b + 1))
                dve.wait_ge(s.mask_done, T * (b + 1))
                for i in range(T):
                    dve.wait_ge(gen.row_loaded, 16 * (T * g + i + 1))
                    if i >= 1:
                        dve.wait_ge(gen.tw_done, T * g + i)
                    dve.tensor_scalar(ZT, adj_row, glob[:, 1:2], None, ALU.subtract).then_inc(gen.row_less, 1)
                    dve.wait_ge(gen.tw_ready, T * g + i + 1)
                    dve.tensor_copy(twT[:, :, 128 * i:128 * i + 128], PTP.rearrange("p (t n) -> p t n", t=T))\
                       .then_inc(gen.tw_evac, 1)
                dve.wait_ge(gen.tw_evac, T * (g + 1))
                dve.sem_inc(wait_taken, 1)
                with dve.Fori(0, L3.H) as h:
                    n = L3.H * g + h
                    dve.memset(VG[:, :, L3.C:L3.W], 1.0).then_inc(gen.values, 1)
                    dve.tensor_copy(VG[:, :, 0:L3.C], XP[:, :, bass.ds(L3.C * h, L3.C)]).then_inc(gen.values, 1)
                    dve.wait_ge(gen.q_evac, n + 1 + CREDIT)
                    dve.tensor_reduce(q_most[:, :], QB[0][:, :], AX.X, ALU.max).then_inc(gen.q_max, 1)
                    dve.wait_ge(gen.q_max, n + 1)
                    dve.tensor_scalar(neg_most[:, :], q_most[:, :], Mb[:, bass.ds(h, 1)], 0.0, ALU.add, ALU.max)\
                       .then_inc(gen.shift, 1)
                    dve.wait_ge(gen.shift, 2 * n + 1)
                    dve.tensor_scalar(neg_most[:, :], neg_most[:, :], -1.0, None, ALU.mult).then_inc(gen.shift, 1)
                    dve.wait_ge(gen.shift, 2 * n + 2)
                    for j in range(T):
                        m = T * n + j
                        dve.tensor_scalar(PM, QB[0][:, :], XP[:, j, bass.ds(D + h, 1)], None, ALU.add)\
                           .then_inc(gen.z_sum, 1)
                        dve.wait_ge(gen.z_sum, m + 1)
                        dve.scalar_tensor_tensor(ZT, PM, SLOPE, PM, ALU.mult, ALU.max).then_inc(gen.z_leaky, 1)
                        dve.wait_ge(gen.z_leaky, m + 1)
                        dve.tensor_tensor(ZT, ZT, twT[:, j, :], ALU.mult).then_inc(gen.z_done, 1)
                        dve.wait_ge(gen.p_exp, m + 1)
                        dve.tensor_tensor(PM, PX, mask[:, j, :], ALU.mult).then_inc(gen.p_done, 1)
                        dve.wait_ge(gen.mm_done, m + 1)
                        part = PTP[:, 0:T * 32].rearrange("p (t c) -> p t c", t=T)[:, :, 0:L3.W]
                        whole = sums[:, :, bass.ds(h, 1), :].rearrange("p t h c -> p t (h c)")
                        if j == 0:
                            dve.tensor_copy(whole, part).then_inc(gen.acc_done, 1)
                        else:
                            dve.tensor_tensor(whole, whole, part, ALU.add).then_inc(gen.acc_done, 1)
                        dve.wait_ge(gen.acc_done, m + 1)
                    dve.sem_inc(wait_taken, 1)

            def heads_layer(L, b, g, general, st):
                s, H, C, W, l = s23[L.layer], L.H, L.C, L.W, L.layer
                uv, rs, pc, mvv, tt = views(L)
                src, dst = X[l - 2], X[l - 1]
                kq = XP[:, :, D:D + 2 * H]
                key = XP[:, :, D:D + H]
                qry = XP[:, :, D + H:D + 2 * H]


                def projected(hf):
                    dve.wait_ge(s.pj_ready, 2 * b + hf + 1)
                    own = XP[:, 4 * hf:4 * hf + 4, 0:D]
                    ps = SP[hf][:, HALF:N].rearrange("p (t c) -> p t c", t=4)
                    if l == 2:
                        dve.tensor_tensor(own, ps, bias2[:, 0:D].unsqueeze(1).to_broadcast([128, 4, D]), ALU.add)\
                           .then_inc(s.xp_done, 1)
                    else:
                        dve.tensor_copy(own, ps).then_inc(s.xp_done, 1)

                projected(0)
                kq_ps = OP[0][:, 0:T * 2 * H].rearrange("p (t c) -> p t c", t=T)
                dve.wait_ge(s.kq_ready, b + 1)
                if l == 2:
                    dve.tensor_tensor(kq, kq_ps, bias2[:, D:D + 2 * H].unsqueeze(1).to_broadcast([128, T, 2 * H]),
                                      ALU.add).then_inc(s.kq_done, 1)
                else:
                    dve.tensor_copy(kq, kq_ps).then_inc(s.kq_done, 1)
                dve.wait_ge(s.kq_done, 2 * b + 1)
                dve.tensor_reduce(kml[:, 0:H], key.rearrange("p t h -> p h t"), AX.X, ALU.max).then_inc(s.kq_done, 1)
                dve.wait_ge(s.mb_ready, 2 * b + 1)
                st.done(dve.tensor_reduce(kcol[0:H, :], OP[1][0:H, 0:128], AX.X, ALU.max))
                st.wait()
                dve.tensor_scalar(kdiag[0:H, 0:H], identf[0:H, 0:H], kcol[0:H, 0:1], None, ALU.mult)\
                   .then_inc(s.kdiag_done, 1)
                if l == 2:
                    st.done(dve.tensor_tensor(kbig[:, :, 0:H], key, bias2[:, D + H:D + 2 * H].unsqueeze(1)
                                              .to_broadcast([128, T, H]), ALU.add))
                    st.wait()
                    st.done(dve.tensor_scalar(kneg[:, :, 0:H], kbig[:, :, 0:H], -1.0, None, ALU.mult))
                    dve.tensor_scalar(kbig[:, :, 0:H], kbig[:, :, 0:H], STEEP, None, ALU.mult)\
                       .then_inc(s.kbig_done, 1)
                else:
                    st.done(dve.tensor_scalar(kneg[:, :, 0:H], key, -1.0, None, ALU.mult))
                    dve.tensor_scalar(kbig[:, :, 0:H], key, STEEP, None, ALU.mult).then_inc(s.kbig_done, 1)
                dve.wait_ge(s.mb_ready, 2 * b + 2)
                st.done(dve.tensor_copy(Mb[:, 0:H], OP[1][:, 256:256 + H]))
                st.wait()
                mb_all = Mb[:, 0:H].unsqueeze(1).to_broadcast([128, T, H])
                st.done(dve.tensor_tensor(nkey[:, :, 0:H], key, mb_all, ALU.subtract))
                st.done(dve.tensor_tensor(R[:, :, 0:H], qry, mb_all, ALU.add))
                st.wait()
                dve.tensor_scalar(R[:, :, 0:H], R[:, :, 0:H], 0.0, None, ALU.max).then_inc(s.shift_done, 1)
                projected(1)
                dve.wait_ge(s.xp_done, 2 * b + 2)

                def products(k):
                    dve.wait_ge(s.ac_done, 3 * b + 2 - k)
                    dve.tensor_tensor(uv[:, :, :, k, 0:C], XP[:, :, 0:D].rearrange("p t (h c) -> p t h c", h=H),
                                      uv[:, :, :, k, C:W].to_broadcast([128, T, H, C]), ALU.mult)\
                       .then_inc(s.uv_done, 1)

                def residue(k):
                    dve.wait_ge(s.uv_done, 2 * b + 2 - k)
                    dve.wait_ge(s.cast1, 2 * b + 2 - k)
                    dve.tensor_tensor(rs[:, :, :, k * W:(k + 1) * W], uv[:, :, :, k, :],
                                      pc[:, :, :, 0, k * W:(k + 1) * W], ALU.subtract).then_inc(s.res1, 1)

                def last_part(k):
                    dve.wait_ge(s.res1, 2 * b + 2 - k)
                    dve.wait_ge(s.cast2, 2 * b + 2 - k)
                    dve.tensor_tensor(pc[:, :, :, 2, k * W:(k + 1) * W], rs[:, :, :, k * W:(k + 1) * W],
                                      pc[:, :, :, 1, k * W:(k + 1) * W], ALU.subtract).then_inc(s.parts_done, 1)

                def query_rest():
                    dve.wait_ge(s.qr_ready, b + 1)
                    dve.wait_ge(s.q_hi, b + 1)
                    dve.tensor_tensor(q_res[0:H, :], PTP[0:H, :], q_parts[0:H, :], ALU.subtract).then_inc(s.q_res, 1)

                def query_last():
                    dve.wait_ge(s.q_res, b + 1)
                    dve.wait_ge(s.q_mid, 2 * b + 2)
                    dve.tensor_tensor(q_parts[64:64 + H, :], q_res[0:H, :], q_mid[0:H, :], ALU.subtract)\
                       .then_inc(s.q_split, 1)

                def mask_sums(i):
                    dve.wait_ge(s.mv_ready, T * b + i + 1)
                    dve.tensor_copy(mvv[:, i, :, :], ps_proj[i % 2][:, 0:H * W].rearrange("p (h c) -> p h c", h=H))\
                       .then_inc(s.mv_evac, 1)

                def take(h, q):
                    dve.wait_ge(s.o_ready, 2 * (H * b + h) + q + 1 + CREDIT)
                    dve.tensor_copy(tt[:, 4 * q:4 * q + 4, h:h + 1, :].rearrange("p i h k -> p i (h k)"),
                                    OP[q][:, 0:8 * W].rearrange("p (i k) -> p i k", i=4)).then_inc(s.o_evac, 1)

                RELUS = 2 * T + STEPPED * (H - 2)

                def cut(h, par, j):
                    if is_head(h, 0) or is_head(h, 1):
                        n = T * h + j + 1
                    else:
                        n = 2 * T + STEPPED * (h - 2) + j + 1
                    dve.wait_ge(s.relu_done, RELUS * b + n)
                    dve.tensor_tensor(G[:, par, j, :], G[:, par, j, :], mask[:, j, :], ALU.min)\
                       .then_inc(s.g_ready, 1)

                def own_step(h, par, j):
                    dve.wait_ge(s.q3_ready, (H - 2) * b + h - 1)
                    dve.scalar_tensor_tensor(G[:, par, j, :], Q3, kneg[:, j, h:h + 1], mask[:, j, :],
                                             ALU.is_gt, ALU.mult).then_inc(s.g_ready, 1)

                def body(h, par):
                    if is_head(h, 0):
                        for step in (products, residue, last_part):
                            step(1)
                            step(0)
                        for j in range(4):
                            cut(h, par, j)
                        mask_sums(0)
                        query_rest()
                        for j in range(4, T):
                            mask_sums(j - 3)
                            cut(h, par, j)
                    elif is_head(h, 1):
                        for j in range(2):
                            cut(h, par, j)
                        query_last()
                        for j in range(2, T):
                            cut(h, par, j)
                        for q in range(2):
                            take(h - 1, q)
                        for i in range(MV_BEFORE, MV_BEFORE + MV_BETWEEN):
                            mask_sums(i)
                    else:
                        if is_head(h, 2):
                            for j in range(STEPPED):
                                cut(h, par, j)
                            for i in range(MV_BEFORE + MV_BETWEEN, T):
                                mask_sums(i)
                        else:
                            dve.wait_ge(s.o_ready, 2 * (H * b + h - 1) + CREDIT)
                        for j in range(STEPPED, T):
                            own_step(h, par, j)
                        if not is_head(h, 2):
                            for j in range(STEPPED):
                                cut(h, par, j)
                        for q in range(2):
                            take(h - 1, q)
                    dve.sem_inc(wait_taken, 1)

                def fast():
                    dve.sem_inc(wait_taken, 1)
                    each_head(dve, H, body)

                def last_combined(hf):
                    h, half = H - 1, slice(4 * hf, 4 * hf + 4)
                    take(h, hf)
                    dve.wait_ge(s.o_evac, 2 * (H * b + h) + hf + 1)
                    own, tth = mvv[:, half, h, :], tt[:, half, h, :]
                    st.done(dve.tensor_tensor(own, own, tth[:, :, W:2 * W], ALU.subtract))
                    st.wait()
                    st.done(dve.tensor_tensor(own, own, R[:, half, h:h + 1].to_broadcast([128, 4, W]), ALU.mult))
                    st.wait()
                    st.done(dve.tensor_tensor(own, own, tth[:, :, 0:W], ALU.add))
                    dve.wait_ge(s.combined, 3 * (H - 1) * (b + 1))

                def general_layer():
                    products(1)
                    products(0)
                    query_rest()
                    query_last()
                    for k in (1, 0):
                        residue(k)
                    for k in (1, 0):
                        last_part(k)
                    for i in range(T):
                        mask_sums(i)
                    general_heads(b, g, mvv)

                if l == 3 and general:
                    general_layer()
                else:
                    fast()
                rdh = rd[:, 0:T * H].rearrange("p (t h) -> p t h", t=T)

                def outputs(hf):
                    half = slice(4 * hf, 4 * hf + 4)
                    if not (l == 3 and general):
                        last_combined(hf)
                    st.wait()
                    st.done(dve.reciprocal(rdh[:, half, :], mvv[:, half, :, C]))
                    st.wait()
                    st.done(dve.tensor_tensor(O[:, half, :].rearrange("p t (h c) -> p t h c", h=H),
                                              mvv[:, half, :, 0:C],
                                              rdh[:, half, :].unsqueeze(3).to_broadcast([128, 4, H, C]), ALU.mult))
                    st.wait()
                    if l == 3:
                        dve.tensor_scalar(OE[:, half, :], O[:, half, :], 0.0, None, ALU.min).then_inc(s.neg_out, 1)
                        st.done(dve.tensor_scalar(O[:, half, :], O[:, half, :], 0.0, -1.0, ALU.max, ALU.add))

                def statistics(hf):
                    half = slice(4 * hf, 4 * hf + 4)
                    st.wait()
                    if l == 3:
                        dve.wait_ge(s.exp_out, 2 * b + hf + 1)
                        st.done(dve.tensor_tensor(O[:, half, :], O[:, half, :], OE[:, half, :], ALU.add))
                        st.wait()
                    st.done(dve.tensor_tensor(Z[:, half, :], O[:, half, :], src[:, half, :], ALU.add))
                    st.wait()
                    for i in range(4 * hf, 4 * hf + 4):
                        m = dve.bn_stats(stats[:, i, :], Z[:, i, :])
                    st.done(m)
                    st.wait()
                    st.carry()
                    for i in range(4 * hf, 4 * hf + 4):
                        m = dve.bn_aggr(mv[:, i, :], stats[:, i, :])
                    st.done(m)
                    st.wait()
                    dve.tensor_scalar(vare[:, half], mv[:, half, 1], EPS, None, ALU.add).then_inc(s.var_ready, 1)

                def normal(hf):
                    dve.wait_ge(s.rstd_ready, 2 * b + hf + 1)
                    for i in range(4 * hf, 4 * hf + 4):
                        dve.tensor_scalar(dst[:, i, :], Z[:, i, :], mv[:, i, 0:1], rstd[:, i:i + 1],
                                          ALU.subtract, ALU.mult).then_inc(s.x_done, 1)

                def next_mask():
                    dve.wait_ge(s.g_ready, T * H * (b + 1))
                    for j in range(T):
                        own = slice(0, N) if general else slice(128 * j, 128 * j + 128)
                        dve.tensor_scalar(mask[:, j, own], codeT[:, j, own], 0.0, None, ALU.not_equal)\
                           .then_inc(s23[3].mask_done, 1)

                if l == 2:
                    next_mask()
                outputs(0)
                statistics(0)
                outputs(1)
                if l == 2:
                    normal(0)
                statistics(1)
                if l == 2:
                    normal(1)

            def graphs(base, general):
                with dve.Fori(0, B) as g:
                    b = base + g if base else g
                    st = Steps(dve, dve_steps, DVE_PER * b)
                    attention(0, b, g, general, st)
                    attention(1, b, g, general, st)
                    heads_layer(L2, b, g, general, st)
                    heads_layer(L3, b, g, general, st)
                    dve.sem_inc(dve_steps, DVE_PER - st.n)

            def most(k, values):
                n = 5 * k
                dve.tensor_reduce(stat[:, k:k + 1], values, AX.X, ALU.max).then_inc(flag_steps, 1)
                dve.wait_ge(flag_steps, n + 1)
                dve.tensor_copy(srep[:, k, :], stat[:, k:k + 1].to_broadcast([128, 128])).then_inc(flag_steps, 1)
                dve.wait_ge(flag_rep, k + 1)
                dve.tensor_reduce(glob[:, k:k + 1], ps_one[0][:, 128 * k:128 * k + 128], AX.X, ALU.max)\
                   .then_inc(flag_steps, 1)

            graphs(0, False)
            dve.wait_ge(scan_sq, B)
            most(0, ksq[:, :])
            dve.wait_ge(flag_steps, 3)
            dve.tensor_scalar(glob[:, 0:1], glob[:, 0:1], T * N * 0.25, None, ALU.is_gt).then_inc(flag_steps, 1)
            dve.wait_ge(flag_steps, 4)
            dve.tensor_copy(flag[:, :], glob[:, 0:1]).then_inc(flag_steps, 1)
            dve.wait_ge(flag_steps, 5)
            general = dve.value_load(flag[0:1, 0:1], min_val=0, max_val=1)
            with dve.If(general != 0):
                with dve.Fori(0, B) as g:
                    for c in range(CHUNKS):
                        dve.wait_ge(scan_loaded[c % 2], 16 * (CHUNKS // 2 * g + c // 2 + 1))
                        dve.tensor_reduce(kmax[:, bass.ds(CHUNKS * g + c, 1)],
                                          adj_in[:, c % 2, :, :].rearrange("p t n -> p (t n)"),
                                          AX.X, ALU.max).then_inc(scan_max, 1)
                dve.wait_ge(scan_max, CHUNKS * B + SCANNED)
                most(1, kmax[:, :])
                dve.wait_ge(flag_steps, 8)
                dve.sem_inc(wait_taken, 1)
                graphs(B, True)
            with dve.Else():
                dve.nop()
            dve.nop()

        @block.tensor
        def _(pe):
            pe.wait_ge(ident_done, 2)
            pe.wait_ge(const_done, 7)
            pe.wait_ge(weights_in, 16 * n_weight_dmas)
            pe.wait_ge(att_in, 16 * n_att_dmas)
            pe.transpose(ps_one[1][:, 0:128], w3_cat[:, :], identf[:, :])
            pe.transpose(ps_one[1][:, 128:256], w2_nat[:, :], identf[:, :]).then_inc(setup_pe, 1)
            pe.wait_ge(setup_dve, 2)
            pe.matmul(SP[0][:, 0:8], w2_nat[:, :], att[2][:, :], start=True, stop=True)
            pe.matmul(SP[0][:, 8:24], w3_nat[:, :], att[3][:, :], start=True, stop=True)
            pe.matmul(SP[0][:, 32:160], ones[0:1, :], b2_row[:, :], start=True, stop=True)
            pe.matmul(SP[0][:, 160:168], b2_rep[:, :], att[2][:, :], start=True, stop=True).then_inc(setup_pe, 1)
            pe.wait_ge(setup_dve, 7)
            pe.wait_ge(sel_done, NP)

            def further_kinds(l, b, g, i):
                s, n = kind, 3 * (T * (2 * g + l) + i)
                pe.wait_ge(s01[l].e_done, T * b + i + 1)
                for k in range(3):
                    pe.wait_ge(s.kind_mask, 7 * (T * (2 * g + l) + i) + 2 * k + 2)
                    if k >= 1:
                        pe.wait_ge(s.kind_sum, n + k)
                    for c in range(2):
                        o = SP[i % 2][:, c * HALF:(c + 1) * HALF]
                        pe.matmul(o, aK, xT[:, c * HALF:(c + 1) * HALF], start=True, stop=False)
                        mm = pe.matmul(o, identb[:, :], NK[:, c * HALF:(c + 1) * HALF], start=False, stop=True)
                    mm.then_inc(s.kind_ready, 1)
                pe.wait_ge(s.kind_sum, n + 3)

            def general_heads(b, g):
                pe.wait_ge(s23[3].q_mid, 2 * b + 2)
                pe.wait_ge(s23[3].q_split, b + 1)
                for i in range(T):
                    pe.wait_ge(gen.tw_done, T * g + i + 1)
                    if i >= 1:
                        pe.wait_ge(gen.tw_evac, T * g + i)
                    for j in range(T):
                        mm = pe.transpose(PTP[:, 128 * j:128 * j + 128], PX[:, 128 * j:128 * j + 128], identf[:, :])
                    mm.then_inc(gen.tw_ready, 1)
                with pe.Fori(0, L3.H) as h:
                    n = L3.H * g + h
                    pe.wait_ge(gen.q_evac, n + CREDIT)
                    for c in range(2):
                        mm = pe.matmul(SP[0][:, c * HALF:(c + 1) * HALF],
                                       sel[:, bass.ds(h, 1), :].rearrange("p h n -> p (h n)"),
                                       q_parts[:, c * HALF:(c + 1) * HALF], start=True, stop=True)
                    mm.then_inc(gen.q_ready, 1)
                    for j in range(T):
                        pe.wait_ge(gen.p_done, T * n + j + 1)
                        pe.wait_ge(gen.values, 2 * n + 2)
                        for i in range(T):
                            mm = pe.matmul(PTP[:, 32 * i:32 * i + L3.W], PM[:, 128 * i:128 * i + 128], VG[:, j, :],
                                           start=True, stop=True)
                        mm.then_inc(gen.mm_done, 1)
                pe.wait_ge(gen.q_evac, L3.H * (g + 1) + CREDIT)

            def codes(b, tiles):
                for j in tiles:
                    if j == 0:
                        pe.wait_ge(code_done, T * b + T + CODED)
                    if j in (4, 5):
                        pe.wait_ge(s01[0].var_ready, T * b + j + 3)
                    if j in (2, 3, 6, 7):
                        pe.wait_ge(ct_evac, T * b + j - 1)
                    for i in range(T):
                        mm = pe.transpose(ct_ps[j][:, 128 * i:128 * i + 128], code[:, i, 128 * j:128 * j + 128],
                                          identb[:, :])
                    mm.then_inc(ct_ready, 1)

            def transposes(s, src, b, hf, done):
                for i in range(4 * hf, 4 * hf + 4):
                    if done is not None:
                        pe.wait_ge(done, T * b + i + 1)
                    mm = pe.transpose(SP[hf][:, 128 * (i % 4):128 * (i % 4) + 128], src[:, i, :], identf[:, :])
                mm.then_inc(s.t_ready, 1)

            def attention(l, b, g, general):
                s = s01[l]
                src = X[l]
                if l == 0:
                    pe.wait_ge(x0_ready, b + 1 + CREDIT)
                for hf in range(2):
                    transposes(s, src, b, hf, s01[0].x_done if l == 1 else None)
                    if l == 1:
                        codes(b, (4,) if hf == 0 else (5, 6))

                def scores(i):
                    if i >= 2:
                        pe.wait_ge(s.e_done, T * b + i - 1)
                    if i == 0:
                        pe.wait_ge(s.xt_done, 2 * b + 2)
                        pe.wait_ge(s.at_done, 2 * b + 2)
                        if l == 1:
                            pe.wait_ge(ct_evac, T * b + 4)
                    for n in range(2):
                        pe.matmul(SP[i % 2][:, n * HALF:(n + 1) * HALF], aT[:, 128 * i:128 * i + 128],
                                  xT[:, n * HALF:(n + 1) * HALF], start=True, stop=False)
                    if l == 0:
                        pe.wait_ge(neg_done, T * b + i + 1)
                    for n in range(2):
                        mm = pe.matmul(SP[i % 2][:, n * HALF:(n + 1) * HALF], identb[:, :],
                                       other[:, i, n * HALF:(n + 1) * HALF], start=False, stop=True)
                    mm.then_inc(s.s_ready, 1)
                    if general:
                        further_kinds(l, b, g, i)

                scores(0)
                if l == 1:
                    codes(b, (7,))
                scores(1)
                for i in range(T):
                    pe.wait_ge(s.p_ready, T * b + i + 1)
                    if i >= 1:
                        pe.wait_ge(s.pt_act, T * b + i)
                        pe.wait_ge(s.pt_dve, T * b + i)
                    for j in range(T):
                        mm = pe.transpose(PTP[:, 128 * j:128 * j + 128], P[i % 2][:, 128 * j:128 * j + 128],
                                          identf[:, :])
                    mm.then_inc(s.pt_ready, 1)
                    if i + 2 < T:
                        scores(i + 2)
                    elif l == 0:
                        codes(b, (i + 2 - T,))
                    pe.wait_ge(s.pt_act, T * b + i + 1)
                    pe.wait_ge(s.pt_dve, T * b + i + 1)
                    if l == 1 and i == 0:
                        pe.wait_ge(ct_evac, T * b + T)
                    if i >= 2:
                        pe.wait_ge(s.var_ready, T * b + i - 1)
                    for j in range(T):
                        mm = pe.matmul(ps_one[i % 2][:, 0:D], PT[i % 2][:, 128 * j:128 * j + 128], src[:, j, :],
                                       start=(j == 0), stop=(j == T - 1))
                    mm.then_inc(s.pv_ready, 1)
                if l == 0:
                    codes(b, (2, 3))

            def heads_layer(L, b, g, general):
                s, H, C, W, l = s23[L.layer], L.H, L.C, L.W, L.layer
                uv, rs, pc, mvv, tt = views(L)
                for hf in range(2):
                    transposes(s, X[l - 2], b, hf, s01[1].x_done if l == 2 else s23[2].x_done)
                    pe.wait_ge(s.xt_done, 2 * b + hf + 1)
                    for j in range(4 * hf, 4 * hf + 4):
                        mm = pe.matmul(OP[0][:, 2 * H * j:2 * H * (j + 1)], xT[:, 128 * j:128 * j + 128],
                                       wall[l][:, D:D + 2 * H], start=True, stop=True)
                    if hf == 1:
                        mm.then_inc(s.kq_ready, 1)
                    for j in range(4 * hf, 4 * hf + 4):
                        mm = pe.matmul(SP[hf][:, HALF + D * (j % 4):HALF + D * (j % 4 + 1)],
                                       xT[:, 128 * j:128 * j + 128], wall[l][:, 0:D], start=True, stop=True)
                    mm.then_inc(s.pj_ready, 1)
                pe.wait_ge(s.kq_done, 2 * b + 2)
                pe.transpose(OP[1][0:H, 0:128], kml[:, 0:H], identf[:, :]).then_inc(s.mb_ready, 1)
                pe.wait_ge(s.kdiag_done, b + 1)
                pe.matmul(OP[1][:, 256:256 + H], ones[0:H, :], kdiag[0:H, 0:H], start=True, stop=True)\
                  .then_inc(s.mb_ready, 1)

                def first_query(h):
                    pe.wait_ge(s.xp_done, 2 * b + h + 1)
                    for n in range(2):
                        mm = pe.matmul(SP[h][:, n * HALF:(n + 1) * HALF], wq_rep[l][:, h, :],
                                       xT[:, n * HALF:(n + 1) * HALF], start=True, stop=True)
                    mm.then_inc(s.qb_ready, 1)

                if not (l == 3 and general):
                    first_query(0)
                    first_query(1)
                pe.wait_ge(s.shift_done, b + 1)
                for n in range(2):
                    mm = pe.matmul(PTP[0:H, n * HALF:(n + 1) * HALF], wall[l][:, L.QCOL:L.QCOL + H],
                                   xT[:, n * HALF:(n + 1) * HALF], start=True, stop=True)
                mm.then_inc(s.qr_ready, 1)

                def spread_row(h, room, ready):
                    for n in range(2):
                        mm = pe.matmul(room[:, n * HALF:(n + 1) * HALF],
                                       sel[:, h:h + 1, :].rearrange("p h n -> p (h n)"),
                                       q_parts[:, n * HALF:(n + 1) * HALF], start=True, stop=True)
                    mm.then_inc(ready, 1)

                def query_row(h, par):
                    spread_row(h, SP[par], s.qb_ready)

                def mask_products(tiles):
                    for i in tiles:
                        if i == 0:
                            pe.wait_ge(s.parts_done, 2 * b + 1)
                            pe.wait_ge(s.mask_done, T * (b + 1))
                        if i >= 2:
                            pe.wait_ge(s.mv_evac, T * b + i - 1)
                        for j in range(T):
                            for n in range(NP):
                                mm = pe.matmul(ps_proj[i % 2][:, 0:H * W], mask[:, j, 128 * i:128 * i + 128],
                                               pc[:, j, :, n, W:2 * W], start=(j == 0 and n == 0),
                                               stop=(j == T - 1 and n == NP - 1))
                        mm.then_inc(s.mv_ready, 1)

                def body(h, par):
                    if is_head(h, 0):
                        mask_products(range(MV_BEFORE))
                        pe.wait_ge(s.q_res, b + 1)
                        pe.wait_ge(s.parts_done, 2 * b + 2)
                    if not (is_head(h, 0) or is_head(h, 1) or is_head(h, 2) or is_last(h, H)):
                        pe.wait_ge(s.g_ready, T * (H * b + h) + T - STEPPED)
                        spread_row(h + 1, Q3, s.q3_ready)
                    pe.wait_ge(s.g_ready, T * (H * b + h + 1))
                    if is_head(h, 2) and not is_last(h, H):
                        spread_row(h + 1, Q3, s.q3_ready)
                    if not is_head(h, 0) and not is_last(h, H):
                        query_row(h + 2, par)
                    for i in range(T):
                        if i % 4 == 0 and not is_head(h, 0):
                            pe.wait_ge(s.o_evac, 2 * (H * b + h - 1) + i // 4 + 1)
                        for j in range(T):
                            for n in range(NP):
                                mm = pe.matmul(OP[i // 4][:, 2 * W * (i % 4):2 * W * (i % 4 + 1)],
                                               G[:, par, j, 128 * i:128 * i + 128],
                                               pc[:, j, h:h + 1, n, :].rearrange("p h k -> p (h k)"),
                                               start=(j == 0 and n == 0), stop=(j == T - 1 and n == NP - 1))
                        if i % 4 == 3:
                            mm.then_inc(s.o_ready, 1)
                    if is_head(h, 0):
                        pe.wait_ge(s.q_mid, 2 * b + 2)
                        pe.wait_ge(s.q_split, b + 1)
                        query_row(2, par)
                        mask_products(range(MV_BEFORE, MV_BEFORE + MV_BETWEEN))
                    if is_head(h, 1):
                        mask_products(range(MV_BEFORE + MV_BETWEEN, T))
                        pe.wait_ge(s.mv_evac, T * (b + 1))
                        spread_row(2, Q3, s.q3_ready)

                if l == 3 and general:
                    mask_products(range(T))
                    general_heads(b, g)
                else:
                    each_head(pe, H, body)

            def graphs(base, general):
                with pe.Fori(0, B) as g:
                    b = base + g if base else g
                    with pe.Fori(0, 1):
                        attention(0, b, g, general)
                    attention(1, b, g, general)
                    heads_layer(L2, b, g, general)
                    heads_layer(L3, b, g, general)

            def spread(k):
                pe.wait_ge(flag_steps, 5 * k + 2)
                pe.matmul(ps_one[0][:, 128 * k:128 * k + 128], srep[:, k, :], identf[:, :],
                          start=True, stop=True).then_inc(flag_rep, 1)

            graphs(0, False)
            pe.wait_ge(s23[3].x_done, T * B + CREDIT)
            spread(0)
            pe.wait_ge(flag_steps, 5)
            general = pe.value_load(flag[0:1, 0:1], min_val=0, max_val=1)
            with pe.If(general != 0):
                spread(1)
                graphs(B, True)
            with pe.Else():
                pe.nop()
            pe.nop()


_INS = ["x", "adj", "L0_gnn_a", "L1_gnn_a_0", "L1_gnn_a_1", "L1_gnn_a_2", "L1_gnn_a_3", "L2_gnn_W", "L2_gnn_b",
        "L2_gnn_att_src", "L2_gnn_att_dst", "L3_gnn_W", "L3_gnn_a"]


def kernel(**inputs):
    import numpy as _np
    import concourse.bacc as _bacc
    from concourse import mybir as _mybir
    from concourse.bass_utils import run_bass_kernel_spmd as _run

    nc = _bacc.Bacc("TRN2", target_bir_lowering=False, num_devices=1)
    arrays, args = {}, []
    for name in _INS:
        a = _np.ascontiguousarray(inputs[name])
        arrays[f"in_{name}_dram"] = a
        args.append(nc.dram_tensor(f"in_{name}_dram", a.shape, _mybir.dt.from_np(a.dtype), kind="ExternalInput").ap())
    out = nc.dram_tensor("out_dram", (B, N, D), F32, kind="ExternalOutput").ap()
    build(nc, *args, out)
    r = _run(nc, [arrays], core_ids=[0])
    return r.results[0]["out_dram"]
```
